# Optimizing a Trainium2 kernel written in Bass

```python
import numpy as np
import jax
import jax.numpy as jnp

def _softmax(x, axis=-1):
    return jax.nn.softmax(x, axis=axis)

def _gelu(x):
    return jax.nn.gelu(x, approximate=True)

def _silu(x):
    return jax.nn.silu(x)

def _sigmoid(x):
    return jax.nn.sigmoid(x)

def _layernorm(x, axis=-1, eps=1e-05):
    m = jnp.mean(x, axis=axis, keepdims=True)
    v = jnp.var(x, axis=axis, keepdims=True)
    return (x - m) / jnp.sqrt(v + eps)

def _scatter_add(tgt, idx, src, axis=0):
    return tgt.at[idx].add(src)

def _segment_sum(src, seg, n):
    return jax.ops.segment_sum(src, seg, n)
kernel_name = 'mk_early_fusion_d1_tok_img512_r4_5b91b4'

def setup_inputs(seed: int=0):
    np.random.seed(seed)
    _w = jnp.asarray

    def _rec_inputs():
        import jax
        import jax.numpy as jnp
        _rk = jax.random.key(seed)
        x = -0.000121822 + 0.999869 * jax.random.normal(jax.random.fold_in(_rk, 1), (4, 3, 196, 196), jnp.float32)
        txt = 0.322801 + 1.18033 * jax.random.normal(jax.random.fold_in(_rk, 2), (4, 512, 128), jnp.float32)
        return (x, txt)
    x, txt = _rec_inputs()

    def _L0_tok_setup():
        import jax, jax.numpy as jnp
        import numpy as np
        B, C, H, N_P, HID = (64, 3, 196, 14, 128)
        P = H // N_P
        IN_DIM = C * P * P
        SEQ = N_P * N_P + 1

        def sinusoidal_position(length, d):
            pos = jnp.arange(length, dtype=jnp.float32)[:, None]
            i = jnp.arange(d)[None, :]
            angle = pos / jnp.power(10000.0, (2 * (i // 2)).astype(jnp.float32) / d)
            return jnp.where(i % 2 == 0, jnp.sin(angle), jnp.cos(angle)).astype(jnp.float32)
        key = jax.random.key(seed)
        k_img, k_w, k_b, k_tok = jax.random.split(key, 4)
        img = jax.random.normal(k_img, (B, C, H, H), dtype=jnp.float32)
        W = jax.random.normal(k_w, (HID, IN_DIM), dtype=jnp.float32) / np.sqrt(IN_DIM)
        b = jax.random.normal(k_b, (HID,), dtype=jnp.float32) * 0.01
        token = jax.random.uniform(k_tok, (1, HID), dtype=jnp.float32)
        pos = sinusoidal_position(SEQ, HID)
        return {'img': img, 'W': W, 'b': b, 'token': token, 'pos': pos}
    _L0_tok_all = _L0_tok_setup()
    _L0_tok_in = {k: v for k, v in _L0_tok_all.items() if k in ('W', 'b', 'token', 'pos')}
    del _L0_tok_all

    def _L0_attn_setup():
        import jax, jax.numpy as jnp
        import numpy as np
        HIDDEN = 128
        HEADS = 8
        HEAD_DIM = HIDDEN // HEADS
        INNER = int(HIDDEN * 4.0)
        MAX_DIST = 128
        LN_EPS = 1e-05

        def _layernorm(x, g, b):
            mu = jnp.mean(x, axis=-1, keepdims=True)
            var = jnp.var(x, axis=-1, keepdims=True)
            return (x - mu) * jax.lax.rsqrt(var + LN_EPS) * g + b
        key = jax.random.key(seed)
        ks = jax.random.split(key, 12)
        B, T = (4, 512)
        s = 0.02
        return {'x': jax.random.normal(ks[0], (B, T, HIDDEN), dtype=jnp.float32), 'w_qkv': jax.random.normal(ks[1], (HIDDEN, 3 * HIDDEN), dtype=jnp.float32) * s, 'b_qkv': jnp.zeros((3 * HIDDEN,), dtype=jnp.float32), 'w_out': jax.random.normal(ks[2], (HIDDEN, HIDDEN), dtype=jnp.float32) * s, 'b_out': jnp.zeros((HIDDEN,), dtype=jnp.float32), 'ln1_g': jnp.ones((HIDDEN,), dtype=jnp.float32), 'ln1_b': jnp.zeros((HIDDEN,), dtype=jnp.float32), 'ln2_g': jnp.ones((HIDDEN,), dtype=jnp.float32), 'ln2_b': jnp.zeros((HIDDEN,), dtype=jnp.float32), 'w_mlp1': jax.random.normal(ks[3], (HIDDEN, INNER), dtype=jnp.float32) * s, 'b_mlp1': jnp.zeros((INNER,), dtype=jnp.float32), 'w_mlp2': jax.random.normal(ks[4], (INNER, HIDDEN), dtype=jnp.float32) * s, 'b_mlp2': jnp.zeros((HIDDEN,), dtype=jnp.float32), 'rel_table': jax.random.normal(ks[5], (2 * MAX_DIST + 1, HEADS), dtype=jnp.float32) * s}
    _L0_attn_all = _L0_attn_setup()
    _L0_attn_in = {k: v for k, v in _L0_attn_all.items() if k in ('w_qkv', 'b_qkv', 'w_out', 'b_out', 'ln1_g', 'ln1_b', 'ln2_g', 'ln2_b', 'w_mlp1', 'b_mlp1', 'w_mlp2', 'b_mlp2', 'rel_table')}
    del _L0_attn_all

    def _L0_ffn_setup():
        import jax, jax.numpy as jnp
        import numpy as np
        S, B, I, O, H, E, K = (128, 32, 128, 128, 128, 8, 2)

        def _expert(x_seq, Wi, Wh, b, Wo, bo):
            Bsz = x_seq.shape[1]
            Hd = Wh.shape[0]

            def step(carry, xt):
                h, c = carry
                gates = xt @ Wi + h @ Wh + b
                i_, f_, g_, o_ = jnp.split(gates, 4, axis=-1)
                c = jax.nn.sigmoid(f_) * c + jax.nn.sigmoid(i_) * jnp.tanh(g_)
                h = jax.nn.sigmoid(o_) * jnp.tanh(c)
                return ((h, c), h @ Wo + bo)
            init = (jnp.zeros((Bsz, Hd), x_seq.dtype), jnp.zeros((Bsz, Hd), x_seq.dtype))
            _, ys = jax.lax.scan(step, init, x_seq)
            return ys
        key = jax.random.key(seed)
        ks = jax.random.split(key, 6)
        s = 0.02
        return {'x': jax.random.normal(ks[0], (S, B, I), dtype=jnp.float32), 'router_w': jax.random.normal(ks[1], (I, E), dtype=jnp.float32) * s, 'router_b': jnp.zeros((E,), dtype=jnp.float32), 'Wi': jax.random.normal(ks[2], (E, I, 4 * H), dtype=jnp.float32) * s, 'Wh': jax.random.normal(ks[3], (E, H, 4 * H), dtype=jnp.float32) * s, 'b': jnp.zeros((E, 4 * H), dtype=jnp.float32), 'Wo': jax.random.normal(ks[4], (E, H, O), dtype=jnp.float32) * s, 'bo': jnp.zeros((E, O), dtype=jnp.float32)}
    _L0_ffn_all = _L0_ffn_setup()
    _L0_ffn_in = {k: v for k, v in _L0_ffn_all.items() if k in ('router_w', 'router_b', 'Wi', 'Wh', 'b', 'Wo', 'bo')}
    del _L0_ffn_all
    return {'x': x, 'txt': txt, 'L0_tok_W': _L0_tok_in['W'], 'L0_tok_b': _L0_tok_in['b'], 'L0_tok_token': _L0_tok_in['token'], 'L0_tok_pos': _L0_tok_in['pos'], 'L0_attn_w_qkv': _L0_attn_in['w_qkv'], 'L0_attn_b_qkv': _L0_attn_in['b_qkv'], 'L0_attn_w_out': _L0_attn_in['w_out'], 'L0_attn_b_out': _L0_attn_in['b_out'], 'L0_attn_ln1_g': _L0_attn_in['ln1_g'], 'L0_attn_ln1_b': _L0_attn_in['ln1_b'], 'L0_attn_ln2_g': _L0_attn_in['ln2_g'], 'L0_attn_ln2_b': _L0_attn_in['ln2_b'], 'L0_attn_w_mlp1': _L0_attn_in['w_mlp1'], 'L0_attn_b_mlp1': _L0_attn_in['b_mlp1'], 'L0_attn_w_mlp2': _L0_attn_in['w_mlp2'], 'L0_attn_b_mlp2': _L0_attn_in['b_mlp2'], 'L0_attn_rel_table': _L0_attn_in['rel_table'], 'L0_ffn_router_w': _L0_ffn_in['router_w'], 'L0_ffn_router_b': _L0_ffn_in['router_b'], 'L0_ffn_Wi': _L0_ffn_in['Wi'], 'L0_ffn_Wh': _L0_ffn_in['Wh'], 'L0_ffn_b': _L0_ffn_in['b'], 'L0_ffn_Wo': _L0_ffn_in['Wo'], 'L0_ffn_bo': _L0_ffn_in['bo']}

def reference(x, txt, L0_tok_W, L0_tok_b, L0_tok_token, L0_tok_pos, L0_attn_w_qkv, L0_attn_b_qkv, L0_attn_w_out, L0_attn_b_out, L0_attn_ln1_g, L0_attn_ln1_b, L0_attn_ln2_g, L0_attn_ln2_b, L0_attn_w_mlp1, L0_attn_b_mlp1, L0_attn_w_mlp2, L0_attn_b_mlp2, L0_attn_rel_table, L0_ffn_router_w, L0_ffn_router_b, L0_ffn_Wi, L0_ffn_Wh, L0_ffn_b, L0_ffn_Wo, L0_ffn_bo):
    import jax
    import jax.numpy as jnp

    def _L0_tok_ref(img, W, b, token, pos):
        import jax, jax.numpy as jnp
        import numpy as np
        B, C, H, N_P, HID = (64, 3, 196, 14, 128)
        P = H // N_P
        IN_DIM = C * P * P
        SEQ = N_P * N_P + 1

        def sinusoidal_position(length, d):
            pos = jnp.arange(length, dtype=jnp.float32)[:, None]
            i = jnp.arange(d)[None, :]
            angle = pos / jnp.power(10000.0, (2 * (i // 2)).astype(jnp.float32) / d)
            return jnp.where(i % 2 == 0, jnp.sin(angle), jnp.cos(angle)).astype(jnp.float32)
        Bn = img.shape[0]
        patches = img.reshape(Bn, C, N_P, P, N_P, P)
        patches = patches.transpose(0, 2, 4, 1, 3, 5).reshape(Bn, N_P * N_P, IN_DIM)
        tokens = jnp.einsum('bsd,hd->bsh', patches, W) + b
        cls = jnp.broadcast_to(token[None, :, :], (Bn, 1, HID))
        out = jnp.concatenate([cls, tokens], axis=1) + pos
        return out

    def _L0_attn_ref(x, w_qkv, b_qkv, w_out, b_out, ln1_g, ln1_b, ln2_g, ln2_b, w_mlp1, b_mlp1, w_mlp2, b_mlp2, rel_table):
        import jax, jax.numpy as jnp
        import numpy as np
        HIDDEN = 128
        HEADS = 8
        HEAD_DIM = HIDDEN // HEADS
        INNER = int(HIDDEN * 4.0)
        MAX_DIST = 128
        LN_EPS = 1e-05

        def _layernorm(x, g, b):
            mu = jnp.mean(x, axis=-1, keepdims=True)
            var = jnp.var(x, axis=-1, keepdims=True)
            return (x - mu) * jax.lax.rsqrt(var + LN_EPS) * g + b
        B, T, C = x.shape
        scale = HEAD_DIM ** (-0.5)
        qkv = x @ w_qkv + b_qkv
        qkv = qkv.reshape(B, T, 3, HEADS, HEAD_DIM)
        q = qkv[:, :, 0].transpose(0, 2, 1, 3)
        k = qkv[:, :, 1].transpose(0, 2, 1, 3)
        v = qkv[:, :, 2].transpose(0, 2, 1, 3)
        logits = jnp.einsum('bhqd,bhkd->bhqk', q, k) * scale
        rel = jnp.clip(jnp.arange(T)[:, None] - jnp.arange(T)[None, :], -MAX_DIST, MAX_DIST) + MAX_DIST
        bias = rel_table[rel].transpose(2, 0, 1)
        logits = logits + bias[None]
        attn = jax.nn.softmax(logits, axis=-1)
        out = jnp.einsum('bhqk,bhkd->bhqd', attn, v)
        out = out.transpose(0, 2, 1, 3).reshape(B, T, C)
        out = out @ w_out + b_out
        x = _layernorm(x + out, ln1_g, ln1_b)
        h = jax.nn.gelu(x @ w_mlp1 + b_mlp1, approximate=False)
        mlp_out = h @ w_mlp2 + b_mlp2
        return _layernorm(x + mlp_out, ln2_g, ln2_b)

    def _L0_ffn_ref(x, router_w, router_b, Wi, Wh, b, Wo, bo):
        import jax, jax.numpy as jnp
        import numpy as np
        S, B, I, O, H, E, K = (128, 32, 128, 128, 128, 8, 2)

        def _expert(x_seq, Wi, Wh, b, Wo, bo):
            Bsz = x_seq.shape[1]
            Hd = Wh.shape[0]

            def step(carry, xt):
                h, c = carry
                gates = xt @ Wi + h @ Wh + b
                i_, f_, g_, o_ = jnp.split(gates, 4, axis=-1)
                c = jax.nn.sigmoid(f_) * c + jax.nn.sigmoid(i_) * jnp.tanh(g_)
                h = jax.nn.sigmoid(o_) * jnp.tanh(c)
                return ((h, c), h @ Wo + bo)
            init = (jnp.zeros((Bsz, Hd), x_seq.dtype), jnp.zeros((Bsz, Hd), x_seq.dtype))
            _, ys = jax.lax.scan(step, init, x_seq)
            return ys
        S_, B_, I_ = x.shape
        N = S_ * B_
        flat_x = x.reshape(N, I_)
        logits = flat_x @ router_w + router_b
        top_vals, top_idx = jax.lax.top_k(logits, K)
        rw = jax.nn.softmax(top_vals, axis=1)
        mask = (top_idx.T[:, None, :] == jnp.arange(E)[None, :, None]).astype(x.dtype)
        expert_x = (mask[..., None] * flat_x[None, None]).reshape(K, E, S_, B_, I_)
        run_e = jax.vmap(_expert, in_axes=(0, 0, 0, 0, 0, 0))
        run_ke = jax.vmap(run_e, in_axes=(0, None, None, None, None, None))
        out = run_ke(expert_x, Wi, Wh, b, Wo, bo)
        out = out.reshape(K, E, N, -1)
        y = jnp.einsum('ken,nk,keno->no', mask, rw, out)
        return y.reshape(S_, B_, -1)
    h = _L0_tok_ref(x, L0_tok_W, L0_tok_b, L0_tok_token, L0_tok_pos)
    h = jnp.concatenate([h, txt], axis=1)
    h = h + _L0_attn_ref(_layernorm(h, axis=-1), L0_attn_w_qkv, L0_attn_b_qkv, L0_attn_w_out, L0_attn_b_out, L0_attn_ln1_g, L0_attn_ln1_b, L0_attn_ln2_g, L0_attn_ln2_b, L0_attn_w_mlp1, L0_attn_b_mlp1, L0_attn_w_mlp2, L0_attn_b_mlp2, L0_attn_rel_table)
    h = h + _L0_ffn_ref(_layernorm(h, axis=-1), L0_ffn_router_w, L0_ffn_router_b, L0_ffn_Wi, L0_ffn_Wh, L0_ffn_b, L0_ffn_Wo, L0_ffn_bo)
    return h

_drawn_inputs = setup_inputs


def setup_inputs(seed=0):
    import zlib

    import numpy as np

    out = dict(_drawn_inputs(seed))
    spreads = {'L0_attn_b_qkv': (0.0, 0.75),
     'L0_attn_b_out': (0.0, 0.1),
     'L0_attn_ln1_g': (1.0, 0.2),
     'L0_attn_ln1_b': (0.0, 0.1),
     'L0_attn_ln2_g': (1.0, 0.2),
     'L0_attn_ln2_b': (0.0, 0.1),
     'L0_attn_b_mlp1': (0.0, 0.639),
     'L0_attn_b_mlp2': (0.0, 0.1),
     'L0_ffn_router_b': (0.0, 0.49),
     'L0_ffn_b': (0.0, 0.8),
     'L0_ffn_bo': (0.0, 0.1)}
    factors = {'L0_tok_b': 8.0,
     'L0_tok_token': 4.344,
     'L0_attn_w_qkv': 8.0,
     'L0_attn_w_out': 4.762,
     'L0_attn_rel_table': 8.0,
     'L0_ffn_Wi': 8.0,
     'L0_ffn_Wh': 8.0,
     'L0_ffn_Wo': 8.0}
    for name, (base, spread) in spreads.items():
        noise = np.random.default_rng([zlib.crc32(name.encode()), seed]).standard_normal(out[name].shape)
        drawn = base * np.exp(spread * noise) if base else spread * noise
        out[name] = jnp.asarray(drawn.astype(out[name].dtype))
    for name, factor in factors.items():
        out[name] = (out[name] * factor).astype(out[name].dtype)
    return out
```

```python
from contextlib import ExitStack

import concourse.bass as bass
from concourse import mybir

F32 = mybir.dt.float32
BF16 = mybir.dt.bfloat16
U32 = mybir.dt.uint32
I32 = mybir.dt.int32
ALU = mybir.AluOpType
ACT = mybir.ActivationFunctionType

P = 128
B = 4
HID = 128
HEADS = 8
DH = HID // HEADS
NP_SIDE = 14
N_PATCH = NP_SIDE * NP_SIDE
PATCH_DIM = 3 * NP_SIDE * NP_SIDE
PCH = 6
PROWS = PATCH_DIM // PCH
TXT = 512
T = 1 + N_PATCH + TXT
NT = -(-T // P)
TPAD = NT * P
LAST = T - (NT - 1) * P
TXT0 = 1 + N_PATCH - P
HALF = 512
INNER = 512
NCH = INNER // P
MAXD = 128
EXT = 2 * TPAD
GW = (NT - 1) * P + T
BAND = 3 * P
QR = 96
XR = 2 + 3 * NT
KR = QR + XR
GROUPS = 2
GH = HEADS // GROUPS
E = 8
EPS = 1e-5
LOWEST = -3.0e38
HALVES = [(0, HALF), (HALF, T)]
Q_PARTS = [0, 0, 1, 0, 2, 1]
K_PARTS = [0, 1, 0, 2, 0, 1]

M0, M1, W0, W1, W01 = range(5)
PICKS = 5


def rows_of(t):
    return P if t < NT - 1 else LAST


def dram(ap, offset, pattern):
    return bass.AP(tensor=ap.tensor, offset=offset, ap=pattern)


def apart(dve, spare):
    dve.memset(spare[0:1, 0:1], 0.0)


def every_partition(ap, n):
    return dram(ap, 0, [[0, P], [1, n]])


def column(ap, n=P, offset=0):
    return dram(ap, offset, [[1, n], [1, 1]])


def allocate(nc, ctx, spec, prefix):
    return {name: ctx.enter_context(nc.sbuf_tensor(prefix + name, shape, dt)) for name, (shape, dt) in spec.items()}


def semaphores(nc, ctx, names, prefix):
    return {name: ctx.enter_context(nc.semaphore(prefix + name)) for name in names.split()}


def attention_phase(nc, d, keep, ps, scratch):
    tok = [P, NT, HID]
    with ExitStack() as ctx:
        s = allocate(nc, ctx, {
            "ones": ([P, P], F32),
            "head_sum": ([P, P], F32),
            "w_tok": ([PROWS, PCH, HID], F32), "w_qkv": ([P, 3 * HID], F32), "w_out": ([P, GROUPS, HID], F32),
            "w_mlp1": ([P, INNER], F32), "w_mlp2": ([P, NCH, HID], F32), "router_w": ([P, E], F32),
            "pos_b": ([P, 2, HID], F32), "tok_add": ([P, 2, HID], F32),
            "bq": ([P, 1], F32), "bq4": ([P, 1], F32), "bk": ([P, 1], F32), "b_mlp1": ([P, NCH], F32),
            "ln1_g": ([P, 1], F32), "ln1_b": ([P, 1], F32),
            "bv": ([P, HID], F32), "b_out": ([P, HID], F32), "b_mlp2": ([P, HID], F32),
            "ln2_g": ([P, HID], F32), "ln2_b": ([P, HID], F32), "router_b": ([P, E], F32),
            "minus_half": ([P, NT], F32), "iota_e": ([P, E], F32),
            "bias_qk": ([P, HEADS, GW], F32), "bias_kq": ([P, HEADS, 3, BAND], BF16),
            "ident_b": ([P, P], BF16),
            "txt1": ([P, HID], F32),
            "h0": (tok, F32), "n1": (tok, F32), "n1b": (tok, F32), "xT": ([P, TPAD], F32),
            "qk32": ([P, 2, T], F32), "qk_parts": ([P, 2, 3, T], BF16),
            "q_st": ([P, HEADS, TPAD], BF16), "k_st": ([P, HEADS, TPAD], BF16),
            "v": ([P, NT, HEADS, 32], F32), "big": ([P, 2 * GH * T], F32),
            "top": ([P, GH * NT], F32), "top_hi": ([GH * NT, P], BF16), "top_lo": ([GH * NT, P], BF16),
            "o_inv": ([P, 2, T], F32), "att": ([P, GROUPS, TPAD], F32),
            "r": (tok, F32),
            "spare": ([P, 1], F32), "eps": ([P, NT], F32), "stats": ([P, NT, 6], F32), "mom": ([P, NT, 2], F32), "veps": ([P, NT], F32), "rstd": ([P, NT], F32),
            "lg": ([P, NT, E], F32), "v8": ([P, NT, 8], F32), "i8": ([P, NT, 8], U32), "if8": ([P, NT, 8], F32),
            "gap": ([P, NT], F32), "egap": ([P, NT], F32), "den": ([P, NT], F32), "w2": ([P, NT, 2], F32),
            "rt": ([P, NT, P], F32), "wk": ([P, NT, 16], F32), "wr": ([P, NT, 16], F32), "wb": ([P, NT, 16], BF16),
        }, "a_")
        S = semaphores(nc, ctx, """
            weights_in patterns_in zeroed key_rows_ready ident_ready consts_ready pos_ready band_in0 band_in1 band_step band_ready
            const_parts const_step const_in rows_fixed
            batch_done inputs_in tokens_psum h0_step h0_ready stats_ready moments_ready veps_ready rstd_ready
            normed n1b_ready turned xT_ready q_psum k_psum v_psum qk32_ready qk_hi qk_rest_ready qk_mid qk_lo
            v_ready parts_out stacked s_psum maxed top_turned top_hi_ready top_lo_ready top_rows_in
            logits_psum exp_done av_done oT_ready sum_psum inv_ready att_ready o_psum r_ready
            m1_psum gel_ready m2_psum y_scaled y_ready h1_ready route_psum route_step gap_ready egap_ready
            route_ready drain_dve
        """, "a_")

        def w(t):
            return ps[t]

        def tm(t):
            return ps[t][:, 0:TPAD].rearrange("p (t c) -> p t c", t=NT)

        probs = s["big"][:, :].rearrange("p (a j t) -> p a j t", a=2, j=GH)
        s["const_f"] = s["big"][0:NT, :].rearrange("k (h t) -> k h t", h=HEADS)
        s["patches"] = s["big"][0:PROWS, 0:PCH * 2 * P].rearrange("p (c n) -> p c n", c=PCH)
        s["gel"] = s["big"][:, 0:NCH * TPAD].rearrange("p (c n) -> p c n", c=NCH)
        s["const_p"] = s["qk_parts"][0:NT, 0, :, :]
        s["qk_rest"] = s["o_inv"]
        s["oT"], s["inv"] = s["o_inv"][:, 0, :], s["o_inv"][:, 1, :]
        s["x1"] = s["n1b"]
        s["band_f"] = s["n1b"][:].rearrange("p t c -> p (t c)").rearrange("p (a n) -> p a n", a=2)
        s["pat_f"] = s["r"][:].rearrange("p t c -> p (t c)")


        N_W = 18 + NCH
        band_in = (S["band_in0"], S["band_in1"])
        block = ctx.enter_context(nc.Block())

        @block.sync
        def _(sp):
            loads = [
                (s["w_tok"][:], d["tok_W"].rearrange("(c p) n -> p c n", p=PROWS)),
                (s["w_qkv"][:], d["w_qkv"]), (s["w_mlp1"][:], d["w_mlp1"]),
                (s["w_mlp2"][:], d["w_mlp2"].rearrange("(c p) n -> p c n", p=P)), (s["router_w"][:], d["router_w"]),
                (s["bq"][:], column(d["b_qkv"])), (s["bk"][:], column(d["b_qkv"], offset=HID)),
                (s["bv"][:], dram(d["b_qkv"], 2 * HID, [[0, P], [1, HID]])),
                (s["ln1_g"][:], column(d["ln1_g"])), (s["ln1_b"][:], column(d["ln1_b"])),
                (s["b_out"][:], every_partition(d["b_out"], HID)), (s["b_mlp2"][:], every_partition(d["b_mlp2"], HID)),
                (s["ln2_g"][:], every_partition(d["ln2_g"], HID)), (s["ln2_b"][:], every_partition(d["ln2_b"], HID)),
                (s["router_b"][:], every_partition(d["router_b"], E)),
                (s["head_sum"][:], d["c_head_sum"]), (s["pat_f"][QR:KR, :], d["c_key_rows"]), (keep["ident"][:], d["c_ident"]),
            ]
            loads += [(s["b_mlp1"][:, c:c + 1], column(d["b_mlp1"], offset=c * P)) for c in range(NCH)]
            assert len(loads) == N_W
            for dst, src in loads:
                sp.dma_start(dst, src).then_inc(S["weights_in"], 16)
            sp.wait_ge(S["zeroed"], 1)
            sp.dma_start(s["tok_add"][0:1, 0, :], d["token"]).then_inc(S["patterns_in"], 16)
            sp.dma_start(s["tok_add"][1:P, 0, :], dram(d["tok_b"], 0, [[0, P - 1], [1, HID]])).then_inc(S["patterns_in"], 16)
            sp.dma_start(s["tok_add"][0:TXT0, 1, :], dram(d["tok_b"], 0, [[0, TXT0], [1, HID]])).then_inc(S["patterns_in"], 16)
            sp.dma_start(s["pos_b"][:, 0, :], d["pos"][0:P, :]).then_inc(S["patterns_in"], 16)
            sp.dma_start(s["pos_b"][0:TXT0, 1, :], d["pos"][P:1 + N_PATCH, :]).then_inc(S["patterns_in"], 16)
            for g in range(GROUPS):
                for j in range(GH):
                    sp.dma_start(s["w_out"][32 * j:32 * j + DH, g, :],
                                 d["w_out"][(g * GH + j) * DH:(g * GH + j + 1) * DH, :]).then_inc(S["patterns_in"], 16)
            for kt in range(NT):
                left, right = kt * P - P, kt * P + 2 * P
                if left > 0:
                    sp.dma_start(s["const_f"][kt:kt + 1, :, 0:left],
                                 dram(d["rel_ext"], 0, [[0, 1], [EXT, HEADS], [1, left]])).then_inc(S["const_in"], 16)
                if right < T:
                    sp.dma_start(s["const_f"][kt:kt + 1, :, right:T],
                                 dram(d["rel_ext"], EXT - (T - right), [[0, 1], [EXT, HEADS], [1, T - right]])
                                 ).then_inc(S["const_in"], 16)
            for h in range(HEADS):
                if h >= 2:
                    sp.wait_ge(S["band_ready"], h - 1)
                sp.dma_start(s["band_f"][:, h % 2, :],
                             d["rel_band"][h, :, :]).then_inc(band_in[h % 2], 16)
            for h in range(HEADS):
                sp.dma_start(s["bias_qk"][:, h, :],
                             d["rel_strip"][h, :, :]).then_inc(S["patterns_in"], 16)
            for h in range(HEADS):
                sp.wait_ge(S["const_parts"], h + 1)
                for part in range(3):
                    r = QR + 2 + NT * part
                    sp.dma_start(s["q_st"][r:r + NT, h, 0:T], s["const_p"][:, part, :]).then_inc(S["rows_fixed"], 16)

            with sp.Fori(0, B) as i:
                sp.wait_ge(S["batch_done"], i + 1)
                sp.dma_start(s["patches"][:], d["patches"][bass.ds(i, 1), :, :].rearrange(
                    "o (c p) n -> p (o c) n", p=PROWS)).then_inc(S["inputs_in"], 16)
                txt = d["txt"][bass.ds(i, 1), :, :].rearrange("o t c -> (o t) c")
                n1 = P - TXT0
                sp.dma_start(s["txt1"][TXT0:P, :], txt[0:n1, :]).then_inc(S["inputs_in"], 16)
                sp.dma_start(s["h0"][:, 2:NT - 1, :],
                             txt[n1:n1 + (NT - 3) * P, :].rearrange("(t p) c -> p t c", p=P)).then_inc(S["inputs_in"], 16)
                sp.dma_start(s["h0"][0:LAST, NT - 1, :], txt[TXT - LAST:TXT, :]).then_inc(S["inputs_in"], 16)
                for a in range(2):
                    sp.wait_ge(S["qk_lo"], 2 * i + a + 1)
                    sp.dma_start(scratch[a].rearrange("m p n -> p m n"), s["qk_parts"][:, a, :, :]).then_inc(S["parts_out"], 16)
                sp.wait_ge(S["parts_out"], 32 * i + 32)
                for a, (st, parts) in enumerate(((s["q_st"], Q_PARTS), (s["k_st"], K_PARTS))):
                    for r, part in enumerate(parts):
                        sp.dma_start(st[DH * r:DH * r + DH, :, 0:T],
                                     scratch[a, part].rearrange("(h x) n -> x h n", x=DH)).then_inc(S["stacked"], 16)
                for g in range(GROUPS):
                    sp.wait_ge(S["top_lo_ready"], 2 * i + g + 1)
                    for r, src in enumerate((s["top_hi"], s["top_lo"])):
                        dst = s["q_st"][QR + r:QR + r + 1, g * GH:(g + 1) * GH, :].rearrange(
                            "o h (t c) -> o (h t) c", c=P)
                        sp.dma_start(dst, src[:, :]).then_inc(S["top_rows_in"], 16)

        @block.gpsimd
        def _(pool):
            pool.memset(s["tok_add"][:], 0.0)
            pool.memset(s["pos_b"][:], 0.0)
            pool.memset(s["w_out"][:], 0.0)
            pool.memset(s["const_f"][:], 0.0)
            pool.memset(s["q_st"][:], 0.0)
            pool.memset(s["k_st"][:], 0.0)
            pool.memset(s["txt1"][:], 0.0)
            pool.memset(s["minus_half"][:], -0.5)
            pool.memset(s["eps"][:], EPS)
            pool.memset(s["rt"][:], 0.0)
            pool.memset(s["v"][:], 0.0)
            pool.memset(s["att"][:], 0.0)
            pool.memset(s["xT"][:], 0.0)
            pool.memset(s["h0"][:], 0.0).then_inc(S["zeroed"], 1)
            pool.wait_ge(S["zeroed"], 1)
            pool.memset(s["v"][:, :, :, DH:DH + 1], 1.0).then_inc(S["consts_ready"], 1)
            pool.iota(s["iota_e"][:], pattern=[[1, E]], base=0, channel_multiplier=0,
                      allow_small_or_imprecise_dtypes=True).then_inc(S["consts_ready"], 1)
            pool.wait_ge(S["weights_in"], 16 * N_W)
            pool.tensor_copy(s["ident_b"][:], keep["ident"][:]).then_inc(S["ident_ready"], 1)
            pool.tensor_scalar(s["bq4"][:], s["bq"][:], DH ** -0.5, None, ALU.mult).then_inc(S["consts_ready"], 1)
            pool.wait_ge(S["patterns_in"], 16 * (5 + HEADS + HEADS))
            pool.tensor_tensor(s["pos_b"][:], s["pos_b"][:], s["tok_add"][:], ALU.add).then_inc(S["pos_ready"], 1)
            pool.wait_ge(S["pos_ready"], 1)
            pool.memset(s["veps"][:], 0.0).then_inc(S["batch_done"], 1)

            with pool.Fori(0, B) as i:
                def rstd(n):
                    pool.wait_ge(S["moments_ready"], 4 * i + n + 1)
                    pool.tensor_tensor(s["veps"][:], s["mom"][:, :, 1], s["eps"][:], ALU.add).then_inc(S["veps_ready"], 1)
                    pool.wait_ge(S["veps_ready"], 4 * i + n + 1)
                    pool.tensor_tensor(s["rstd"][:], s["veps"][:], s["minus_half"][:], ALU.pow).then_inc(S["rstd_ready"], 1)

                rstd(0)
                pool.wait_ge(S["normed"], 4 * i + 1)
                for t in range(NT):
                    ins = pool.tensor_tensor(s["n1b"][:, t, :], s["n1"][:, t, :], s["b_out"][:], ALU.add)
                ins.then_inc(S["n1b_ready"], 1)
                rstd(1)
                rstd(2)
                rstd(3)

        @block.vector
        def _(dve):
            def split(src, hi, mid, lo, step, done, n):
                dve.tensor_copy(hi, src).then_inc(step, 1)
                dve.wait_ge(step, 4 * n + 1)
                dve.tensor_tensor(src, src, hi, ALU.subtract).then_inc(step, 1)
                dve.wait_ge(step, 4 * n + 2)
                dve.tensor_copy(mid, src).then_inc(step, 1)
                dve.wait_ge(step, 4 * n + 3)
                dve.tensor_tensor(src, src, mid, ALU.subtract).then_inc(step, 1)
                dve.wait_ge(step, 4 * n + 4)
                dve.tensor_copy(lo, src).then_inc(done, 1)

            for h in range(HEADS):
                dve.wait_ge(band_in[h % 2], 16 * (h // 2 + 1))
                split(s["band_f"][:, h % 2, :], s["bias_kq"][:, h, 0, :], s["bias_kq"][:, h, 1, :], s["bias_kq"][:, h, 2, :],
                      S["band_step"], S["band_ready"], h)
            dve.wait_ge(S["const_in"], 16 * 8)
            for h in range(HEADS):
                if h >= 1:
                    dve.wait_ge(S["rows_fixed"], 48 * h)
                split(s["const_f"][:, h, :], s["const_p"][:, 0, :], s["const_p"][:, 1, :], s["const_p"][:, 2, :],
                      S["const_step"], S["const_parts"], h)

            dve.wait_ge(S["pos_ready"], 1)
            with dve.Fori(0, B) as i:
                def layer_norm(n, src, dst):
                    for t in range(NT):
                        ins = dve.bn_stats(s["stats"][:, t, :], src[:, t, :])
                    ins.then_inc(S["stats_ready"], 1)
                    dve.wait_ge(S["stats_ready"], 4 * i + n + 1)
                    apart(dve, s["spare"])
                    for t in range(NT):
                        ins = dve.bn_aggr(s["mom"][:, t, :], s["stats"][:, t, :])
                    ins.then_inc(S["moments_ready"], 1)
                    dve.wait_ge(S["rstd_ready"], 4 * i + n + 1)
                    for t in range(NT):
                        ins = dve.tensor_scalar(dst[:, t, :], src[:, t, :], s["mom"][:, t, 0:1], s["rstd"][:, t:t + 1],
                                                ALU.subtract, ALU.mult)
                    ins.then_inc(S["normed"], 1)

                dve.wait_ge(S["batch_done"], i + 1)
                dve.wait_ge(S["inputs_in"], 64 * i + 64)
                dve.wait_ge(S["tokens_psum"], i + 1)
                dve.tensor_tensor(s["h0"][:, 0:2, :], tm(0)[:, 0:2, :], s["pos_b"][:], ALU.add).then_inc(S["h0_step"], 1)
                dve.wait_ge(S["h0_step"], i + 1)
                dve.tensor_tensor(s["h0"][:, 1, :], s["h0"][:, 1, :], s["txt1"][:], ALU.add).then_inc(S["h0_ready"], 1)
                dve.wait_ge(S["h0_ready"], i + 1)
                layer_norm(0, s["h0"], s["n1"])

                for a in range(2):
                    dve.wait_ge(S["qk_hi"], 2 * i + a + 1)
                    dve.tensor_tensor(s["qk_rest"][:, a, :], s["qk32"][:, a, :], s["qk_parts"][:, a, 0, :],
                                      ALU.subtract).then_inc(S["qk_rest_ready"], 1)
                dve.wait_ge(S["v_psum"], i + 1)
                for t in range(NT):
                    ins = dve.tensor_tensor(s["v"][:, t, :, 0:DH],
                                            tm(0)[:, t, :].rearrange("p (h x) -> p h x", h=HEADS),
                                            s["bv"][:].rearrange("p (h x) -> p h x", h=HEADS), ALU.add)
                ins.then_inc(S["v_ready"], 1)
                for a in range(2):
                    dve.wait_ge(S["qk_mid"], 2 * i + a + 1)
                    dve.tensor_tensor(s["qk_parts"][:, a, 2, :], s["qk_rest"][:, a, :], s["qk_parts"][:, a, 1, :],
                                      ALU.subtract).then_inc(S["qk_lo"], 1)

                def maxima(g):
                    for n in range(GH * NT):
                        t, j = divmod(n, GH)
                        dve.wait_ge(S["s_psum"], 48 * i + 24 * g + n + 1)
                        apart(dve, s["spare"])
                        off = (NT - 1 - t) * P
                        dve.tensor_tensor_reduce(s["inv"], w(2)[:, 0:T], s["bias_qk"][:, g * GH + j, off:off + T],
                                                 1.0, LOWEST, ALU.add, ALU.max,
                                                 s["top"][:, j * NT + t:j * NT + t + 1]).then_inc(S["maxed"], 1)

                def top_rows(g):
                    dve.wait_ge(S["top_turned"], 2 * i + g + 1)
                    if g == 1:
                        dve.wait_ge(S["top_rows_in"], 64 * i + 32)
                    src = w(2)[0:GH * NT, 0:P]
                    dve.tensor_scalar(s["top_hi"][:], src, -1.0, None, ALU.mult).then_inc(S["top_hi_ready"], 1)
                    dve.wait_ge(S["top_hi_ready"], 2 * i + g + 1)
                    dve.scalar_tensor_tensor(s["top_lo"][:], src, -1.0, s["top_hi"][:], ALU.mult,
                                             ALU.subtract).then_inc(S["top_lo_ready"], 1)

                def normalise(g):
                    dve.wait_ge(S["sum_psum"], 2 * i + g + 1)
                    dve.reciprocal(s["inv"], w(3)[:, 0:T]).then_inc(S["inv_ready"], 1)
                    dve.wait_ge(S["inv_ready"], 2 * i + g + 1)
                    dve.tensor_tensor(s["att"][:, g, 0:T], s["oT"], s["inv"], ALU.mult).then_inc(S["att_ready"], 1)

                maxima(0)
                top_rows(0)
                maxima(1)
                top_rows(1)
                normalise(0)
                normalise(1)
                dve.wait_ge(S["o_psum"], i + 1)
                dve.wait_ge(S["n1b_ready"], i + 1)
                dve.tensor_tensor(s["r"][:], tm(0), s["n1b"][:], ALU.add).then_inc(S["r_ready"], 1)
                dve.wait_ge(S["r_ready"], 2 * i + 1)
                layer_norm(1, s["r"], s["x1"])
                dve.wait_ge(S["m2_psum"], i + 1)
                for t in range(NT):
                    ins = dve.tensor_tensor(s["r"][:, t, :], tm(0)[:, t, :], s["b_mlp2"][:], ALU.add)
                ins.then_inc(S["r_ready"], 1)
                dve.wait_ge(S["r_ready"], 2 * i + 2)
                layer_norm(2, s["r"], s["x1"])
                dve.wait_ge(S["normed"], 4 * i + 3)
                for t in range(NT):
                    ins = dve.tensor_tensor(s["x1"][:, t, :], s["x1"][:, t, :], s["ln2_g"][:], ALU.mult)
                ins.then_inc(S["y_scaled"], 1)
                dve.wait_ge(S["y_scaled"], i + 1)
                for t in range(NT):
                    ins = dve.tensor_tensor(s["x1"][:, t, :], s["x1"][:, t, :], s["ln2_b"][:], ALU.add)
                ins.then_inc(S["y_ready"], 1)
                dve.wait_ge(S["y_ready"], i + 1)
                dve.tensor_tensor(s["r"][:], s["h0"][:], s["x1"][:], ALU.add).then_inc(S["h1_ready"], 1)
                dve.wait_ge(S["h1_ready"], i + 1)
                layer_norm(3, s["r"], s["n1"])

                def step(ins, n):
                    ins.then_inc(S["route_step"], 1)
                    dve.wait_ge(S["route_step"], 11 * i + n)
                    if n == 1:
                        apart(dve, s["spare"])

                dve.wait_ge(S["route_psum"], i + 1)
                for t in range(NT):
                    ins = dve.tensor_tensor(s["lg"][:, t, :], w(2)[:, t * E:(t + 1) * E], s["router_b"][:], ALU.add)
                step(ins, 1)
                for t in range(NT):
                    ins = dve.max(s["v8"][:, t, :], s["lg"][:, t, :])
                step(ins, 2)
                dve.tensor_tensor(s["gap"][:], s["v8"][:, :, 1], s["v8"][:, :, 0], ALU.subtract).then_inc(S["gap_ready"], 1)
                for t in range(NT):
                    ins = dve.max_index(s["i8"][:, t, :], s["v8"][:, t, :], s["lg"][:, t, :])
                step(ins, 3)
                step(dve.tensor_copy(s["if8"][:], s["i8"][:]), 4)
                for k in range(2):
                    for t in range(NT):
                        ins = dve.tensor_scalar(s["rt"][:, t, E * k:E * k + E], s["iota_e"][:], s["if8"][:, t, k:k + 1], None,
                                                ALU.is_equal)
                dve.wait_ge(S["egap_ready"], i + 1)
                step(dve.tensor_scalar(s["den"][:], s["egap"][:], 1.0, None, ALU.add), 5)
                step(dve.reciprocal(s["w2"][:, :, 0], s["den"][:]), 6)
                step(dve.tensor_tensor(s["w2"][:, :, 1], s["egap"][:], s["w2"][:, :, 0], ALU.mult), 7)
                for k in range(2):
                    for t in range(NT):
                        ins = dve.tensor_scalar(s["wk"][:, t, E * k:E * k + E], s["rt"][:, t, E * k:E * k + E],
                                                s["w2"][:, t, k:k + 1], None, ALU.mult)
                step(ins, 8)
                step(dve.tensor_copy(s["wb"][:], s["wk"][:]), 9)
                dve.tensor_copy(s["rt"][:, :, 16:32], s["wb"][:])
                step(dve.tensor_tensor(s["wr"][:], s["wk"][:], s["wb"][:], ALU.subtract), 10)
                step(dve.tensor_copy(s["wb"][:], s["wr"][:]), 11)
                dve.tensor_copy(s["rt"][:, :, 32:48], s["wb"][:])
                dve.tensor_tensor(s["rt"][:, :, 48:64], s["wr"][:], s["wb"][:], ALU.subtract).then_inc(S["route_ready"], 1)

        @block.scalar
        def _(act):
            act.wait_ge(S["zeroed"], 1)
            act.wait_ge(S["weights_in"], 16 * N_W)
            for h in range(HEADS):
                ins = act.activation(s["k_st"][QR:KR, h, :], s["pat_f"][QR:KR, :], ACT.Copy)
            ins.then_inc(S["key_rows_ready"], 1)
            act.wait_ge(S["consts_ready"], 3)
            with act.Fori(0, B) as i:
                act.wait_ge(S["batch_done"], i + 1)
                act.wait_ge(S["turned"], 4 * i + 1)
                act.activation(s["xT"][:, 0:T], w(1)[:, 0:T], ACT.Copy).then_inc(S["xT_ready"], 1)
                act.wait_ge(S["q_psum"], i + 1)
                act.activation(s["qk32"][:, 0, :], w(2)[:, 0:T], ACT.Identity, bias=s["bq4"][:],
                               scale=DH ** -0.5).then_inc(S["qk32_ready"], 1)
                act.wait_ge(S["k_psum"], i + 1)
                act.activation(s["qk32"][:, 1, :], w(3)[:, 0:T], ACT.Identity, bias=s["bk"][:],
                               scale=1.0).then_inc(S["qk32_ready"], 1)
                for a in range(2):
                    act.wait_ge(S["qk32_ready"], 2 * i + a + 1)
                    act.activation(s["qk_parts"][:, a, 0, :], s["qk32"][:, a, :], ACT.Copy).then_inc(S["qk_hi"], 1)
                for a in range(2):
                    act.wait_ge(S["qk_rest_ready"], 2 * i + a + 1)
                    act.activation(s["qk_parts"][:, a, 1, :], s["qk_rest"][:, a, :], ACT.Copy).then_inc(S["qk_mid"], 1)

                for g in range(GROUPS):
                    for n in range(GH * NT):
                        kt, j = divmod(n, GH)
                        act.wait_ge(S["logits_psum"], 48 * i + 24 * g + n + 1)
                        if kt >= 2:
                            act.wait_ge(S["av_done"], 12 * i + 6 * g + kt - 1)
                        act.activation(probs[0:rows_of(kt), kt % 2, j, :], w(n % 2)[0:rows_of(kt), 0:T],
                                       ACT.Exp).then_inc(S["exp_done"], 1)
                    act.wait_ge(S["av_done"], 12 * i + 6 * g + NT)
                    if g == 1:
                        act.wait_ge(S["att_ready"], 2 * i + 1)
                    act.activation(s["oT"], w(3)[:, 0:T], ACT.Copy).then_inc(S["oT_ready"], 1)

                act.wait_ge(S["turned"], 4 * i + 2)
                act.activation(s["xT"][:, 0:T], w(1)[:, 0:T], ACT.Identity, bias=s["ln1_b"][:],
                               scale=s["ln1_g"][:]).then_inc(S["xT_ready"], 1)
                for c in range(NCH):
                    act.wait_ge(S["m1_psum"], NCH * i + c + 1)
                    act.activation(s["gel"][:, c, 0:T], w(2 + c % 2)[:, 0:T], ACT.Gelu,
                                   bias=s["b_mlp1"][:, c:c + 1]).then_inc(S["gel_ready"], 1)
                act.wait_ge(S["turned"], 4 * i + 3)
                act.activation(s["xT"][:, 0:T], w(1)[:, 0:T], ACT.Copy).then_inc(S["xT_ready"], 1)
                act.activation(keep["n2T"][:, bass.ds(i, 1), :], w(1)[:, 0:T].unsqueeze(1), ACT.Copy)
                act.activation(keep["h1"][:, bass.ds(i, 1), :], s["r"][:].rearrange("p t c -> p (t c)").unsqueeze(1), ACT.Copy)
                act.wait_ge(S["gap_ready"], i + 1)
                act.activation(s["egap"][:], s["gap"][:], ACT.Exp).then_inc(S["egap_ready"], 1)
                act.wait_ge(S["turned"], 4 * i + 4)
                act.activation(keep["rt"][:, bass.ds(i, 1), :], w(3)[0:64, 0:T].unsqueeze(1),
                               ACT.Copy).then_inc(S["batch_done"], 1)

        @block.tensor
        def _(pe):
            pe.wait_ge(S["ident_ready"], 1)
            pe.wait_ge(S["patterns_in"], 16 * (5 + HEADS + HEADS))
            pe.wait_ge(S["consts_ready"], 3)
            pe.wait_ge(S["key_rows_ready"], 1)
            pe.wait_ge(S["band_ready"], HEADS)
            pe.wait_ge(S["rows_fixed"], 48 * HEADS)
            with pe.Fori(0, B) as i:
                def turn(slot, src):
                    for t in range(NT):
                        ins = pe.transpose(w(slot)[:, t * P:(t + 1) * P], src[:, t, :], keep["ident"][:])
                    ins.then_inc(S["turned"], 1)

                def over_tokens(slot, lhsT, rhs, start=True, stop=True):
                    for a, b in HALVES:
                        ins = pe.matmul(w(slot)[:, a:b], lhsT, rhs[:, a:b], start=start, stop=stop)
                    return ins

                pe.wait_ge(S["batch_done"], i + 1)
                pe.wait_ge(S["inputs_in"], 64 * i + 64)
                for t in range(2):
                    for c in range(PCH):
                        ins = pe.matmul(tm(0)[:, t, :], s["patches"][:, c, t * P:(t + 1) * P], s["w_tok"][:, c, :],
                                        start=c == 0, stop=c == PCH - 1)
                ins.then_inc(S["tokens_psum"], 1)
                pe.wait_ge(S["normed"], 4 * i + 1)
                turn(1, s["n1"])
                pe.wait_ge(S["xT_ready"], 3 * i + 1)
                over_tokens(2, s["w_qkv"][:, 0:HID], s["xT"]).then_inc(S["q_psum"], 1)
                over_tokens(3, s["w_qkv"][:, HID:2 * HID], s["xT"]).then_inc(S["k_psum"], 1)
                for t in range(NT):
                    ins = pe.matmul(tm(0)[:, t, :], s["xT"][:, t * P:(t + 1) * P], s["w_qkv"][:, 2 * HID:3 * HID],
                                    start=True, stop=True)
                ins.then_inc(S["v_psum"], 1)

                def scores(g, n):
                    t, j = divmod(n, GH)
                    h = g * GH + j
                    if n >= 1:
                        pe.wait_ge(S["maxed"], 48 * i + 24 * g + n)
                    for a, b in HALVES:
                        ins = pe.matmul(w(2)[:, a:b], s["q_st"][0:QR, h, t * P:(t + 1) * P], s["k_st"][0:QR, h, a:b],
                                        start=True, stop=True)
                    ins.then_inc(S["s_psum"], 1)

                def turn_top(g):
                    pe.wait_ge(S["maxed"], 48 * i + 24 * g + 24)
                    pe.transpose(w(2)[0:GH * NT, 0:P], s["top"][:], keep["ident"][:]).then_inc(S["top_turned"], 1)

                def logits(g, n):
                    kt, j = divmod(n, GH)
                    h, m, k0 = g * GH + j, rows_of(kt), kt * P
                    if n >= 2:
                        pe.wait_ge(S["exp_done"], 48 * i + 24 * g + n - 1)
                    out = w(n % 2)[0:m, :]
                    lo, hi = max(0, k0 - P), min(T, k0 + 2 * P)
                    for a, b in HALVES:
                        x, y = max(a, lo), min(b, hi)
                        ins = pe.matmul(out[:, a:b], s["k_st"][0:KR, h, k0:k0 + m], s["q_st"][0:KR, h, a:b],
                                        start=True, stop=True)
                        if x < y:
                            for part in range(3):
                                ins = pe.matmul(out[:, x:y], s["ident_b"][:, 0:m],
                                                s["bias_kq"][:, h, part, x - k0 + P:y - k0 + P],
                                                start=False, stop=part == 2, skip_group_check=True)
                    ins.then_inc(S["logits_psum"], 1)

                def values(g, kt):
                    m = rows_of(kt)
                    pe.wait_ge(S["exp_done"], 48 * i + 24 * g + GH * (kt + 1))
                    for a, b in HALVES:
                        for j in range(GH):
                            ins = pe.matmul(w(3)[32 * j:32 * j + 32, a:b], s["v"][0:m, kt, g * GH + j, :],
                                            probs[0:m, kt % 2, j, a:b], start=kt == 0, stop=kt == NT - 1,
                                            tile_position=(0, 32 * j))
                    ins.then_inc(S["av_done"], 1)

                def sums(g):
                    pe.wait_ge(S["oT_ready"], 2 * i + g + 1)
                    over_tokens(3, s["head_sum"][:], s["oT"]).then_inc(S["sum_psum"], 1)

                pe.wait_ge(S["stacked"], 192 * i + 192)
                pe.wait_ge(S["qk_hi"], 2 * i + 2)
                for n in range(GH * NT):
                    scores(0, n)
                turn_top(0)
                pe.wait_ge(S["v_ready"], i + 1)
                pe.wait_ge(S["top_rows_in"], 64 * i + 32)
                for n in range(GH * NT):
                    logits(0, n)
                    if n >= 1 and n % GH == 0:
                        values(0, n // GH - 1)
                    scores(1, n)
                values(0, NT - 1)
                turn_top(1)
                sums(0)
                pe.wait_ge(S["top_rows_in"], 64 * i + 64)
                for n in range(GH * NT):
                    logits(1, n)
                    if n == GH:
                        pe.wait_ge(S["att_ready"], 2 * i + 1)
                    if n >= 1 and n % GH == 0:
                        values(1, n // GH - 1)
                values(1, NT - 1)
                sums(1)
                pe.wait_ge(S["att_ready"], 2 * i + 2)
                for t in range(NT):
                    for g in range(GROUPS):
                        ins = pe.matmul(tm(0)[:, t, :], s["att"][:, g, t * P:(t + 1) * P], s["w_out"][:, g, :],
                                        start=g == 0, stop=g == GROUPS - 1)
                ins.then_inc(S["o_psum"], 1)
                pe.wait_ge(S["normed"], 4 * i + 2)
                turn(1, s["x1"])
                pe.wait_ge(S["xT_ready"], 3 * i + 2)
                for c in range(NCH):
                    if c >= 2:
                        pe.wait_ge(S["gel_ready"], NCH * i + c - 1)
                    over_tokens(2 + c % 2, s["w_mlp1"][:, c * P:(c + 1) * P], s["xT"]).then_inc(S["m1_psum"], 1)
                pe.wait_ge(S["gel_ready"], NCH * i + NCH)
                for t in range(NT):
                    for c in range(NCH):
                        pe.matmul(tm(0)[:, t, :], s["gel"][:, c, t * P:(t + 1) * P], s["w_mlp2"][:, c, :],
                                  start=c == 0, stop=False)
                    ins = pe.matmul(tm(0)[:, t, :], s["xT"][:, t * P:(t + 1) * P], keep["ident"][:], start=False, stop=True)
                ins.then_inc(S["m2_psum"], 1)
                pe.wait_ge(S["normed"], 4 * i + 4)
                turn(1, s["n1"])
                pe.wait_ge(S["xT_ready"], 3 * i + 3)
                for t in range(NT):
                    ins = pe.matmul(w(2)[:, t * E:(t + 1) * E], s["xT"][:, t * P:(t + 1) * P], s["router_w"][:],
                                    start=True, stop=True)
                ins.then_inc(S["route_psum"], 1)
                pe.wait_ge(S["route_ready"], i + 1)
                turn(3, s["rt"])




def expert_phase(nc, d, keep, ps):
    with ExitStack() as ctx:
        s = allocate(nc, ctx, {
            "wi": ([P, 2, 4 * HID], F32), "wh": ([P, 2, 4 * HID], F32), "wo": ([P, 2, HID], F32),
            "b": ([P, 2, 4], F32), "b1": ([P, 2, 4], F32),
            "pick_f": ([64, 2, PICKS, P], F32), "pick": ([64, 2, PICKS, P], BF16),
            "z": ([P, 2, 8], F32),
            "x": ([P, 4, T], F32),
            "gate": ([P, 2, 4, T], F32),
            "h_first": ([P, T], F32), "h": ([P, 2, T], F32), "c": ([P, 2, T], F32),
            "tc": ([P, T], F32), "ig": ([P, T], F32), "fc": ([P, T], F32),
            "part": ([P, 2, T], F32), "hs": ([P, 2, T], F32), "yT": ([P, B, T], F32),
            "spare": ([P, 1], F32), "bo_f": ([64, HID], F32), "bo_p": ([64, 3, HID], BF16),
            "yb": ([P, TPAD], F32), "out": ([P, NT, HID], F32),
        }, "e_")
        S = semaphores(nc, ctx, """
            first_weights weights0 weights1 pick_ready bo_zeroed bo_in bo_step bo_ready y_zeroed
            z_gates z_c z_tc z_h gate_psum gate_read aux_psum aux_read masked ig_ready fc_ready c_ready tc_ready
            h_ready hs_ready biased yb_ready turned_y out_ready stored
        """, "e_")
        IG, FG, GG, OG = range(4)
        ZI, ZG, ZO, ZC, ZT, ZH = range(6)
        weights_in = (S["weights0"], S["weights1"])
        N_LOADS = 5

        UNITS = [(0, None), (1, 0), (1, 1), (2, 0), (2, 1), (3, None)]
        NU = len(UNITS)
        ORDER = [[IG, GG, OG] if st == 0 else [IG, GG, FG, OG] for st, _ in UNITS]
        BEFORE = [sum(len(o) for o in ORDER[:n]) for n in range(NU + 1)]
        NG = BEFORE[NU]
        AUX = [("mask", 1, 0), ("mask", 1, 1), ("b1",), ("mask", 2, 0), ("mask", 2, 1), ("seed", 0, 0),
               ("seed", 0, 1), ("scale", 0, W01), ("y", 0), ("scale", 1, W0), ("scale", 1, W1), ("y", 1),
               ("scale", 2, W0), ("scale", 2, W1), ("merge", 3, M1), ("y", 2), ("scale", 3, W01), ("y", 3)]
        NA = len(AUX)
        FREE = 2


        def at(i, u, per, n):
            return 2 * per * i + per * u + n

        block = ctx.enter_context(nc.Block())

        @block.sync
        def _(sp):
            sp.wait_ge(S["bo_zeroed"], 1)
            for part in range(3):
                for k in range(2):
                    row = 16 + 16 * part + E * k
                    sp.dma_start(s["bo_f"][row:row + E, :], d["bo"]).then_inc(S["bo_in"], 16)

            def load(u, e):
                for dst, src in ((s["wi"][:, u, :], d["Wi"][bass.ds(e, 1)].rearrange("o p n -> (o p) n")),
                                 (s["wh"][:, u, :], d["Wh"][bass.ds(e, 1)].rearrange("o p n -> (o p) n")),
                                 (s["wo"][:, u, :], d["Wo"][bass.ds(e, 1)].rearrange("o p n -> (o p) n")),
                                 (s["b"][:, u, :], d["b"][bass.ds(e, 1)].rearrange("o p g -> (o p) g")),
                                 (s["pick_f"][:, u, :, :], d["c_pick"][bass.ds(e, 1)].rearrange("o p a n -> (o p) a n"))):
                    sp.dma_start(dst, src).then_inc(weights_in[u], 16)

            load(0, 0)
            load(1, 1)
            with sp.Fori(1, E // 2) as i:
                for u in range(2):
                    sp.wait_ge(S["aux_read"], FREE + at(i, u, NA, -NA))
                    load(u, 2 * i + u)
            with sp.Fori(0, B) as b:
                sp.wait_ge(S["out_ready"], b + 1)
                dst = d["out"][bass.ds(b, 1)].rearrange("o t c -> (o t) c")
                sp.dma_start(dst[0:(NT - 1) * P, :].rearrange("(t p) c -> p t c", p=P),
                             s["out"][:, 0:NT - 1, :]).then_inc(S["stored"], 16)
                sp.dma_start(dst[(NT - 1) * P:T, :], s["out"][0:LAST, NT - 1, :]).then_inc(S["stored"], 16)
            sp.wait_ge(S["stored"], 32 * B + 32)

        @block.gpsimd
        def _(pool):
            pool.memset(s["bo_f"][:], 0.0).then_inc(S["bo_zeroed"], 1)
            pool.memset(s["yT"][:], 0.0)
            pool.memset(s["yb"][:], 0.0).then_inc(S["y_zeroed"], 1)
            pool.sem_inc(S["h_ready"], FREE)
            pool.sem_inc(S["gate_read"], FREE)
            pool.sem_inc(S["aux_read"], FREE)
            pool.sem_inc(S["stored"], 32)
            with pool.Fori(0, E // 2) as i:
                for u in range(2):
                    for n, (st, k) in enumerate(UNITS):
                        gate = s["gate"][:, n % 2]
                        pool.wait_ge(S["gate_read"], FREE + at(i, u, NG, BEFORE[n] + 2))
                        if n == 0:
                            if u:
                                pool.wait_ge(S["c_ready"], at(i, u, NU, 0))
                            else:
                                pool.wait_ge(S["h_ready"], FREE + at(i, u, NU, 0))
                            pool.tensor_tensor(s["ig"][:], gate[:, IG, :], gate[:, GG, :], ALU.mult).then_inc(S["c_ready"], 1)
                        else:
                            if n == 1:
                                pool.wait_ge(S["aux_read"], FREE + at(i, u, NA, 7))
                            else:
                                pool.wait_ge(S["c_ready"], at(i, u, NU, n))
                            pool.tensor_tensor(s["ig"][:], gate[:, IG, :], gate[:, GG, :], ALU.mult).then_inc(S["ig_ready"], 1)
                        if (st, k) in ((1, 1), (2, 1)):
                            pool.wait_ge(S["aux_read"], FREE + at(i, u, NA, 11 if st == 1 else 14))
                            pool.tensor_tensor(s["hs"][:, st % 2, :], s["part"][:, 0, :], s["part"][:, 1, :],
                                               ALU.add).then_inc(S["hs_ready"], 1)

        @block.vector
        def _(dve):
            dve.wait_ge(S["bo_in"], 16 * 6)
            for part in range(3):
                dve.tensor_copy(s["bo_p"][:, part, :], s["bo_f"][:]).then_inc(S["bo_step"] if part < 2 else S["bo_ready"], 1)
                if part < 2:
                    dve.wait_ge(S["bo_step"], 2 * part + 1)
                    dve.tensor_tensor(s["bo_f"][:], s["bo_f"][:], s["bo_p"][:, part, :], ALU.subtract).then_inc(S["bo_step"], 1)
                    dve.wait_ge(S["bo_step"], 2 * part + 2)
            dve.wait_ge(S["y_zeroed"], 1)
            with dve.Fori(0, E // 2) as i:
                for u in range(2):
                    z = s["z"][:, u, :]

                    def aux(n):
                        dve.wait_ge(S["aux_psum"], at(i, u, NA, n + 1))
                        return ps[2 + n % 2][:, 0:T]

                    def mask(n):
                        _, st, k = AUX[n]
                        dve.tensor_tensor(s["x"][:, 2 * (st - 1) + k, :], keep["n2T"][:, st, :], aux(n),
                                          ALU.mult).then_inc(S["aux_read"], 1)

                    def seed(n):
                        k = AUX[n][2]
                        m = aux(n)
                        dve.scalar_tensor_tensor(s["h"][:, k, :], s["h_first"][:], z[:, ZH:ZH + 1], m,
                                                 ALU.subtract, ALU.mult)
                        dve.scalar_tensor_tensor(s["c"][:, k, :], s["ig"][:], z[:, ZC:ZC + 1], m,
                                                 ALU.subtract, ALU.mult).then_inc(S["aux_read"], 1)

                    def output(n):
                        y = s["yT"][:, AUX[n][1], :]
                        dve.tensor_tensor(y, y, aux(n), ALU.add).then_inc(S["aux_read"], 1)

                    def scale(n, src, dst):
                        dve.tensor_tensor(dst, src, aux(n), ALU.mult).then_inc(S["aux_read"], 1)

                    def cell(n):
                        st, k = UNITS[n]
                        k = k or 0
                        gate = s["gate"][:, n % 2]
                        done = at(i, u, NU, n + 1)
                        if st:
                            dve.wait_ge(S["gate_read"], FREE + at(i, u, NG, BEFORE[n] + 3))
                            if st == 1:
                                dve.scalar_tensor_tensor(s["fc"][:], s["c"][:, k, :], z[:, ZC:ZC + 1], gate[:, FG, :],
                                                         ALU.add, ALU.mult).then_inc(S["fc_ready"], 1)
                            else:
                                dve.tensor_tensor(s["fc"][:], s["c"][:, k, :], gate[:, FG, :], ALU.mult).then_inc(S["fc_ready"], 1)
                            dve.wait_ge(S["fc_ready"], at(i, u, NU - 1, n))
                            dve.wait_ge(S["ig_ready"], at(i, u, NU - 1, n))
                            dve.tensor_tensor(s["c"][:, k, :], s["fc"][:], s["ig"][:], ALU.add).then_inc(S["c_ready"], 1)
                        dve.wait_ge(S["tc_ready"], done)
                        dst = s["h"][:, k, :] if st else s["h_first"][:]
                        dve.tensor_tensor(dst, gate[:, OG, :], s["tc"][:], ALU.mult).then_inc(S["h_ready"], 1)

                    def h_is_there(n):
                        dve.wait_ge(S["h_ready"], FREE + at(i, u, NU, n + 1))

                    dve.wait_ge(S["pick_ready"], at(i, u, 1, 1))
                    mask(0)
                    mask(1)
                    dve.wait_ge(S["z_gates"], at(i, u, 1, 1))
                    dve.tensor_tensor(z[:, ZC:ZC + 1], z[:, ZI:ZI + 1], z[:, ZG:ZG + 1], ALU.mult).then_inc(S["z_c"], 1)
                    dve.wait_ge(S["z_tc"], at(i, u, 1, 1))
                    dve.tensor_tensor(z[:, ZH:ZH + 1], z[:, ZO:ZO + 1], z[:, ZT:ZT + 1], ALU.mult).then_inc(S["z_h"], 1)
                    dve.tensor_tensor(s["b1"][:, u, :], aux(2)[:, 0:4], s["b"][:, u, :], ALU.add).then_inc(S["aux_read"], 1)
                    mask(3)
                    mask(4)
                    cell(0)
                    h_is_there(0)
                    dve.wait_ge(S["z_h"], at(i, u, 1, 1))
                    seed(5)
                    seed(6)
                    scale(7, s["h_first"][:], s["hs"][:, 0, :])
                    cell(1)
                    output(8)
                    h_is_there(1)
                    scale(9, s["h"][:, 0, :], s["part"][:, 0, :])
                    cell(2)
                    h_is_there(2)
                    scale(10, s["h"][:, 1, :], s["part"][:, 1, :])
                    cell(3)
                    output(11)
                    h_is_there(3)
                    scale(12, s["h"][:, 0, :], s["part"][:, 0, :])
                    cell(4)
                    h_is_there(4)
                    scale(13, s["h"][:, 1, :], s["part"][:, 1, :])
                    m = aux(14).bitcast(I32)
                    apart(dve, s["spare"])
                    dve.copy_predicated(s["h"][:, 0, :], m, s["h"][:, 1, :])
                    dve.copy_predicated(s["c"][:, 0, :], m, s["c"][:, 1, :]).then_inc(S["aux_read"], 1)
                    dve.wait_ge(S["aux_read"], FREE + at(i, u, NA, 15))
                    cell(5)
                    output(15)
                    h_is_there(5)
                    scale(16, s["h"][:, 0, :], s["hs"][:, 1, :])
                    output(17)
            with dve.Fori(0, B) as b:
                dve.wait_ge(S["biased"], b + 1)
                dve.tensor_tensor(s["yb"][:, 0:T].unsqueeze(1), ps[0][:, 0:T].unsqueeze(1), s["yT"][:, bass.ds(b, 1), :],
                                  ALU.add).then_inc(S["yb_ready"], 1)
                dve.wait_ge(S["turned_y"], b + 1)
                dve.wait_ge(S["stored"], 32 * b + 32)
                dve.tensor_tensor(s["out"][:].rearrange("p t c -> p (t c)").unsqueeze(1), ps[1][:, 0:TPAD].unsqueeze(1),
                                  keep["h1"][:, bass.ds(b, 1), :], ALU.add).then_inc(S["out_ready"], 1)

        @block.scalar
        def _(act):
            with act.Fori(0, E // 2) as i:
                for u in range(2):
                    z = s["z"][:, u, :]
                    b, b1 = s["b"][:, u, :], s["b1"][:, u, :]
                    act.wait_ge(weights_in[u], 16 * N_LOADS * i + 16 * N_LOADS)
                    act.activation(s["pick"][:, u, :, :], s["pick_f"][:, u, :, :], ACT.Copy).then_inc(S["pick_ready"], 1)
                    act.activation(z[:, ZI:ZI + 1], b[:, IG:IG + 1], ACT.Sigmoid)
                    act.activation(z[:, ZG:ZG + 1], b[:, GG:GG + 1], ACT.Tanh)
                    act.activation(z[:, ZO:ZO + 1], b[:, OG:OG + 1], ACT.Sigmoid).then_inc(S["z_gates"], 1)
                    act.wait_ge(S["z_c"], at(i, u, 1, 1))
                    act.activation(z[:, ZT:ZT + 1], z[:, ZC:ZC + 1], ACT.Tanh).then_inc(S["z_tc"], 1)
                    for n, (st, k) in enumerate(UNITS):
                        unit = at(i, u, NU, n)
                        act.wait_ge(S["h_ready"], unit + 1)
                        for m, g in enumerate(ORDER[n]):
                            place = BEFORE[n] + m
                            slot = (NG * u + place) % 2
                            act.wait_ge(S["gate_psum"], at(i, u, NG, place + 1))
                            if st == 1 and m == 0:
                                act.wait_ge(S["aux_read"], FREE + at(i, u, NA, 3))
                            act.activation(s["gate"][:, n % 2, g, :], ps[slot][:, 0:T],
                                           ACT.Tanh if g == GG else ACT.Sigmoid,
                                           bias=(b1 if st == 1 else b)[:, g:g + 1]).then_inc(S["gate_read"], 1)
                        act.wait_ge(S["c_ready"], unit + 1)
                        act.wait_ge(S["h_ready"], unit + FREE)
                        act.activation(s["tc"][:], s["c"][:, k or 0, :] if st else s["ig"][:], ACT.Tanh).then_inc(S["tc_ready"], 1)

        @block.tensor
        def _(pe):
            pe.wait_ge(S["bo_ready"], 1)
            with pe.Fori(0, E // 2) as i:
                for u in range(2):
                    def both(slot, lhsT, rhs, start=True, stop=True):
                        for a, b in HALVES:
                            ins = pe.matmul(ps[slot][:, a:b], lhsT, rhs[:, a:b], start=start, stop=stop)
                        return ins

                    def aux(n):
                        what = AUX[n]
                        pe.wait_ge(S["aux_read"], at(i, u, NA, n + 1))
                        slot = 2 + n % 2
                        if what[0] == "y":
                            pe.wait_ge(S["aux_read"] if what[1] in (0, 3) else S["hs_ready"],
                                       FREE + at(i, u, NA, n) if what[1] in (0, 3) else at(i, u, 2, what[1]))
                            ins = both(slot, s["wo"][:, u, :], s["hs"][:, what[1] % 2, :])
                        elif what[0] == "b1":
                            pe.wait_ge(S["z_h"], at(i, u, 1, 1))
                            for g in range(4):
                                ins = pe.matmul(ps[slot][:, g:g + 1], s["wh"][:, u, g * HID:(g + 1) * HID],
                                                s["z"][:, u, ZH:ZH + 1], start=True, stop=True)
                        else:
                            st = what[1]
                            row = what[2] if what[0] in ("scale", "merge") else (M0, M1)[what[2]]
                            ins = both(slot, s["pick"][:, u, row, :], keep["rt"][:, st, :])
                        ins.then_inc(S["aux_psum"], 1)

                    def gates(n, then={}):
                        st, k = UNITS[n]
                        x = keep["n2T"][:, st, :] if k is None else s["x"][:, 2 * (st - 1) + k, :]
                        if k is not None:
                            pe.wait_ge(S["aux_read"], FREE + at(i, u, NA, {(1, 0): 1, (1, 1): 2, (2, 0): 4, (2, 1): 5}[st, k]))
                        for m, g in enumerate(ORDER[n]):
                            place = BEFORE[n] + m
                            slot = (NG * u + place) % 2
                            cols = slice(g * HID, (g + 1) * HID)
                            pe.wait_ge(S["gate_read"], at(i, u, NG, place + 1))
                            ins = both(slot, s["wi"][:, u, cols], x, stop=st == 0)
                            if st:
                                if m == 0 and st == 1:
                                    pe.wait_ge(S["aux_read"], FREE + at(i, u, NA, 6 + k))
                                if m == 0 and st == 2:
                                    pe.wait_ge(S["h_ready"], FREE + at(i, u, NU, n - 1))
                                if m == 0 and st == 3:
                                    pe.wait_ge(S["aux_read"], FREE + at(i, u, NA, 15))
                                ins = both(slot, s["wh"][:, u, cols], s["h"][:, k or 0, :], start=False)
                            ins.then_inc(S["gate_psum"], 1)
                            for a in then.get(m, ()):
                                aux(a)

                    pe.wait_ge(weights_in[u], 16 * N_LOADS * i + 16 * N_LOADS)
                    pe.wait_ge(S["pick_ready"], at(i, u, 1, 1))
                    aux(0)
                    aux(1)
                    gates(0, {0: [2], 2: [3, 4, 5, 6]})
                    gates(1, {0: [7], 3: [8]})
                    gates(2, {0: [9], 3: [10]})
                    gates(3, {2: [11], 3: [12]})
                    gates(4, {3: [13, 14]})
                    gates(5, {2: [15, 16], 3: [17]})
            with pe.Fori(0, B) as b:
                pe.wait_ge(S["aux_read"], FREE + NA * E)
                for a, z in HALVES:
                    for part in range(3):
                        ins = pe.matmul(ps[0][:, a:z].unsqueeze(1), s["bo_p"][:, part, :], keep["rt"][:, bass.ds(b, 1), a:z],
                                        start=part == 0, stop=part == 2)
                ins.then_inc(S["biased"], 1)
                pe.wait_ge(S["yb_ready"], b + 1)
                for t in range(NT):
                    ins = pe.transpose(ps[1][:, t * P:(t + 1) * P], s["yb"][:, t * P:(t + 1) * P], keep["ident"][:])
                ins.then_inc(S["turned_y"], 1)


def build(nc, d, scratch):
    with ExitStack() as ctx:
        keep = allocate(nc, ctx, {
            "ident": ([P, P], F32),
            "h1": ([P, B, TPAD], F32),
            "n2T": ([P, B, T], F32),
            "rt": ([64, B, T], BF16),
        }, "k_")
        ps = [ctx.enter_context(nc.psum_tensor(f"ps{n}", [P, 2 * HALF], F32)) for n in range(4)]
        attention_phase(nc, d, keep, ps, scratch)
        expert_phase(nc, d, keep, ps)


def arranged(x, txt, **p):
    import numpy as np

    f = lambda a: np.ascontiguousarray(np.asarray(a))
    x = f(x).reshape(B, 3, NP_SIDE, NP_SIDE, NP_SIDE, NP_SIDE)
    patches = np.zeros((B, PATCH_DIM, 2 * P), np.float32)
    patches[:, :, 1:1 + N_PATCH] = x.transpose(0, 1, 3, 5, 2, 4).reshape(B, PATCH_DIM, N_PATCH)
    table = f(p["L0_attn_rel_table"]).T
    side = TPAD - MAXD
    ext = np.pad(table, ((0, 0), (side, side - 1)), mode="edge")
    row, col, band = np.arange(P)[:, None], np.arange(GW)[None, :], np.arange(BAND)[None, :]
    head_sum = np.zeros((P, P), np.float32)
    for j in range(GH):
        head_sum[32 * j + DH, 32 * j:32 * j + 32] = 1.0
    key_rows = np.zeros((XR, TPAD), np.float32)
    key_rows[0:2] = 1.0
    for r in range(3 * NT):
        key_rows[2 + r, (r % NT) * P:(r % NT + 1) * P] = 1.0
    pick = np.zeros((E, 64, PICKS, P), np.float32)
    for e in range(E):
        pick[e, e, M0] = pick[e, E + e, M1] = 1.0
        for part in range(3):
            r = 16 + 16 * part + e
            pick[e, r, W0] = pick[e, r, W01] = pick[e, r + E, W1] = pick[e, r + E, W01] = 1.0
    return {
        "patches": patches, "txt": f(txt), "tok_W": f(f(p["L0_tok_W"]).T), "tok_b": f(p["L0_tok_b"]),
        "token": f(p["L0_tok_token"]), "pos": f(p["L0_tok_pos"]),
        "w_qkv": f(p["L0_attn_w_qkv"]), "b_qkv": f(p["L0_attn_b_qkv"]), "w_out": f(p["L0_attn_w_out"]),
        "b_out": f(p["L0_attn_b_out"]), "ln1_g": f(p["L0_attn_ln1_g"]), "ln1_b": f(p["L0_attn_ln1_b"]),
        "ln2_g": f(p["L0_attn_ln2_g"]), "ln2_b": f(p["L0_attn_ln2_b"]), "w_mlp1": f(p["L0_attn_w_mlp1"]),
        "b_mlp1": f(p["L0_attn_b_mlp1"]), "w_mlp2": f(p["L0_attn_w_mlp2"]), "b_mlp2": f(p["L0_attn_b_mlp2"]),
        "rel_ext": f(ext), "rel_strip": f(ext[:, TPAD + row - col + (NT - 1) * P]),
        "rel_band": f(ext[:, TPAD - P + band - row]),
        "router_w": f(p["L0_ffn_router_w"]), "router_b": f(p["L0_ffn_router_b"]),
        "Wi": f(p["L0_ffn_Wi"]), "Wh": f(p["L0_ffn_Wh"]), "b": f(f(p["L0_ffn_b"]).reshape(E, 4, HID).transpose(0, 2, 1)), "Wo": f(p["L0_ffn_Wo"]),
        "bo": f(p["L0_ffn_bo"]),
        "c_ident": np.eye(P, dtype=np.float32), "c_head_sum": head_sum, "c_key_rows": key_rows, "c_pick": pick,
    }


def kernel(**inputs):
    import concourse.bacc as bacc
    from concourse.bass_utils import run_bass_kernel_spmd

    nc = bacc.Bacc("TRN2", target_bir_lowering=False, num_devices=1)
    arrays = {f"in_{name}": a for name, a in arranged(**inputs).items()}
    d = {
        name[3:]: nc.dram_tensor(name, a.shape, mybir.dt.from_np(a.dtype), kind="ExternalInput").ap()
        for name, a in arrays.items()}
    d["out"] = nc.dram_tensor("out_0", (B, T, HID), F32, kind="ExternalOutput").ap()
    scratch = nc.dram_tensor("qk_scratch", (2, 3, P, T), BF16, kind="Internal").ap()
    build(nc, d, scratch)
    return run_bass_kernel_spmd(nc, [arrays], core_ids=[0]).results[0]["out_0"]
```

```python
from contextlib import ExitStack

import concourse.bass as bass
from concourse import mybir

F32 = mybir.dt.float32
BF16 = mybir.dt.bfloat16
U32 = mybir.dt.uint32
I32 = mybir.dt.int32
ALU = mybir.AluOpType
ACT = mybir.ActivationFunctionType

P = 128
B = 4
HID = 128
HEADS = 8
DH = HID // HEADS
NP_SIDE = 14
N_PATCH = NP_SIDE * NP_SIDE
PATCH_DIM = 3 * NP_SIDE * NP_SIDE
PCH = 6
PROWS = PATCH_DIM // PCH
TXT = 512
T = 1 + N_PATCH + TXT
NT = -(-T // P)
TPAD = NT * P
LAST = T - (NT - 1) * P
TXT0 = 1 + N_PATCH - P
HALF = 512
INNER = 512
NCH = INNER // P
MAXD = 128
GW = (NT - 1) * P + T
BAND = 3 * P
QR = 96
XR = 2 + 3 * NT
KR = QR + XR
GROUPS = 2
GH = HEADS // GROUPS
E = 8
EPS = 1e-5
LOWEST = -3.0e38
HALVES = [(0, HALF), (HALF, T)]
PAIRS = ((0, 3), (1, 2), (2, 1))

M0, M1, W0, W1, W01 = range(5)
PICKS = 5


R_BV, R_BOUT, R_BMLP2, R_LN2G, R_LN2B = (slice(n * HID, n * HID + HID) for n in range(5))
R_RB = slice(5 * HID, 5 * HID + E)
ROWS_N = 5 * HID + E
C_BQ, C_BK, C_LN1G, C_LN1B, C_BMLP1 = range(5)
COLS_N = C_BMLP1 + NCH


def rows_of(t):
    return P if t < NT - 1 else LAST


def dram(ap, offset, pattern):
    return bass.AP(tensor=ap.tensor, offset=offset, ap=pattern)


def apart(dve, spare):
    dve.memset(spare[0:1, 0:1], 0.0)


def every_partition(ap, n):
    return dram(ap, 0, [[0, P], [1, n]])


def allocate(nc, ctx, spec, prefix):
    return {name: ctx.enter_context(nc.sbuf_tensor(prefix + name, shape, dt)) for name, (shape, dt) in spec.items()}


def semaphores(nc, ctx, names, prefix):
    return {name: ctx.enter_context(nc.semaphore(prefix + name)) for name in names.split()}


class Slots:

    def __init__(self, pe):
        self.pe, self.read = pe, {}

    def take(self, slot, sem, value):
        if slot in self.read:
            self.pe.wait_ge(*self.read[slot])
        self.read[slot] = (sem, value)


def over_tokens(pe, out, lhsT, rhs, start=True, stop=True):
    for a, b in HALVES:
        ins = pe.matmul(out[:, a:b], lhsT, rhs[:, a:b], start=start, stop=stop)
    return ins


def turn(pe, out, src, ident):
    for t in range(NT):
        ins = pe.transpose(out[:, t * P:(t + 1) * P], src[:, t, :], ident)
    return ins


def tiles(slot):
    return slot[:, 0:TPAD].rearrange("p (t c) -> p t c", t=NT)


def over_tiles(row):
    return row.unsqueeze(1).broadcast_to([P, NT, HID])


def norm_stats(dve, s, S, b, src):
    for t in range(NT):
        ins = dve.bn_stats(s["stats"][:, b, t, :], src[:, t, :])
    ins.then_inc(S["stats_ready"], 1)


def norm_moments(dve, s, S, b, n):
    dve.wait_ge(S["stats_ready"], n + 1)
    for t in range(NT):
        ins = dve.bn_aggr(s["mom"][:, b, t, :], s["stats"][:, b, t, :])
    ins.then_inc(S["moments_ready"], 1)


def norm_rstd(pool, s, S, b, n):
    pool.wait_ge(S["moments_ready"], n + 1)
    pool.tensor_tensor(s["veps"][:, b, :], s["mom"][:, b, :, 1], s["eps"][:], ALU.add).then_inc(S["veps_ready"], 1)
    pool.wait_ge(S["veps_ready"], n + 1)
    pool.tensor_tensor(s["rstd"][:, b, :], s["veps"][:, b, :], s["minus_half"][:], ALU.pow).then_inc(S["rstd_ready"], 1)


def norm_apply(dve, s, S, b, n, src, dst):
    dve.wait_ge(S["rstd_ready"], n + 1)
    for t in range(NT):
        ins = dve.tensor_scalar(dst[:, t, :], src[:, t, :], s["mom"][:, b, t, 0:1], s["rstd"][:, b, t:t + 1],
                                ALU.subtract, ALU.mult)
    ins.then_inc(S["normed"], 1)


NORM_TILES = {
    "stats": ([P, B, NT, 6], F32), "mom": ([P, B, NT, 2], F32), "veps": ([P, B, NT], F32),
    "rstd": ([P, B, NT], F32), "eps": ([P, NT], F32), "minus_half": ([P, NT], F32),
}
NORM_SEMS = "stats_ready moments_ready veps_ready rstd_ready normed "


def embedding_phase(nc, d, keep, across, ps):
    with ExitStack() as ctx:
        s = allocate(nc, ctx, {
            "w_tok": ([PROWS, PCH, HID], F32), "w_qkv": ([P, 3 * HID], F32),
            "pos_b": ([P, 2, HID], F32), "tok_add": ([P, 2, HID], F32), "txt1": ([P, B, HID], F32),
            "bq4": ([P, 1], F32), "parts": ([P, 2, 2, 3, T], BF16),
            "key_rows": ([P, TPAD], F32),
            **NORM_TILES,
        }, "m_")
        S = semaphores(nc, ctx, NORM_SEMS + """
            cleared embed_in embed_in1 embed_in2 embed_in3 weights_in ident_in const_in band_in strips_in
            patches_in0 patches_in1 pos_ready patches_used bq4_ready eps_ready
            tokens_psum text_added h0_ready n1b_ready turned xT_ready
            q_psum k_psum v_psum q32_ready k32_ready hi_ready rest_ready mid_ready lo_ready v_ready parts_out0 parts_out1
            const_step const_ready const_out fixed_rows_in band_step band_ready stacks_cleared key_rows_ready v_ones
        """, "m_")
        embed_in = (S["embed_in"], S["embed_in1"], S["embed_in2"], S["embed_in3"])
        patches_in = (S["patches_in0"], S["patches_in1"])
        parts_out = (S["parts_out0"], S["parts_out1"])
        h0 = keep["h1"][:, :, :].rearrange("p b (t c) -> p b t c", t=NT)
        n1 = across["n1b"]
        s["band_f"] = across["att"][:, 0:2].rearrange("p b g (a n) -> p (b g a) n", a=2)
        last_strips = across["bias_qk"][0:HEADS * NT, HEADS - 2:HEADS, :].rearrange("p h n -> p (h n)")
        s["const_f"] = last_strips[:, 0:T]
        s["const_p"] = last_strips[:, T:T + 3 * T // 2 + 1].bitcast(BF16)[:, 0:3 * T].rearrange("p (m n) -> p m n", m=3)
        s["xT"] = across["att"][:, 2:4].rearrange("p b g n -> p (b g) n")
        s["qk32"], s["rest"] = keep["n2T"][:, 0:2, :], keep["n2T"][:, 2:4, :]
        s["patches"] = across["k_st"][0:PROWS].rearrange("p g h n -> p (g h n)").bitcast(F32).rearrange(
            "p (u c n) -> p u c n", u=2, c=PCH)
        block = ctx.enter_context(nc.Block())

        def load_patches(eng, b):
            eng.dma_start(s["patches"][:, b % 2, :, :], d["patches"][b, :, :].rearrange("(c p) n -> p c n", p=PROWS)
                          ).then_inc(patches_in[b % 2], 16)

        @block.sync
        def _(sp):
            load_patches(sp, 0)
            sp.dma_start(s["w_tok"][:], d["tok_W"].rearrange("(c p) n -> p c n", p=PROWS)).then_inc(S["weights_in"], 16)
            sp.dma_start(s["pos_b"][:], d["pos"]).then_inc(S["weights_in"], 16)
            sp.dma_start(s["tok_add"][:], d["tok_add"]).then_inc(S["weights_in"], 16)
            load_patches(sp, 1)
            sp.wait_ge(S["cleared"], 1)
            first = P - TXT0
            for b in range(B):
                sp.dma_start(s["txt1"][TXT0:P, b, :], d["txt"][b, 0:first, :]).then_inc(embed_in[b], 16)
                sp.dma_start(h0[:, b, 2:NT - 1, :], d["txt"][b, first:first + (NT - 3) * P, :].rearrange(
                    "(t p) c -> p t c", p=P)).then_inc(embed_in[b], 16)
                sp.dma_start(h0[0:LAST, b, NT - 1, :], d["txt"][b, TXT - LAST:TXT, :]).then_inc(embed_in[b], 16)
            for b in range(2, B):
                sp.wait_ge(S["tokens_psum"], b - 1)
                load_patches(sp, b)
            for b in range(B):
                sp.wait_ge(S["lo_ready"], 2 * b + 2)
                row = 0
                for part, count in PAIRS:
                    for _ in range(count):
                        sp.dma_start(d["q_parts"][b, row:row + DH].rearrange("x h n -> h x n"),
                                     s["parts"][:, b % 2, 0, part, :]).then_inc(parts_out[b % 2], 16)
                        row += DH
                for part in range(3):
                    sp.dma_start(d["k_parts"][b, part * DH:(part + 1) * DH].rearrange("x h n -> h x n"),
                                 s["parts"][:, b % 2, 1, part, :]).then_inc(parts_out[b % 2], 16)
            sp.wait_ge(S["const_ready"], 1)
            sp.dma_start(d["const_d"].rearrange("m k h n -> (k h) m n"), s["const_p"]).then_inc(S["const_out"], 16)
            sp.wait_ge(S["const_out"], 16)
            for h in range(HEADS - 2, HEADS):
                sp.dma_start(across["bias_qk"][:, h, :], d["rel_strip"][h, :, :]).then_inc(S["strips_in"], 16)
            sp.wait_ge(S["stacks_cleared"], 1)
            for g in range(GROUPS):
                sp.dma_start(across["q_st"][QR + 2:KR, g, :, 0:T], d["const_d"][:, :, g * GH:(g + 1) * GH, :].rearrange(
                    "m k h n -> (m k) h n")).then_inc(S["fixed_rows_in"], 16)
            sp.wait_ge(S["fixed_rows_in"], 16 * GROUPS)
            sp.wait_ge(parts_out[0], 16 * 9 * B // 2)
            sp.wait_ge(parts_out[1], 16 * 9 * B // 2)
            sp.wait_ge(S["strips_in"], 16 * (HEADS + 1))

        @block.scalar
        def _(act):
            act.dma_start(keep["ident"][:], d["c_ident"]).then_inc(S["ident_in"], 16)
            act.dma_start(across["cols"][:], d["cols"]).then_inc(S["ident_in"], 16)
            act.dma_start(across["rows"][:], every_partition(d["rows"], ROWS_N)).then_inc(S["ident_in"], 16)
            act.dma_start(s["w_qkv"][:], d["w_qkv"]).then_inc(S["ident_in"], 16)
            act.dma_start(s["const_f"][:], d["const_rows"]).then_inc(S["const_in"], 16)
            act.dma_start(s["key_rows"][QR:KR, :], d["c_key_rows"]).then_inc(S["const_in"], 16)
            act.dma_start(s["band_f"][:], d["rel_band"].rearrange("h p n -> p h n")).then_inc(S["band_in"], 16)
            for h in range(HEADS - 2):
                act.dma_start(across["bias_qk"][:, h, :], d["rel_strip"][h, :, :]).then_inc(S["strips_in"], 16)
            act.dma_start(across["head_sum"][:], d["c_head_sum"]).then_inc(S["strips_in"], 16)
            act.wait_ge(S["ident_in"], 64)
            act.activation(s["bq4"][:], across["cols"][:, C_BQ:C_BQ + 1], ACT.Copy, scale=DH ** -0.5).then_inc(S["bq4_ready"], 1)
            for b in range(B):
                act.wait_ge(S["turned"], b + 1)
                act.activation(s["xT"][:, b, :], ps[b][:, 0:TPAD], ACT.Copy).then_inc(S["xT_ready"], 1)
            act.wait_ge(S["bq4_ready"], 1)
            for b in range(B):
                if b >= 1:
                    act.wait_ge(S["lo_ready"], 2 * b)
                if b >= 2:
                    act.wait_ge(parts_out[b % 2], 16 * 9 * (b // 2))
                act.wait_ge(S["q_psum"], b + 1)
                act.activation(s["qk32"][:, 0, :], ps[(3 * b) % 4][:, 0:T], ACT.Identity, bias=s["bq4"][:],
                               scale=DH ** -0.5).then_inc(S["q32_ready"], 1)
                act.wait_ge(S["k_psum"], b + 1)
                act.activation(s["qk32"][:, 1, :], ps[(3 * b + 1) % 4][:, 0:T], ACT.Identity, bias=across["cols"][:, C_BK:C_BK + 1],
                               scale=1.0).then_inc(S["k32_ready"], 1)
                for x, ready in enumerate((S["q32_ready"], S["k32_ready"])):
                    act.wait_ge(ready, b + 1)
                    act.activation(s["parts"][:, b % 2, x, 0, :], s["qk32"][:, x, :], ACT.Copy).then_inc(S["hi_ready"], 1)
                for x in range(2):
                    act.wait_ge(S["rest_ready"], 2 * b + x + 1)
                    act.activation(s["parts"][:, b % 2, x, 1, :], s["rest"][:, x, :], ACT.Copy).then_inc(S["mid_ready"], 1)
            act.wait_ge(S["const_in"], 32)
            act.wait_ge(S["stacks_cleared"], 1)
            for g in range(GROUPS):
                for j in range(GH):
                    ins = act.activation(across["k_st"][QR:KR, g, j, :], s["key_rows"][QR:KR, :], ACT.Copy)
            ins.then_inc(S["key_rows_ready"], 1)

        @block.gpsimd
        def _(pool):
            pool.memset(s["minus_half"][:], -0.5)
            pool.memset(s["eps"][:], EPS).then_inc(S["eps_ready"], 1)
            pool.memset(across["v"][:, :, :, :, DH:32], 0.0).then_inc(S["v_ones"], 1)
            pool.wait_ge(S["v_ones"], 1)
            pool.memset(across["v"][:, :, :, :, DH:DH + 1], 1.0).then_inc(S["v_ones"], 1)
            pool.wait_ge(S["eps_ready"], 1)
            for b in range(B):
                norm_rstd(pool, s, S, b, b)
            pool.memset(across["q_st"][:], 0.0)
            pool.wait_ge(S["tokens_psum"], B)
            pool.memset(across["k_st"][:], 0.0).then_inc(S["stacks_cleared"], 1)
            pool.wait_ge(S["ident_in"], 64)
            pool.tensor_copy(across["ident_b"][:], keep["ident"][:])
            for b in range(B):
                pool.wait_ge(S["turned"], b + 1)
                pool.tensor_tensor(n1[:, b], n1[:, b], over_tiles(across["rows"][:, R_BOUT]), ALU.add)
            pool.wait_ge(S["band_in"], 16)
            for part in range(3):
                pool.tensor_copy(across["bias_kq"][:, part, :, :], s["band_f"][:]).then_inc(S["band_step"], 1)
                if part < 2:
                    pool.wait_ge(S["band_step"], 2 * part + 1)
                    pool.tensor_tensor(s["band_f"][:], s["band_f"][:], across["bias_kq"][:, part, :, :],
                                       ALU.subtract).then_inc(S["band_step"], 1)
                    pool.wait_ge(S["band_step"], 2 * part + 2)

        @block.vector
        def _(dve):
            dve.memset(h0[:, :, NT - 1, :], 0.0)
            dve.memset(s["txt1"][:], 0.0).then_inc(S["cleared"], 1)
            dve.wait_ge(S["weights_in"], 48)
            dve.tensor_tensor(s["pos_b"][:], s["pos_b"][:], s["tok_add"][:], ALU.add).then_inc(S["pos_ready"], 1)
            dve.wait_ge(S["pos_ready"], 1)
            for b in range(B):
                dve.wait_ge(embed_in[b], 48)
                dve.wait_ge(S["tokens_psum"], b + 1)
                dve.tensor_tensor(h0[:, b, 0:2, :], tiles(ps[b])[:, 0:2, :], s["pos_b"][:], ALU.add).then_inc(S["text_added"], 1)
                dve.wait_ge(S["text_added"], b + 1)
                dve.tensor_tensor(h0[:, b, 1, :], h0[:, b, 1, :], s["txt1"][:, b, :], ALU.add).then_inc(S["h0_ready"], 1)
                dve.wait_ge(S["h0_ready"], b + 1)
                norm_stats(dve, s, S, b, h0[:, b])
                norm_moments(dve, s, S, b, b)
                if b >= 1:
                    norm_apply(dve, s, S, b - 1, b - 1, h0[:, b - 1], n1[:, b - 1])
            norm_apply(dve, s, S, B - 1, B - 1, h0[:, B - 1], n1[:, B - 1])
            for b in range(B):
                for x in range(2):
                    dve.wait_ge(S["hi_ready"], 2 * b + x + 1)
                    dve.tensor_tensor(s["rest"][:, x, :], s["qk32"][:, x, :], s["parts"][:, b % 2, x, 0, :],
                                      ALU.subtract).then_inc(S["rest_ready"], 1)
                dve.wait_ge(S["v_psum"], b + 1)
                for t in range(NT):
                    ins = dve.tensor_tensor(across["v"][:, b, t, :, 0:DH],
                                            tiles(ps[(3 * b + 2) % 4])[:, t, :].rearrange("p (h x) -> p h x", h=HEADS),
                                            across["rows"][:, R_BV].rearrange("p (h x) -> p h x", h=HEADS), ALU.add)
                ins.then_inc(S["v_ready"], 1)
                for x in range(2):
                    dve.wait_ge(S["mid_ready"], 2 * b + x + 1)
                    dve.tensor_tensor(s["parts"][:, b % 2, x, 2, :], s["rest"][:, x, :], s["parts"][:, b % 2, x, 1, :],
                                      ALU.subtract).then_inc(S["lo_ready"], 1)
                if b == 0:
                    dve.wait_ge(S["const_in"], 32)
                    for part in range(3):
                        dve.tensor_copy(s["const_p"][:, part, :], s["const_f"][:]).then_inc(
                            S["const_step"] if part < 2 else S["const_ready"], 1)
                        if part < 2:
                            dve.wait_ge(S["const_step"], 2 * part + 1)
                            dve.tensor_tensor(s["const_f"][:], s["const_f"][:], s["const_p"][:, part, :],
                                              ALU.subtract).then_inc(S["const_step"], 1)
                            dve.wait_ge(S["const_step"], 2 * part + 2)

        @block.tensor
        def _(pe):
            slots = Slots(pe)
            pe.wait_ge(S["weights_in"], 48)
            for b in range(B):
                pe.wait_ge(patches_in[b % 2], 16 * (b // 2) + 16)
                slots.take(b, S["h0_ready"], b + 1)
                for t in range(2):
                    for c in range(PCH):
                        ins = pe.matmul(tiles(ps[b])[:, t, :], s["patches"][:, b % 2, c, t * P:(t + 1) * P],
                                        s["w_tok"][:, c, :], start=c == 0, stop=c == PCH - 1)
                ins.then_inc(S["tokens_psum"], 1)
            pe.wait_ge(S["ident_in"], 64)
            for b in range(B):
                pe.wait_ge(S["normed"], b + 1)
                slots.take(b, S["xT_ready"], b + 1)
                turn(pe, ps[b], n1[:, b], keep["ident"][:]).then_inc(S["turned"], 1)
            for b in range(B):
                pe.wait_ge(S["xT_ready"], b + 1)
                x = s["xT"][:, b, :]
                slots.take(3 * b % 4, S["q32_ready"], b + 1)
                over_tokens(pe, ps[3 * b % 4], s["w_qkv"][:, 0:HID], x).then_inc(S["q_psum"], 1)
                slots.take((3 * b + 1) % 4, S["k32_ready"], b + 1)
                over_tokens(pe, ps[(3 * b + 1) % 4], s["w_qkv"][:, HID:2 * HID], x).then_inc(S["k_psum"], 1)
                slots.take((3 * b + 2) % 4, S["v_ready"], b + 1)
                for t in range(NT):
                    ins = pe.matmul(tiles(ps[(3 * b + 2) % 4])[:, t, :], x[:, t * P:(t + 1) * P],
                                    s["w_qkv"][:, 2 * HID:3 * HID], start=True, stop=True)
                ins.then_inc(S["v_psum"], 1)


def attention_phase(nc, d, keep, across, ps):
    with ExitStack() as ctx:
        s = allocate(nc, ctx, {
            "probs": ([P, 2, GH, T], F32), "vg": ([P, GROUPS, NT, GH, 32], F32),
            "half_top": ([P, 2, GH * NT], F32), "top": ([P, GH * NT], F32), "top_hi": ([GH * NT, P], BF16), "top_lo": ([GH * NT, P], BF16),
            "waste": ([P, T], BF16), "spare": ([P, 2], F32),
        }, "a_")
        S = semaphores(nc, ctx, """
            stacked0 stacked1 s_psum maxed top_ready top_turned top_hi_ready top_lo_ready top_rows_in
            logits_psum exp_done av_done oT_ready sum_psum den_ready inv_ready att_ready
        """, "a_")
        s["oT"], s["den"] = keep["n2T"][:, 0:2, :], keep["n2T"][:, 2:4, :]
        stacked = (S["stacked0"], S["stacked1"])
        N_IN = len(PAIRS) + 2
        NG = GH * NT
        SCORE_HALVES = ((0, 0, (T + 1) // 2), (HALF, (T + 1) // 2, T))
        LAST_G = B * GROUPS - 1
        FIRST_SCORES = 6
        block = ctx.enter_context(nc.Block())

        @block.sync
        def _(sp):
            def load(b, g):
                heads = slice(g * GH, (g + 1) * GH)
                sp.dma_start(across["q_st"][0:QR, g, :, 0:T], d["q_parts"][bass.ds(b, 1), :, heads, :].rearrange(
                    "o r h n -> (o r) h n")).then_inc(stacked[g], 16)
                row = 0
                for _, count in PAIRS:
                    rows = count * DH
                    sp.dma_start(across["k_st"][row:row + rows, g, :, 0:T],
                                 d["k_parts"][bass.ds(b, 1), 0:rows, heads, :].rearrange("o r h n -> (o r) h n")
                                 ).then_inc(stacked[g], 16)
                    row += rows
                sp.dma_start(s["vg"][:, g, :, :, :].rearrange("p t h x -> p t (h x)"),
                             across["v"][:, bass.ds(b, 1), :, g * GH:(g + 1) * GH, :].rearrange(
                                 "p o t h x -> p (o t) (h x)")).then_inc(stacked[g], 16)

            def top_rows(G, g):
                sp.wait_ge(S["top_lo_ready"], G + 1)
                for r, src in enumerate((s["top_hi"], s["top_lo"])):
                    dst = across["q_st"][QR + r:QR + r + 1, g, :, :].rearrange("o h (t c) -> o (h t) c", c=P)
                    sp.dma_start(dst, src[:, :]).then_inc(S["top_rows_in"], 16)

            load(0, 0)
            load(0, 1)
            top_rows(0, 0)
            with sp.Fori(0, B - 1) as i:
                top_rows(2 * i + 1, 1)
                for g in range(GROUPS):
                    if g == 1:
                        top_rows(2 * i + 2, 0)
                    sp.wait_ge(S["av_done"], NT * (2 * i + g + 1))
                    load(i + 1, g)
            top_rows(LAST_G, 1)

        @block.scalar
        def _(act):
            def copy_sums(G, g):
                act.wait_ge(S["sum_psum"], G + 1)
                act.activation(s["den"][:, g, :], ps[3][:, 0:T], ACT.Copy).then_inc(S["den_ready"], 1)

            def group(G, g, first=False, last=False):
                for n in range(NG):
                    kt, j = divmod(n, GH)
                    act.wait_ge(S["logits_psum"], NG * G + n + 1)
                    if kt >= 2:
                        act.wait_ge(S["av_done"], NT * G + kt - 1)
                    m = rows_of(kt)
                    act.activation(s["probs"][0:m, kt % 2, j, :], ps[n % 2][0:m, 0:T], ACT.Exp).then_inc(S["exp_done"], 1)
                    if n == GH - 1 and not first:
                        copy_sums(G - 1, 1 - g)
                act.wait_ge(S["av_done"], NT * G + NT)
                if last:
                    act.wait_ge(S["att_ready"], LAST_G - 1)
                act.activation(s["oT"][:, g, :], ps[3][:, 0:T], ACT.Copy).then_inc(S["oT_ready"], 1)

            group(0, 0, first=True)
            with act.Fori(0, B - 1) as i:
                group(2 * i + 1, 1)
                group(2 * i + 2, 0)
            group(LAST_G, 1, last=True)
            copy_sums(LAST_G, 1)

        @block.vector
        def _(dve):
            def maxima(G, g):
                for n in range(NG):
                    t, j = divmod(n, GH)
                    off = (NT - 1 - t) * P
                    for half, (bank, x, y) in enumerate(SCORE_HALVES):
                        dve.wait_ge(S["s_psum"], 2 * NG * G + 2 * n + half + 1)
                        apart(dve, s["spare"][:, half:half + 1])
                        dve.tensor_tensor_reduce(
                            s["waste"][:, x:y], ps[2][:, bank:bank + y - x],
                            across["bias_qk"][:, g * GH + j, off + x:off + y], 1.0, LOWEST, ALU.add, ALU.max,
                            s["half_top"][:, half, j * NT + t:j * NT + t + 1]).then_inc(S["maxed"], 1)

            def top_rows(G, first=False):
                dve.wait_ge(S["maxed"], 2 * NG * G + 2 * NG)
                dve.tensor_tensor(s["top"][:], s["half_top"][:, 0, :], s["half_top"][:, 1, :], ALU.max).then_inc(S["top_ready"], 1)
                dve.wait_ge(S["top_turned"], G + 1)
                if not first:
                    dve.wait_ge(S["top_rows_in"], 32 * G)
                src = ps[2][0:NG, 0:P]
                dve.tensor_scalar(s["top_hi"][:], src, -1.0, None, ALU.mult).then_inc(S["top_hi_ready"], 1)
                dve.wait_ge(S["top_hi_ready"], G + 1)
                dve.scalar_tensor_tensor(s["top_lo"][:], src, -1.0, s["top_hi"][:], ALU.mult,
                                         ALU.subtract).then_inc(S["top_lo_ready"], 1)

            def normalise(G, g, b):
                den = s["den"][:, g, :]
                dve.wait_ge(S["den_ready"], G + 1)
                dve.reciprocal(den, den).then_inc(S["inv_ready"], 1)
                dve.wait_ge(S["inv_ready"], G + 1)
                dve.tensor_tensor(across["att"][:, bass.ds(b, 1), g, 0:T], s["oT"][:, g, :].unsqueeze(1),
                                  den.unsqueeze(1), ALU.mult).then_inc(S["att_ready"], 1)

            dve.memset(across["att"][:, :, :, T:TPAD], 0.0)
            maxima(0, 0)
            top_rows(0, first=True)
            maxima(1, 1)
            top_rows(1)
            with dve.Fori(0, B - 1) as i:
                maxima(2 * i + 2, 0)
                top_rows(2 * i + 2)
                normalise(2 * i, 0, i)
                maxima(2 * i + 3, 1)
                top_rows(2 * i + 3)
                normalise(2 * i + 1, 1, i)
            normalise(LAST_G - 1, 0, B - 1)
            normalise(LAST_G, 1, B - 1)

        @block.tensor
        def _(pe):
            def scores(G, g, n):
                t, j = divmod(n // 2, GH)
                bank, x, y = SCORE_HALVES[n % 2]
                if n >= 2:
                    pe.wait_ge(S["maxed"], 2 * NG * G + n - 1)
                pe.matmul(ps[2][:, bank:bank + y - x], across["q_st"][0:QR, g, j, t * P:(t + 1) * P],
                          across["k_st"][0:QR, g, j, x:y], start=True, stop=True).then_inc(S["s_psum"], 1)

            def turn_top(G):
                pe.wait_ge(S["top_ready"], G + 1)
                pe.transpose(ps[2][0:NG, 0:P], s["top"][:], keep["ident"][:]).then_inc(S["top_turned"], 1)

            def logits(G, g, n, between):
                kt, j = divmod(n, GH)
                h, m, k0 = g * GH + j, rows_of(kt), kt * P
                if n >= 2:
                    pe.wait_ge(S["exp_done"], NG * G + n - 1)
                out = ps[n % 2][0:m, :]
                lo, hi = max(0, k0 - P), min(T, k0 + 2 * P)
                for x, y in HALVES:
                    ins = pe.matmul(out[:, x:y], across["k_st"][0:KR, g, j, k0:k0 + m], across["q_st"][0:KR, g, j, x:y],
                                    start=True, stop=True)
                between()
                for x, y in HALVES:
                    x, y = max(x, lo), min(y, hi)
                    if x < y:
                        for part in range(3):
                            ins = pe.matmul(out[:, x:y], across["ident_b"][:, 0:m],
                                            across["bias_kq"][:, part, h, x - k0 + P:y - k0 + P],
                                            start=False, stop=True, skip_group_check=True)
                ins.then_inc(S["logits_psum"], 1)

            def values(G, g, kt):
                m = rows_of(kt)
                pe.wait_ge(S["exp_done"], NG * G + GH * (kt + 1))
                for x, y in HALVES:
                    for j in range(GH):
                        ins = pe.matmul(ps[3][32 * j:32 * j + 32, x:y], s["vg"][0:m, g, kt, j, :],
                                        s["probs"][0:m, kt % 2, j, x:y], start=kt == 0, stop=kt == NT - 1,
                                        tile_position=(0, 32 * j))
                ins.then_inc(S["av_done"], 1)

            def sums(G, g):
                pe.wait_ge(S["oT_ready"], G + 1)
                over_tokens(pe, ps[3], across["head_sum"][:], s["oT"][:, g, :]).then_inc(S["sum_psum"], 1)

            def start_scores(G, g, b, first=False):
                pe.wait_ge(stacked[g], 16 * N_IN * (b + 1))
                if not first:
                    pe.wait_ge(S["top_lo_ready"], G)

            def group(G, g, next_b=None, first=False):
                pe.wait_ge(S["top_rows_in"], 32 * G + 32)
                todo = iter(range(2 * NG) if next_b is not None else ())
                for n in range(NG):
                    def between(count=1, n=n):
                        if n >= FIRST_SCORES:
                            for _, half in zip(range(count), todo):
                                scores(G + 1, 1 - g, half)

                    if n == FIRST_SCORES and next_b is not None:
                        start_scores(G + 1, 1 - g, next_b)
                    logits(G, g, n, between)
                    between()
                    if n == 1 and not first:
                        sums(G - 1, 1 - g)
                    if n >= GH and n % GH == 2:
                        if n == GH + 2 and not first:
                            pe.wait_ge(S["den_ready"], G)
                        values(G, g, n // GH - 1)
                    between()
                    if n == NG - 2 and next_b is not None:
                        for half in todo:
                            scores(G + 1, 1 - g, half)
                        turn_top(G + 1)
                values(G, g, NT - 1)

            start_scores(0, 0, 0, first=True)
            for half in range(2 * NG):
                scores(0, 0, half)
            turn_top(0)
            group(0, 0, next_b=0, first=True)
            with pe.Fori(0, B - 1) as i:
                group(2 * i + 1, 1, next_b=i + 1)
                group(2 * i + 2, 0, next_b=i + 1)
            group(LAST_G, 1)
            sums(LAST_G, 1)


def closing_phase(nc, d, keep, across, ps):
    with ExitStack() as ctx:
        s = allocate(nc, ctx, {
            "w_out": ([P, GROUPS, HID], F32), "w_mlp1": ([P, INNER], F32), "w_mlp2": ([P, NCH, HID], F32),
            "router_w": ([P, E], F32),
            "iota_e": ([P, E], F32),
            "lg": ([P, B, NT, E], F32), "v8": ([P, B, NT, 8], F32), "i8": ([P, B, NT, 8], U32),
            "if8": ([P, B, NT, 8], F32), "gap": ([P, B, NT], F32), "egap": ([P, B, NT], F32),
            "den": ([P, B, NT], F32), "w2": ([P, B, NT, 2], F32), "wk": ([P, B, NT, 16], F32),
            "wr": ([P, B, NT, 16], F32), "wb": ([P, B, NT, 16], BF16), "rt": ([P, B, NT, 64], F32), **NORM_TILES,
        }, "c_")
        S = semaphores(nc, ctx, NORM_SEMS + """
            weights_in eps_ready iota_ready lg_cleared o_psum r_ready turned xT_ready m1_psum gel_ready m2_psum
            y_scaled y_ready h1_ready n2_turned n2T_ready route_psum route_step gap_ready egap_ready route_ready
            rt_turned rt_ready
        """, "c_")
        h0 = keep["h1"][:, :, :].rearrange("p b (t c) -> p b t c", t=NT)
        n1b = across["n1b"]
        gel = across["bias_qk"][:].rearrange("p h n -> p (h n)")[:, 0:2 * NCH * TPAD].rearrange(
            "p (u c n) -> p u c n", u=2, c=NCH)
        q_mem, k_mem = (across[name][:].rearrange("p g h n -> p (g h n)").bitcast(F32) for name in ("q_st", "k_st"))
        s["r"] = q_mem.rearrange("p (b t c) -> p b t c", b=B, t=NT)
        s["x1T"] = k_mem.rearrange("p (b n) -> p b n", b=B)
        WORK = [("o", b) for b in range(B)] + [("x", 0), ("x", 1), ("m2", 0), ("x", 2), ("m2", 1), ("x", 3), ("m2", 2),
                                               ("n2", 0), ("m2", 3), ("n2", 1), ("n2", 2), ("n2", 3)]
        RT_SLOT = (3, 0, 1, 2)
        NORMS = [(1, b) for b in range(B)]
        for b in range(B + 1):
            NORMS += [(2, b)] * (b < B) + [(3, b - 1)] * (b > 0)

        def slot(what, b):
            return ps[WORK.index((what, b)) % 2]

        def nth(norm, b):
            return NORMS.index((norm, b))

        block = ctx.enter_context(nc.Block())

        @block.sync
        def _(sp):
            for dst, src in ((s["w_out"][:], d["w_out"]), (s["w_mlp1"][:], d["w_mlp1"]),
                             (s["w_mlp2"][:], d["w_mlp2"].rearrange("(c p) n -> p c n", p=P)), (s["router_w"][:], d["router_w"])):
                sp.dma_start(dst, src).then_inc(S["weights_in"], 16)

        @block.scalar
        def _(act):
            for b in range(B):
                act.wait_ge(S["turned"], b + 1)
                act.activation(s["x1T"][:, b, :], slot("x", b)[:, 0:TPAD], ACT.Identity,
                               bias=across["cols"][:, C_LN1B:C_LN1B + 1],
                               scale=across["cols"][:, C_LN1G:C_LN1G + 1]).then_inc(S["xT_ready"], 1)
                if b >= 2:
                    act.wait_ge(S["m2_psum"], b - 1)
                for c in range(NCH):
                    act.wait_ge(S["m1_psum"], NCH * b + c + 1)
                    act.activation(gel[:, b % 2, c, :], ps[2 + c % 2][:, 0:TPAD], ACT.Gelu,
                                   bias=across["cols"][:, C_BMLP1 + c:C_BMLP1 + c + 1]).then_inc(S["gel_ready"], 1)
            for b in range(B):
                act.wait_ge(S["n2_turned"], b + 1)
                act.activation(keep["n2T"][:, b, :], slot("n2", b)[:, 0:T], ACT.Copy).then_inc(S["n2T_ready"], 1)
            act.wait_ge(S["gap_ready"], 1)
            act.activation(s["egap"][:], s["gap"][:], ACT.Exp).then_inc(S["egap_ready"], 1)
            for b in range(B):
                act.wait_ge(S["rt_turned"], b + 1)
                act.activation(keep["rt"][:, b, :], ps[RT_SLOT[b]][0:64, 0:T], ACT.Copy).then_inc(S["rt_ready"], 1)

        @block.gpsimd
        def _(pool):
            pool.memset(s["minus_half"][:], -0.5)
            pool.memset(s["eps"][:], EPS).then_inc(S["eps_ready"], 1)
            pool.iota(s["iota_e"][:], pattern=[[1, E]], base=0, channel_multiplier=0,
                      allow_small_or_imprecise_dtypes=True).then_inc(S["iota_ready"], 1)
            pool.memset(s["lg"][:], 0.0).then_inc(S["lg_cleared"], 1)
            pool.wait_ge(S["eps_ready"], 1)
            for b in range(B):
                norm_rstd(pool, s, S, b, nth(1, b))
            for b in range(B + 1):
                if b < B:
                    norm_rstd(pool, s, S, b, nth(2, b))
                if b >= 1:
                    norm_rstd(pool, s, S, b - 1, nth(3, b - 1))
                if b < B:
                    pool.wait_ge(S["normed"], nth(2, b) + 1)
                    pool.tensor_tensor(n1b[:, b], n1b[:, b], over_tiles(across["rows"][:, R_LN2G]),
                                       ALU.mult).then_inc(S["y_scaled"], 1)
                    pool.wait_ge(S["y_scaled"], b + 1)
                    pool.tensor_tensor(n1b[:, b], n1b[:, b], over_tiles(across["rows"][:, R_LN2B]),
                                       ALU.add).then_inc(S["y_ready"], 1)

        @block.vector
        def _(dve):
            for b in range(B):
                dve.wait_ge(S["o_psum"], b + 1)
                dve.tensor_tensor(s["r"][:, b], tiles(slot("o", b)), n1b[:, b], ALU.add).then_inc(S["r_ready"], 1)
                dve.wait_ge(S["r_ready"], b + 1)
                norm_stats(dve, s, S, b, s["r"][:, b])
                norm_moments(dve, s, S, b, nth(1, b))
                if b >= 1:
                    norm_apply(dve, s, S, b - 1, nth(1, b - 1), s["r"][:, b - 1], n1b[:, b - 1])
            norm_apply(dve, s, S, B - 1, nth(1, B - 1), s["r"][:, B - 1], n1b[:, B - 1])
            for b in range(B + 1):
                if b < B:
                    dve.wait_ge(S["m2_psum"], b + 1)
                    dve.tensor_tensor(s["r"][:, b], tiles(slot("m2", b)), over_tiles(across["rows"][:, R_BMLP2]),
                                      ALU.add).then_inc(S["r_ready"], 1)
                    dve.wait_ge(S["r_ready"], B + b + 1)
                    norm_stats(dve, s, S, b, s["r"][:, b])
                    norm_moments(dve, s, S, b, nth(2, b))
                if b >= 1:
                    dve.wait_ge(S["y_ready"], b)
                    dve.tensor_tensor(h0[:, b - 1], h0[:, b - 1], n1b[:, b - 1], ALU.add).then_inc(S["h1_ready"], 1)
                    dve.wait_ge(S["h1_ready"], b)
                    norm_stats(dve, s, S, b - 1, h0[:, b - 1])
                    norm_moments(dve, s, S, b - 1, nth(3, b - 1))
                if b < B:
                    norm_apply(dve, s, S, b, nth(2, b), s["r"][:, b], n1b[:, b])
                if b >= 1:
                    norm_apply(dve, s, S, b - 1, nth(3, b - 1), h0[:, b - 1], s["r"][:, b - 1])

            def step(ins, n):
                ins.then_inc(S["route_step"], 1)
                dve.wait_ge(S["route_step"], n)

            dve.wait_ge(S["route_psum"], 1)
            dve.wait_ge(S["lg_cleared"], 1)
            logits = ps[2][:, 0:B * NT * E].rearrange("p (b t e) -> p b t e", b=B, t=NT)
            bias = across["rows"][:, R_RB].unsqueeze(1).unsqueeze(1)
            dve.tensor_tensor(s["lg"][:, :, 0:NT - 1, :], logits[:, :, 0:NT - 1, :],
                              bias.broadcast_to([P, B, NT - 1, E]), ALU.add)
            step(dve.tensor_tensor(s["lg"][0:LAST, :, NT - 1, :], logits[0:LAST, :, NT - 1, :],
                                   bias[0:LAST, 0].broadcast_to([LAST, B, E]), ALU.add), 1)
            for b in range(B):
                for t in range(NT):
                    ins = dve.max(s["v8"][:, b, t, :], s["lg"][:, b, t, :])
            step(ins, 2)
            dve.tensor_tensor(s["gap"][:], s["v8"][:, :, :, 1], s["v8"][:, :, :, 0], ALU.subtract).then_inc(S["gap_ready"], 1)
            for b in range(B):
                for t in range(NT):
                    ins = dve.max_index(s["i8"][:, b, t, :], s["v8"][:, b, t, :], s["lg"][:, b, t, :])
            step(ins, 3)
            step(dve.tensor_copy(s["if8"][:], s["i8"][:]), 4)
            dve.wait_ge(S["iota_ready"], 1)
            by_e = [P, B, NT, E]
            for k in range(2):
                dve.tensor_tensor(s["rt"][:, :, :, E * k:E * k + E], s["iota_e"][:].unsqueeze(1).unsqueeze(1).broadcast_to(by_e),
                                  s["if8"][:, :, :, k:k + 1].broadcast_to(by_e), ALU.is_equal)
            dve.wait_ge(S["egap_ready"], 1)
            step(dve.tensor_scalar(s["den"][:], s["egap"][:], 1.0, None, ALU.add), 5)
            step(dve.reciprocal(s["w2"][:, :, :, 0], s["den"][:]), 6)
            step(dve.tensor_tensor(s["w2"][:, :, :, 1], s["egap"][:], s["w2"][:, :, :, 0], ALU.mult), 7)
            for k in range(2):
                ins = dve.tensor_tensor(s["wk"][:, :, :, E * k:E * k + E], s["rt"][:, :, :, E * k:E * k + E],
                                        s["w2"][:, :, :, k:k + 1].broadcast_to(by_e), ALU.mult)
            step(ins, 8)
            step(dve.tensor_copy(s["wb"][:], s["wk"][:]), 9)
            dve.tensor_copy(s["rt"][:, :, :, 16:32], s["wb"][:])
            step(dve.tensor_tensor(s["wr"][:], s["wk"][:], s["wb"][:], ALU.subtract), 10)
            step(dve.tensor_copy(s["wb"][:], s["wr"][:]), 11)
            dve.tensor_copy(s["rt"][:, :, :, 32:48], s["wb"][:])
            dve.tensor_tensor(s["rt"][:, :, :, 48:64], s["wr"][:], s["wb"][:], ALU.subtract).then_inc(S["route_ready"], 1)

        @block.tensor
        def _(pe):
            slots = Slots(pe)

            def project(b):
                slots.take(b % 2, S["r_ready"], b + 1)
                for t in range(NT):
                    for g in range(GROUPS):
                        ins = pe.matmul(tiles(slot("o", b))[:, t, :], across["att"][:, b, g, t * P:(t + 1) * P],
                                        s["w_out"][:, g, :], start=g == 0, stop=g == GROUPS - 1)
                ins.then_inc(S["o_psum"], 1)

            def take(what, b, sem, value):
                slots.take(WORK.index((what, b)) % 2, sem, value)

            def inner(b):
                pe.wait_ge(S["normed"], nth(1, b) + 1)
                take("x", b, S["xT_ready"], b + 1)
                turn(pe, slot("x", b), n1b[:, b], keep["ident"][:]).then_inc(S["turned"], 1)
                pe.wait_ge(S["xT_ready"], b + 1)
                for c in range(NCH):
                    slots.take(2 + c % 2, S["gel_ready"], NCH * b + c + 1)
                    for x, y in ((0, HALF), (HALF, TPAD)):
                        ins = pe.matmul(ps[2 + c % 2][:, x:y], s["w_mlp1"][:, c * P:(c + 1) * P], s["x1T"][:, b, x:y],
                                        start=True, stop=True)
                    ins.then_inc(S["m1_psum"], 1)

            def outer(b):
                pe.wait_ge(S["gel_ready"], NCH * b + NCH)
                take("m2", b, S["r_ready"], B + b + 1)
                out = tiles(slot("m2", b))
                for t in range(NT):
                    for c in range(NCH):
                        pe.matmul(out[:, t, :], gel[:, b % 2, c, t * P:(t + 1) * P], s["w_mlp2"][:, c, :],
                                  start=c == 0, stop=False)
                    ins = pe.matmul(out[:, t, :], s["x1T"][:, b, t * P:(t + 1) * P], keep["ident"][:], start=False, stop=True)
                ins.then_inc(S["m2_psum"], 1)

            def turn_n2(b):
                pe.wait_ge(S["normed"], nth(3, b) + 1)
                take("n2", b, S["n2T_ready"], b + 1)
                turn(pe, slot("n2", b), s["r"][:, b], keep["ident"][:]).then_inc(S["n2_turned"], 1)

            pe.wait_ge(S["weights_in"], 64)
            for b in range(B):
                project(b)
            inner(0)
            for b in range(1, B):
                inner(b)
                outer(b - 1)
            turn_n2(0)
            outer(B - 1)
            for b in range(1, B):
                turn_n2(b)
            slots.take(2, S["route_step"], 1)
            for b in range(B):
                pe.wait_ge(S["n2T_ready"], b + 1)
                for t in range(NT):
                    n, m = (b * NT + t) * E, rows_of(t)
                    ins = pe.matmul(ps[2][0:m, n:n + E], keep["n2T"][:, b, t * P:t * P + m], s["router_w"][:],
                                    start=True, stop=True)
            ins.then_inc(S["route_psum"], 1)
            pe.wait_ge(S["route_ready"], 1)
            for b in range(B):
                slots.take(RT_SLOT[b], S["rt_ready"], b + 1)
                for t in range(NT):
                    ins = pe.transpose(ps[RT_SLOT[b]][0:64, t * P:(t + 1) * P], s["rt"][:, b, t, :], keep["ident"][:])
                ins.then_inc(S["rt_turned"], 1)


def expert_phase(nc, d, keep, ps):
    with ExitStack() as ctx:
        s = allocate(nc, ctx, {
            "wi": ([P, 2, 4 * HID], F32), "wh": ([P, 2, 4 * HID], F32), "wo": ([P, 2, HID], F32),
            "b": ([P, 2, 4], F32), "b1": ([P, 2, 4], F32),
            "pick_f": ([64, 2, PICKS, P], F32), "pick": ([64, 2, PICKS, P], BF16),
            "z": ([P, 2, 8], F32),
            "x": ([P, 4, T], F32),
            "gate": ([P, 2, 4, T], F32),
            "h_first": ([P, T], F32), "h": ([P, 2, T], F32), "c": ([P, 2, T], F32),
            "tc": ([P, T], F32), "ig": ([P, T], F32), "fc": ([P, T], F32),
            "part": ([P, 2, T], F32), "hs": ([P, 2, T], F32), "yT": ([P, B, T], F32),
            "spare": ([P, 1], F32), "bo_f": ([64, HID], F32), "bo_p": ([64, 3, HID], BF16),
            "yb": ([P, TPAD], F32), "out": ([P, NT, HID], F32),
        }, "e_")
        S = semaphores(nc, ctx, """
            first_weights weights0 weights1 pick_ready bo_zeroed bo_in bo_step bo_ready y_zeroed
            z_gates z_c z_tc z_h gate_psum gate_read aux_psum aux_read masked ig_ready fc_ready c_ready tc_ready
            h_ready hs_ready biased yb_ready turned_y out_ready stored
        """, "e_")
        IG, FG, GG, OG = range(4)
        ZI, ZG, ZO, ZC, ZT, ZH = range(6)
        weights_in = (S["weights0"], S["weights1"])
        N_LOADS = 5

        UNITS = [(0, None), (1, 0), (1, 1), (2, 0), (2, 1), (3, None)]
        NU = len(UNITS)
        ORDER = [[IG, GG, OG] if st == 0 else [IG, GG, FG, OG] for st, _ in UNITS]
        BEFORE = [sum(len(o) for o in ORDER[:n]) for n in range(NU + 1)]
        NG = BEFORE[NU]
        AUX = [("mask", 1, 0), ("mask", 1, 1), ("b1",), ("mask", 2, 0), ("mask", 2, 1), ("seed", 0, 0),
               ("seed", 0, 1), ("scale", 0, W01), ("y", 0), ("scale", 1, W0), ("scale", 1, W1), ("y", 1),
               ("scale", 2, W0), ("scale", 2, W1), ("merge", 3, M1), ("y", 2), ("scale", 3, W01), ("y", 3)]
        NA = len(AUX)
        FREE = 2


        def at(i, u, per, n):
            return 2 * per * i + per * u + n

        block = ctx.enter_context(nc.Block())

        @block.sync
        def _(sp):
            sp.wait_ge(S["bo_zeroed"], 1)
            for part in range(3):
                for k in range(2):
                    row = 16 + 16 * part + E * k
                    sp.dma_start(s["bo_f"][row:row + E, :], d["bo"]).then_inc(S["bo_in"], 16)

            def load(u, e):
                for dst, src in ((s["wi"][:, u, :], d["Wi"][bass.ds(e, 1)].rearrange("o p n -> (o p) n")),
                                 (s["wh"][:, u, :], d["Wh"][bass.ds(e, 1)].rearrange("o p n -> (o p) n")),
                                 (s["wo"][:, u, :], d["Wo"][bass.ds(e, 1)].rearrange("o p n -> (o p) n")),
                                 (s["b"][:, u, :], d["b"][bass.ds(e, 1)].rearrange("o p g -> (o p) g")),
                                 (s["pick_f"][:, u, :, :], d["c_pick"][bass.ds(e, 1)].rearrange("o p a n -> (o p) a n"))):
                    sp.dma_start(dst, src).then_inc(weights_in[u], 16)

            load(0, 0)
            load(1, 1)
            with sp.Fori(1, E // 2) as i:
                for u in range(2):
                    sp.wait_ge(S["aux_read"], FREE + at(i, u, NA, -NA))
                    load(u, 2 * i + u)
            with sp.Fori(0, B) as b:
                sp.wait_ge(S["out_ready"], b + 1)
                dst = d["out"][bass.ds(b, 1)].rearrange("o t c -> (o t) c")
                sp.dma_start(dst[0:(NT - 1) * P, :].rearrange("(t p) c -> p t c", p=P),
                             s["out"][:, 0:NT - 1, :]).then_inc(S["stored"], 16)
                sp.dma_start(dst[(NT - 1) * P:T, :], s["out"][0:LAST, NT - 1, :]).then_inc(S["stored"], 16)
            sp.wait_ge(S["stored"], 32 * B + 32)

        @block.gpsimd
        def _(pool):
            pool.memset(s["bo_f"][:], 0.0).then_inc(S["bo_zeroed"], 1)
            pool.memset(s["yT"][:], 0.0)
            pool.memset(s["yb"][:], 0.0).then_inc(S["y_zeroed"], 1)
            pool.sem_inc(S["h_ready"], FREE)
            pool.sem_inc(S["gate_read"], FREE)
            pool.sem_inc(S["aux_read"], FREE)
            pool.sem_inc(S["stored"], 32)
            with pool.Fori(0, E // 2) as i:
                for u in range(2):
                    for n, (st, k) in enumerate(UNITS):
                        gate = s["gate"][:, n % 2]
                        pool.wait_ge(S["gate_read"], FREE + at(i, u, NG, BEFORE[n] + 2))
                        if n == 0:
                            if u:
                                pool.wait_ge(S["c_ready"], at(i, u, NU, 0))
                            else:
                                pool.wait_ge(S["h_ready"], FREE + at(i, u, NU, 0))
                            pool.tensor_tensor(s["ig"][:], gate[:, IG, :], gate[:, GG, :], ALU.mult).then_inc(S["c_ready"], 1)
                        else:
                            if n == 1:
                                pool.wait_ge(S["aux_read"], FREE + at(i, u, NA, 7))
                            else:
                                pool.wait_ge(S["c_ready"], at(i, u, NU, n))
                            pool.tensor_tensor(s["ig"][:], gate[:, IG, :], gate[:, GG, :], ALU.mult).then_inc(S["ig_ready"], 1)
                        if (st, k) in ((1, 1), (2, 1)):
                            pool.wait_ge(S["aux_read"], FREE + at(i, u, NA, 11 if st == 1 else 14))
                            pool.tensor_tensor(s["hs"][:, st % 2, :], s["part"][:, 0, :], s["part"][:, 1, :],
                                               ALU.add).then_inc(S["hs_ready"], 1)

        @block.vector
        def _(dve):
            dve.wait_ge(S["bo_in"], 16 * 6)
            for part in range(3):
                dve.tensor_copy(s["bo_p"][:, part, :], s["bo_f"][:]).then_inc(S["bo_step"] if part < 2 else S["bo_ready"], 1)
                if part < 2:
                    dve.wait_ge(S["bo_step"], 2 * part + 1)
                    dve.tensor_tensor(s["bo_f"][:], s["bo_f"][:], s["bo_p"][:, part, :], ALU.subtract).then_inc(S["bo_step"], 1)
                    dve.wait_ge(S["bo_step"], 2 * part + 2)
            dve.wait_ge(S["y_zeroed"], 1)
            with dve.Fori(0, E // 2) as i:
                for u in range(2):
                    z = s["z"][:, u, :]

                    def aux(n):
                        dve.wait_ge(S["aux_psum"], at(i, u, NA, n + 1))
                        return ps[2 + n % 2][:, 0:T]

                    def mask(n):
                        _, st, k = AUX[n]
                        dve.tensor_tensor(s["x"][:, 2 * (st - 1) + k, :], keep["n2T"][:, st, :], aux(n),
                                          ALU.mult).then_inc(S["aux_read"], 1)

                    def seed(n):
                        k = AUX[n][2]
                        m = aux(n)
                        dve.scalar_tensor_tensor(s["h"][:, k, :], s["h_first"][:], z[:, ZH:ZH + 1], m,
                                                 ALU.subtract, ALU.mult)
                        dve.scalar_tensor_tensor(s["c"][:, k, :], s["ig"][:], z[:, ZC:ZC + 1], m,
                                                 ALU.subtract, ALU.mult).then_inc(S["aux_read"], 1)

                    def output(n):
                        y = s["yT"][:, AUX[n][1], :]
                        dve.tensor_tensor(y, y, aux(n), ALU.add).then_inc(S["aux_read"], 1)

                    def scale(n, src, dst):
                        dve.tensor_tensor(dst, src, aux(n), ALU.mult).then_inc(S["aux_read"], 1)

                    def cell(n):
                        st, k = UNITS[n]
                        k = k or 0
                        gate = s["gate"][:, n % 2]
                        done = at(i, u, NU, n + 1)
                        if st:
                            dve.wait_ge(S["gate_read"], FREE + at(i, u, NG, BEFORE[n] + 3))
                            if st == 1:
                                dve.scalar_tensor_tensor(s["fc"][:], s["c"][:, k, :], z[:, ZC:ZC + 1], gate[:, FG, :],
                                                         ALU.add, ALU.mult).then_inc(S["fc_ready"], 1)
                            else:
                                dve.tensor_tensor(s["fc"][:], s["c"][:, k, :], gate[:, FG, :], ALU.mult).then_inc(S["fc_ready"], 1)
                            dve.wait_ge(S["fc_ready"], at(i, u, NU - 1, n))
                            dve.wait_ge(S["ig_ready"], at(i, u, NU - 1, n))
                            dve.tensor_tensor(s["c"][:, k, :], s["fc"][:], s["ig"][:], ALU.add).then_inc(S["c_ready"], 1)
                        dve.wait_ge(S["tc_ready"], done)
                        dst = s["h"][:, k, :] if st else s["h_first"][:]
                        dve.tensor_tensor(dst, gate[:, OG, :], s["tc"][:], ALU.mult).then_inc(S["h_ready"], 1)

                    def h_is_there(n):
                        dve.wait_ge(S["h_ready"], FREE + at(i, u, NU, n + 1))

                    dve.wait_ge(S["pick_ready"], at(i, u, 1, 1))
                    mask(0)
                    mask(1)
                    dve.wait_ge(S["z_gates"], at(i, u, 1, 1))
                    dve.tensor_tensor(z[:, ZC:ZC + 1], z[:, ZI:ZI + 1], z[:, ZG:ZG + 1], ALU.mult).then_inc(S["z_c"], 1)
                    dve.wait_ge(S["z_tc"], at(i, u, 1, 1))
                    dve.tensor_tensor(z[:, ZH:ZH + 1], z[:, ZO:ZO + 1], z[:, ZT:ZT + 1], ALU.mult).then_inc(S["z_h"], 1)
                    dve.tensor_tensor(s["b1"][:, u, :], aux(2)[:, 0:4], s["b"][:, u, :], ALU.add).then_inc(S["aux_read"], 1)
                    mask(3)
                    mask(4)
                    cell(0)
                    h_is_there(0)
                    dve.wait_ge(S["z_h"], at(i, u, 1, 1))
                    seed(5)
                    seed(6)
                    scale(7, s["h_first"][:], s["hs"][:, 0, :])
                    cell(1)
                    output(8)
                    h_is_there(1)
                    scale(9, s["h"][:, 0, :], s["part"][:, 0, :])
                    cell(2)
                    h_is_there(2)
                    scale(10, s["h"][:, 1, :], s["part"][:, 1, :])
                    cell(3)
                    output(11)
                    h_is_there(3)
                    scale(12, s["h"][:, 0, :], s["part"][:, 0, :])
                    cell(4)
                    h_is_there(4)
                    scale(13, s["h"][:, 1, :], s["part"][:, 1, :])
                    m = aux(14).bitcast(I32)
                    apart(dve, s["spare"])
                    dve.copy_predicated(s["h"][:, 0, :], m, s["h"][:, 1, :])
                    dve.copy_predicated(s["c"][:, 0, :], m, s["c"][:, 1, :]).then_inc(S["aux_read"], 1)
                    dve.wait_ge(S["aux_read"], FREE + at(i, u, NA, 15))
                    cell(5)
                    output(15)
                    h_is_there(5)
                    scale(16, s["h"][:, 0, :], s["hs"][:, 1, :])
                    output(17)
            with dve.Fori(0, B) as b:
                dve.wait_ge(S["biased"], b + 1)
                dve.tensor_tensor(s["yb"][:, 0:T].unsqueeze(1), ps[0][:, 0:T].unsqueeze(1), s["yT"][:, bass.ds(b, 1), :],
                                  ALU.add).then_inc(S["yb_ready"], 1)
                dve.wait_ge(S["turned_y"], b + 1)
                dve.wait_ge(S["stored"], 32 * b + 32)
                dve.tensor_tensor(s["out"][:].rearrange("p t c -> p (t c)").unsqueeze(1), ps[1][:, 0:TPAD].unsqueeze(1),
                                  keep["h1"][:, bass.ds(b, 1), :], ALU.add).then_inc(S["out_ready"], 1)

        @block.scalar
        def _(act):
            with act.Fori(0, E // 2) as i:
                for u in range(2):
                    z = s["z"][:, u, :]
                    b, b1 = s["b"][:, u, :], s["b1"][:, u, :]
                    act.wait_ge(weights_in[u], 16 * N_LOADS * i + 16 * N_LOADS)
                    act.activation(s["pick"][:, u, :, :], s["pick_f"][:, u, :, :], ACT.Copy).then_inc(S["pick_ready"], 1)
                    act.activation(z[:, ZI:ZI + 1], b[:, IG:IG + 1], ACT.Sigmoid)
                    act.activation(z[:, ZG:ZG + 1], b[:, GG:GG + 1], ACT.Tanh)
                    act.activation(z[:, ZO:ZO + 1], b[:, OG:OG + 1], ACT.Sigmoid).then_inc(S["z_gates"], 1)
                    act.wait_ge(S["z_c"], at(i, u, 1, 1))
                    act.activation(z[:, ZT:ZT + 1], z[:, ZC:ZC + 1], ACT.Tanh).then_inc(S["z_tc"], 1)
                    for n, (st, k) in enumerate(UNITS):
                        unit = at(i, u, NU, n)
                        act.wait_ge(S["h_ready"], unit + 1)
                        for m, g in enumerate(ORDER[n]):
                            place = BEFORE[n] + m
                            slot = (NG * u + place) % 2
                            act.wait_ge(S["gate_psum"], at(i, u, NG, place + 1))
                            if st == 1 and m == 0:
                                act.wait_ge(S["aux_read"], FREE + at(i, u, NA, 3))
                            act.activation(s["gate"][:, n % 2, g, :], ps[slot][:, 0:T],
                                           ACT.Tanh if g == GG else ACT.Sigmoid,
                                           bias=(b1 if st == 1 else b)[:, g:g + 1]).then_inc(S["gate_read"], 1)
                        act.wait_ge(S["c_ready"], unit + 1)
                        act.wait_ge(S["h_ready"], unit + FREE)
                        act.activation(s["tc"][:], s["c"][:, k or 0, :] if st else s["ig"][:], ACT.Tanh).then_inc(S["tc_ready"], 1)

        @block.tensor
        def _(pe):
            pe.wait_ge(S["bo_ready"], 1)
            with pe.Fori(0, E // 2) as i:
                for u in range(2):
                    def both(slot, lhsT, rhs, start=True, stop=True):
                        for a, b in HALVES:
                            ins = pe.matmul(ps[slot][:, a:b], lhsT, rhs[:, a:b], start=start, stop=stop)
                        return ins

                    def aux(n):
                        what = AUX[n]
                        pe.wait_ge(S["aux_read"], at(i, u, NA, n + 1))
                        slot = 2 + n % 2
                        if what[0] == "y":
                            pe.wait_ge(S["aux_read"] if what[1] in (0, 3) else S["hs_ready"],
                                       FREE + at(i, u, NA, n) if what[1] in (0, 3) else at(i, u, 2, what[1]))
                            ins = both(slot, s["wo"][:, u, :], s["hs"][:, what[1] % 2, :])
                        elif what[0] == "b1":
                            pe.wait_ge(S["z_h"], at(i, u, 1, 1))
                            for g in range(4):
                                ins = pe.matmul(ps[slot][:, g:g + 1], s["wh"][:, u, g * HID:(g + 1) * HID],
                                                s["z"][:, u, ZH:ZH + 1], start=True, stop=True)
                        else:
                            st = what[1]
                            row = what[2] if what[0] in ("scale", "merge") else (M0, M1)[what[2]]
                            ins = both(slot, s["pick"][:, u, row, :], keep["rt"][:, st, :])
                        ins.then_inc(S["aux_psum"], 1)

                    def gates(n, then={}):
                        st, k = UNITS[n]
                        x = keep["n2T"][:, st, :] if k is None else s["x"][:, 2 * (st - 1) + k, :]
                        if k is not None:
                            pe.wait_ge(S["aux_read"], FREE + at(i, u, NA, {(1, 0): 1, (1, 1): 2, (2, 0): 4, (2, 1): 5}[st, k]))
                        for m, g in enumerate(ORDER[n]):
                            place = BEFORE[n] + m
                            slot = (NG * u + place) % 2
                            cols = slice(g * HID, (g + 1) * HID)
                            pe.wait_ge(S["gate_read"], at(i, u, NG, place + 1))
                            ins = both(slot, s["wi"][:, u, cols], x, stop=st == 0)
                            if st:
                                if m == 0 and st == 1:
                                    pe.wait_ge(S["aux_read"], FREE + at(i, u, NA, 6 + k))
                                if m == 0 and st == 2:
                                    pe.wait_ge(S["h_ready"], FREE + at(i, u, NU, n - 1))
                                if m == 0 and st == 3:
                                    pe.wait_ge(S["aux_read"], FREE + at(i, u, NA, 15))
                                ins = both(slot, s["wh"][:, u, cols], s["h"][:, k or 0, :], start=False)
                            ins.then_inc(S["gate_psum"], 1)
                            for a in then.get(m, ()):
                                aux(a)

                    pe.wait_ge(weights_in[u], 16 * N_LOADS * i + 16 * N_LOADS)
                    pe.wait_ge(S["pick_ready"], at(i, u, 1, 1))
                    aux(0)
                    aux(1)
                    gates(0, {0: [2], 2: [3, 4, 5, 6]})
                    gates(1, {0: [7], 3: [8]})
                    gates(2, {0: [9], 3: [10]})
                    gates(3, {2: [11], 3: [12]})
                    gates(4, {3: [13, 14]})
                    gates(5, {2: [15, 16], 3: [17]})
            with pe.Fori(0, B) as b:
                pe.wait_ge(S["aux_read"], FREE + NA * E)
                for a, z in HALVES:
                    for part in range(3):
                        ins = pe.matmul(ps[0][:, a:z].unsqueeze(1), s["bo_p"][:, part, :], keep["rt"][:, bass.ds(b, 1), a:z],
                                        start=part == 0, stop=part == 2)
                ins.then_inc(S["biased"], 1)
                pe.wait_ge(S["yb_ready"], b + 1)
                for t in range(NT):
                    ins = pe.transpose(ps[1][:, t * P:(t + 1) * P], s["yb"][:, t * P:(t + 1) * P], keep["ident"][:])
                ins.then_inc(S["turned_y"], 1)


def build(nc, d):
    with ExitStack() as ctx:
        keep = allocate(nc, ctx, {
            "ident": ([P, P], F32),
            "h1": ([P, B, TPAD], F32),
            "n2T": ([P, B, T], F32),
            "rt": ([64, B, T], BF16),
        }, "k_")
        ps = [ctx.enter_context(nc.psum_tensor(f"ps{n}", [P, 2 * HALF], F32)) for n in range(4)]
        with ExitStack() as block_ctx:
            across = allocate(nc, block_ctx, {
                "q_st": ([P, GROUPS, GH, TPAD], BF16), "k_st": ([P, GROUPS, GH, TPAD], BF16),
                "v": ([P, B, NT, HEADS, 32], F32),
                "n1b": ([P, B, NT, HID], F32), "att": ([P, B, GROUPS, TPAD], F32),
                "bias_qk": ([P, HEADS, GW], F32), "bias_kq": ([P, 3, HEADS, BAND], BF16),
                "cols": ([P, COLS_N], F32), "rows": ([P, ROWS_N], F32), "head_sum": ([P, P], F32),
                "ident_b": ([P, P], BF16),
            }, "x_")
            embedding_phase(nc, d, keep, across, ps)
            attention_phase(nc, d, keep, across, ps)
            closing_phase(nc, d, keep, across, ps)
        expert_phase(nc, d, keep, ps)


def arranged(x, txt, **p):
    import numpy as np

    f = lambda a: np.ascontiguousarray(np.asarray(a))
    x = f(x).reshape(B, 3, NP_SIDE, NP_SIDE, NP_SIDE, NP_SIDE)
    patches = np.zeros((B, PATCH_DIM, 2 * P), np.float32)
    patches[:, :, 1:1 + N_PATCH] = x.transpose(0, 1, 3, 5, 2, 4).reshape(B, PATCH_DIM, N_PATCH)
    table = f(p["L0_attn_rel_table"]).T
    side = TPAD - MAXD
    ext = np.pad(table, ((0, 0), (side, side - 1)), mode="edge")
    const_rows = np.zeros((NT, HEADS, T), np.float32)
    for kt in range(NT):
        left, right = max(0, kt * P - P), min(T, kt * P + 2 * P)
        const_rows[kt, :, 0:left], const_rows[kt, :, right:T] = table[:, 0:1], table[:, -1:]
    row, col, band = np.arange(P)[:, None], np.arange(GW)[None, :], np.arange(BAND)[None, :]
    head_sum = np.zeros((P, P), np.float32)
    for j in range(GH):
        head_sum[32 * j + DH, 32 * j:32 * j + 32] = 1.0
    key_rows = np.zeros((XR, TPAD), np.float32)
    key_rows[0:2] = 1.0
    for r in range(3 * NT):
        key_rows[2 + r, (r % NT) * P:(r % NT + 1) * P] = 1.0
    tok_b, pos = f(p["L0_tok_b"]), np.zeros((2 * P, HID), np.float32)
    pos[0:1 + N_PATCH] = f(p["L0_tok_pos"])
    tok_add = np.zeros((2 * P, HID), np.float32)
    tok_add[0:1], tok_add[1:1 + N_PATCH] = f(p["L0_tok_token"]), tok_b
    by_tile = lambda a: f(a.reshape(2, P, HID).transpose(1, 0, 2))
    w_out = np.zeros((GROUPS, GH, 32, HID), np.float32)
    w_out[:, :, 0:DH] = f(p["L0_attn_w_out"]).reshape(GROUPS, GH, DH, HID)
    b_qkv = f(p["L0_attn_b_qkv"])
    cols = np.concatenate([np.stack([b_qkv[0:HID], b_qkv[HID:2 * HID], f(p["L0_attn_ln1_g"]), f(p["L0_attn_ln1_b"])]),
                           f(p["L0_attn_b_mlp1"]).reshape(NCH, P)]).T
    rows = np.concatenate([b_qkv[2 * HID:], f(p["L0_attn_b_out"]), f(p["L0_attn_b_mlp2"]), f(p["L0_attn_ln2_g"]),
                           f(p["L0_attn_ln2_b"]), f(p["L0_ffn_router_b"])])
    pick = np.zeros((E, 64, PICKS, P), np.float32)
    for e in range(E):
        pick[e, e, M0] = pick[e, E + e, M1] = 1.0
        for part in range(3):
            r = 16 + 16 * part + e
            pick[e, r, W0] = pick[e, r, W01] = pick[e, r + E, W1] = pick[e, r + E, W01] = 1.0
    return {
        "patches": patches, "txt": f(txt), "tok_W": f(f(p["L0_tok_W"]).T), "tok_add": by_tile(tok_add),
        "pos": by_tile(pos), "cols": f(cols), "rows": rows,
        "w_qkv": f(p["L0_attn_w_qkv"]), "w_out": f(w_out.reshape(GROUPS, P, HID).transpose(1, 0, 2)),
        "w_mlp1": f(p["L0_attn_w_mlp1"]), "w_mlp2": f(p["L0_attn_w_mlp2"]), "router_w": f(p["L0_ffn_router_w"]),
        "const_rows": const_rows.reshape(NT * HEADS, T), "rel_strip": f(ext[:, TPAD + row - col + (NT - 1) * P]),
        "rel_band": f(ext[:, TPAD - P + band - row]),
        "Wi": f(p["L0_ffn_Wi"]), "Wh": f(p["L0_ffn_Wh"]), "b": f(f(p["L0_ffn_b"]).reshape(E, 4, HID).transpose(0, 2, 1)), "Wo": f(p["L0_ffn_Wo"]),
        "bo": f(p["L0_ffn_bo"]),
        "c_ident": np.eye(P, dtype=np.float32), "c_head_sum": head_sum, "c_key_rows": key_rows, "c_pick": pick,
    }


def kernel(**inputs):
    import concourse.bacc as bacc
    from concourse.bass_utils import run_bass_kernel_spmd

    nc = bacc.Bacc("TRN2", target_bir_lowering=False, num_devices=1)
    arrays = {f"in_{name}": a for name, a in arranged(**inputs).items()}
    d = {
        name[3:]: nc.dram_tensor(name, a.shape, mybir.dt.from_np(a.dtype), kind="ExternalInput").ap()
        for name, a in arrays.items()}
    d["out"] = nc.dram_tensor("out_0", (B, T, HID), F32, kind="ExternalOutput").ap()
    d["q_parts"] = nc.dram_tensor("q_parts", (B, QR, HEADS, T), BF16, kind="Internal").ap()
    d["k_parts"] = nc.dram_tensor("k_parts", (B, 3 * DH, HEADS, T), BF16, kind="Internal").ap()
    d["const_d"] = nc.dram_tensor("const_scratch", (3, NT, HEADS, T), BF16, kind="Internal").ap()
    build(nc, d)
    return run_bass_kernel_spmd(nc, [arrays], core_ids=[0]).results[0]["out_0"]
```

```python
from contextlib import ExitStack

import numpy as np

import concourse.bass as bass
from concourse import mybir

F32 = mybir.dt.float32
F32R = mybir.dt.float32r
BF16 = mybir.dt.bfloat16
U32 = mybir.dt.uint32
I32 = mybir.dt.int32
ALU = mybir.AluOpType
ACT = mybir.ActivationFunctionType

P = 128
B = 4
HID = 128
HEADS = 8
DH = HID // HEADS
NP_SIDE = 14
N_PATCH = NP_SIDE * NP_SIDE
PATCH_DIM = 3 * NP_SIDE * NP_SIDE
PCH = 6
PROWS = PATCH_DIM // PCH
TXT = 512
T = 1 + N_PATCH + TXT
TE = T + T % 2
NT = -(-T // P)
TPAD = NT * P
LAST = T - (NT - 1) * P
TXT0 = 1 + N_PATCH - P
HALF = 512
INNER = 512
NCH = INNER // P
MAXD = 128
GW = (NT - 1) * P + T
BAND = 3 * P
QR = 96
XR = 2 + 3 * NT
KR = QR + XR
GROUPS = 2
GH = HEADS // GROUPS
E = 8
EPS = 1e-5
LOWEST = -3.0e38
HALVES = [(0, HALF), (HALF, T)]
PAIRS = ((0, 3), (1, 2), (2, 1))

M0, M1, W0, W1, W01 = range(5)
PICKS = 5


R_BV, R_BOUT, R_LN2G, R_LN2B = (slice(n * HID, n * HID + HID) for n in range(4))
R_RB = slice(4 * HID, 4 * HID + E)
ROWS_N = 4 * HID + E
C_BQ, C_BK, C_LN1G, C_LN1B, C_BMLP2, C_BMLP1 = range(6)
COLS_N = C_BMLP1 + NCH


PARTS_OUT = 16 * 9


def rows_of(t):
    return P if t < NT - 1 else LAST


def dram(ap, offset, pattern):
    return bass.AP(tensor=ap.tensor, offset=offset, ap=pattern)


def apart(dve, spare):
    dve.memset(spare[0:1, 0:1], 0.0)


def every_partition(ap, n):
    return dram(ap, 0, [[0, P], [1, n]])


def allocate(nc, ctx, spec, prefix):
    return {name: ctx.enter_context(nc.sbuf_tensor(prefix + name, shape, dt)) for name, (shape, dt) in spec.items()}


def semaphores(nc, ctx, names, prefix):
    return {name: ctx.enter_context(nc.semaphore(prefix + name)) for name in names.split()}


class Slots:

    def __init__(self, pe):
        self.pe, self.read = pe, {}

    def take(self, slot, sem, value):
        if slot in self.read:
            self.pe.wait_ge(*self.read[slot])
        self.read[slot] = (sem, value)


def over_tokens(pe, out, lhsT, rhs, start=True, stop=True):
    for a, b in HALVES:
        ins = pe.matmul(out[:, a:b], lhsT, rhs[:, a:b], start=start, stop=stop)
    return ins


def turn(pe, out, src, ident):
    for t in range(NT):
        ins = pe.transpose(out[:, t * P:(t + 1) * P], src[:, t, :], ident)
    return ins


def tiles(slot):
    return slot[:, 0:TPAD].rearrange("p (t c) -> p t c", t=NT)


def over_tiles(row):
    return row.unsqueeze(1).broadcast_to([P, NT, HID])


def norm_stats(dve, s, S, b, src):
    for t in range(NT):
        ins = dve.bn_stats(s["stats"][:, b, t, :], src[:, t, :])
    ins.then_inc(S["stats_ready"], 1)


def norm_moments(dve, s, S, b, n):
    dve.wait_ge(S["stats_ready"], n + 1)
    for t in range(NT):
        ins = dve.bn_aggr(s["mom"][:, b, t, :], s["stats"][:, b, t, :])
    ins.then_inc(S["moments_ready"], 1)


def norm_rstd(pool, s, S, b, n):
    pool.wait_ge(S["moments_ready"], n + 1)
    pool.tensor_tensor(s["veps"][:, b, :], s["mom"][:, b, :, 1], s["eps"][:], ALU.add).then_inc(S["veps_ready"], 1)
    pool.wait_ge(S["veps_ready"], n + 1)
    pool.tensor_tensor(s["rstd"][:, b, :], s["veps"][:, b, :], s["minus_half"][:], ALU.pow).then_inc(S["rstd_ready"], 1)


def norm_apply(dve, s, S, b, n, src, dst, done=None):
    dve.wait_ge(S["rstd_ready"], n + 1)
    for t in range(NT):
        ins = dve.tensor_scalar(dst[:, t, :], src[:, t, :], s["mom"][:, b, t, 0:1], s["rstd"][:, b, t:t + 1],
                                ALU.subtract, ALU.mult)
    ins.then_inc(done or S["normed"], 1)


NORM_TILES = {
    "stats": ([P, B, NT, 6], F32), "mom": ([P, B, NT, 2], F32), "veps": ([P, B, NT], F32),
    "rstd": ([P, B, NT], F32), "eps": ([P, NT], F32), "minus_half": ([P, NT], F32),
}
NORM_SEMS = "stats_ready moments_ready veps_ready rstd_ready normed "


def load_stacks(sp, d, across, stacked, b, g):
    heads = slice(g * GH, (g + 1) * GH)
    sp.dma_start(across["q_st"][0:QR, g, :, 0:T], d["q_parts"][bass.ds(b, 1), :, heads, :].rearrange(
        "o r h n -> (o r) h n")).then_inc(stacked[g], 16)
    row = 0
    for _, count in PAIRS:
        rows = count * DH
        sp.dma_start(across["k_st"][row:row + rows, g, :, 0:T],
                     d["k_parts"][bass.ds(b, 1), 0:rows, heads, :].rearrange("o r h n -> (o r) h n")
                     ).then_inc(stacked[g], 16)
        row += rows


def band_floats(across):
    return across["att"][:, 0:2].rearrange("p b g (a n) -> p (b g a) n", a=2)


def embedding_phase(nc, d, keep, across, ps, parts_out, stacked):
    with ExitStack() as ctx:
        s = allocate(nc, ctx, {
            "parts": ([P, 2, 2, 3, T], BF16), "w_tok": ([PROWS, PCH, HID], F32), "w_qkv": ([P, 3 * HID], F32),
            "pos_b": ([P, 2, HID], F32), "tok_add": ([P, 2, HID], F32), "txt1": ([P, B, HID], F32),
            "bq4": ([P, 1], F32),
            "key_rows": ([P, TPAD], F32),
            **NORM_TILES,
        }, "m_")
        S = semaphores(nc, ctx, NORM_SEMS + """
            cleared embed_in embed_in1 embed_in2 embed_in3 weights_in ident_in const_in band_in strips_in
            patches_in0 patches_in1 pos_ready patches_used bq4_ready eps_ready
            tokens_psum pos_added h0_ready n1b_ready turned xT_ready
            q_psum k_psum v_psum q32_ready k32_ready hi_ready rest_ready mid_ready lo_ready v_ready
            const_step const_ready const_out fixed_rows_in stacks_cleared v_ones
        """, "m_")
        embed_in = (S["embed_in"], S["embed_in1"], S["embed_in2"], S["embed_in3"])
        patches_in = (S["patches_in0"], S["patches_in1"])
        h0 = keep["h1"][:, :, :].rearrange("p b (t c) -> p b t c", t=NT)
        n1 = across["n1b"]
        s["band_f"] = band_floats(across)
        last_strips = across["bias_qk"][0:HEADS * NT, HEADS - 2:HEADS, :].rearrange("p h n -> p (h n)")
        s["const_f"] = last_strips[:, 0:T]
        s["const_p"] = last_strips[:, T:T + 3 * T // 2 + 1].bitcast(BF16)[:, 0:3 * T].rearrange("p (m n) -> p m n", m=3)
        s["xT"] = across["att"][:, 2:4].rearrange("p b g n -> p (b g) n")
        s["qk32"], s["rest"] = keep["n2T"][:, 0:2, :], keep["n2T"][:, 2:4, :]
        s["patches"] = across["k_st"][0:PROWS].rearrange("p g h n -> p (g h n)").bitcast(F32).rearrange(
            "p (u c n) -> p u c n", u=2, c=PCH)
        block = ctx.enter_context(nc.Block())

        def load_patches(eng, b):
            eng.dma_start(s["patches"][:, b % 2, :, :], d["patches"][b, :, :].rearrange("(c p) n -> p c n", p=PROWS)
                          ).then_inc(patches_in[b % 2], 16)

        @block.sync
        def _(sp):
            load_patches(sp, 0)
            sp.dma_start(s["w_tok"][:], d["tok_W"].rearrange("(c p) n -> p c n", p=PROWS)).then_inc(S["weights_in"], 16)
            sp.dma_start(s["pos_b"][:], d["pos"]).then_inc(S["weights_in"], 16)
            sp.dma_start(s["tok_add"][:], d["tok_add"]).then_inc(S["weights_in"], 16)
            load_patches(sp, 1)
            sp.wait_ge(S["cleared"], 1)
            first = P - TXT0
            for b in range(B):
                sp.dma_start(s["txt1"][TXT0:P, b, :], d["txt"][b, 0:first, :]).then_inc(embed_in[b], 16)
                sp.dma_start(h0[:, b, 2:NT - 1, :], d["txt"][b, first:first + (NT - 3) * P, :].rearrange(
                    "(t p) c -> p t c", p=P)).then_inc(embed_in[b], 16)
                sp.dma_start(h0[0:LAST, b, NT - 1, :], d["txt"][b, TXT - LAST:TXT, :]).then_inc(embed_in[b], 16)
            for b in range(2, B):
                sp.wait_ge(S["tokens_psum"], b - 1)
                load_patches(sp, b)
            for h in range(HEADS - 2):
                sp.dma_start(across["bias_qk"][:, h, :], d["rel_strip"][h, :, :]).then_inc(S["strips_in"], 16)
            sp.wait_ge(S["const_ready"], 1)
            sp.dma_start(d["const_d"].rearrange("m k h n -> (k h) m n"), s["const_p"]).then_inc(S["const_out"], 16)
            sp.wait_ge(S["const_out"], 16)
            for h in range(HEADS - 2, HEADS):
                sp.dma_start(across["bias_qk"][:, h, :], d["rel_strip"][h, :, :]).then_inc(S["strips_in"], 16)
            sp.wait_ge(S["stacks_cleared"], 2)
            for g in range(GROUPS):
                sp.dma_start(across["q_st"][QR + 2:KR, g, :, 0:T], d["const_d"][:, :, g * GH:(g + 1) * GH, :].rearrange(
                    "m k h n -> (m k) h n")).then_inc(S["fixed_rows_in"], 16)
            for b in range(B):
                row = 0
                for part, count in PAIRS:
                    sp.wait_ge((S["hi_ready"], S["mid_ready"], S["lo_ready"])[part], 2 * b + 1)
                    for _ in range(count):
                        sp.dma_start(d["q_parts"][b, row:row + DH].rearrange("x h n -> h x n"),
                                     s["parts"][:, b % 2, 0, part, :]).then_inc(parts_out[b], 16)
                        row += DH
                if b == 1:
                    sp.wait_ge(parts_out[0], PARTS_OUT)
                    for g in range(GROUPS):
                        load_stacks(sp, d, across, stacked, 0, g)
            sp.wait_ge(S["fixed_rows_in"], 16 * GROUPS)
            sp.wait_ge(S["band_in"], 16)
            sp.wait_ge(S["strips_in"], 16 * (HEADS + 2))

        @block.scalar
        def _(act):
            act.dma_start(keep["ident"][:], d["c_ident"]).then_inc(S["ident_in"], 16)
            act.dma_start(across["cols"][:], d["cols"]).then_inc(S["ident_in"], 16)
            act.dma_start(across["rows"][:], every_partition(d["rows"], ROWS_N)).then_inc(S["ident_in"], 16)
            act.dma_start(s["w_qkv"][:], d["w_qkv"]).then_inc(S["ident_in"], 16)
            act.dma_start(across["w_out"][:], d["w_out"]).then_inc(S["strips_in"], 16)
            act.dma_start(s["const_f"][:], d["const_rows"]).then_inc(S["const_in"], 16)
            act.dma_start(s["key_rows"][QR:KR, :], d["c_key_rows"]).then_inc(S["const_in"], 16)
            act.dma_start(s["band_f"][:], d["rel_band"].rearrange("h p n -> p h n")).then_inc(S["band_in"], 16)
            act.dma_start(across["head_sum"][:], d["c_head_sum"]).then_inc(S["strips_in"], 16)
            act.wait_ge(S["ident_in"], 64)
            act.activation(s["bq4"][:], across["cols"][:, C_BQ:C_BQ + 1], ACT.Copy, scale=DH ** -0.5
                           ).then_inc(S["bq4_ready"], 1)
            for b in range(B):
                act.wait_ge(S["turned"], b + 1)
                act.activation(s["xT"][:, b, :], ps[b][:, 0:TPAD], ACT.Copy).then_inc(S["xT_ready"], 1)
            def store_keys(b):
                for part in range(3):
                    act.wait_ge((S["hi_ready"], S["mid_ready"], S["lo_ready"])[part], 2 * b + 2)
                    act.dma_start(d["k_parts"][b, part * DH:(part + 1) * DH].rearrange("x h n -> h x n"),
                                  s["parts"][:, b % 2, 1, part, :]).then_inc(parts_out[b], 16)

            act.wait_ge(S["bq4_ready"], 1)
            for b in range(B):
                if b >= 2:
                    act.wait_ge(parts_out[b - 2], PARTS_OUT)
                act.wait_ge(S["q_psum"], b + 1)
                act.activation(s["qk32"][:, 0, :], ps[(3 * b) % 4][:, 0:T], ACT.Identity, bias=s["bq4"][:],
                               scale=DH ** -0.5).then_inc(S["q32_ready"], 1)
                act.wait_ge(S["k_psum"], b + 1)
                act.activation(s["qk32"][:, 1, :], ps[(3 * b + 1) % 4][:, 0:T], ACT.Identity, bias=across["cols"][:, C_BK:C_BK + 1],
                               scale=1.0).then_inc(S["k32_ready"], 1)
                for x, ready in enumerate((S["q32_ready"], S["k32_ready"])):
                    act.wait_ge(ready, b + 1)
                    act.activation(s["parts"][:, b % 2, x, 0, :], s["qk32"][:, x, :], ACT.Copy).then_inc(S["hi_ready"], 1)
                if b >= 1:
                    store_keys(b - 1)
                for x in range(2):
                    act.wait_ge(S["rest_ready"], 2 * b + x + 1)
                    act.activation(s["parts"][:, b % 2, x, 1, :], s["rest"][:, x, :], ACT.Copy).then_inc(S["mid_ready"], 1)
                if b >= 1:
                    act.wait_ge(S["const_in"], 32)
                    act.wait_ge(S["stacks_cleared"], 2)
                    for j in ((0,), (1,), (2, 3))[b - 1]:
                        act.activation(across["k_st"][QR:KR, 0, j, :], s["key_rows"][QR:KR, :], ACT.Copy)
            store_keys(B - 1)

        @block.gpsimd
        def _(pool):
            pool.memset(s["minus_half"][:], -0.5)
            pool.memset(s["eps"][:], EPS).then_inc(S["eps_ready"], 1)
            pool.memset(across["v"][:, :, :, :, DH:32], 0.0).then_inc(S["v_ones"], 1)
            pool.wait_ge(S["v_ones"], 1)
            pool.memset(across["v"][:, :, :, :, DH:DH + 1], 1.0).then_inc(S["v_ones"], 1)
            pool.wait_ge(S["eps_ready"], 1)
            for b in range(B):
                norm_rstd(pool, s, S, b, b)
            pool.wait_ge(S["tokens_psum"], B)
            pool.memset(across["k_st"][:], 0.0).then_inc(S["stacks_cleared"], 1)
            pool.wait_ge(S["ident_in"], 64)
            pool.tensor_copy(across["ident_b"][:], keep["ident"][:])
            for b in range(B):
                pool.wait_ge(S["turned"], b + 1)
                pool.tensor_tensor(n1[:, b], n1[:, b], over_tiles(across["rows"][:, R_BOUT]), ALU.add
                                   ).then_inc(S["n1b_ready"], 1)
            pool.wait_ge(S["const_in"], 32)
            pool.wait_ge(S["n1b_ready"], B)
            pool.wait_ge(S["stacks_cleared"], 2)
            for j in range(GH):
                pool.tensor_copy(across["k_st"][QR:KR, 1, j, :], s["key_rows"][QR:KR, :])

        @block.vector
        def _(dve):
            dve.memset(h0[:, :, NT - 1, :], 0.0)
            dve.memset(s["txt1"][:], 0.0).then_inc(S["cleared"], 1)
            dve.memset(across["q_st"][:], 0.0).then_inc(S["stacks_cleared"], 1)
            dve.wait_ge(S["weights_in"], 48)
            dve.tensor_tensor(s["pos_b"][:], s["pos_b"][:], s["tok_add"][:], ALU.add).then_inc(S["pos_ready"], 1)
            dve.wait_ge(S["pos_ready"], 1)
            for b in range(B):
                dve.wait_ge(embed_in[b], 48)
                dve.wait_ge(S["tokens_psum"], b + 1)
                dve.tensor_tensor(h0[:, b, 0:2, :], tiles(ps[b])[:, 0:2, :], s["pos_b"][:], ALU.add
                                  ).then_inc(S["pos_added"], 1)
                dve.wait_ge(S["pos_added"], b + 1)
                dve.tensor_tensor(h0[:, b, 1, :], h0[:, b, 1, :], s["txt1"][:, b, :], ALU.add).then_inc(S["h0_ready"], 1)
                dve.wait_ge(S["h0_ready"], b + 1)
                norm_stats(dve, s, S, b, h0[:, b])
                norm_moments(dve, s, S, b, b)
                if b >= 1:
                    norm_apply(dve, s, S, b - 1, b - 1, h0[:, b - 1], n1[:, b - 1])
            norm_apply(dve, s, S, B - 1, B - 1, h0[:, B - 1], n1[:, B - 1])
            dve.wait_ge(S["const_in"], 32)
            for part in range(3):
                dve.tensor_copy(s["const_p"][:, part, :], s["const_f"][:]).then_inc(
                    S["const_step"] if part < 2 else S["const_ready"], 1)
                if part < 2:
                    dve.wait_ge(S["const_step"], 2 * part + 1)
                    dve.tensor_tensor(s["const_f"][:], s["const_f"][:], s["const_p"][:, part, :], ALU.subtract
                                      ).then_inc(S["const_step"], 1)
                    dve.wait_ge(S["const_step"], 2 * part + 2)
            for b in range(B):
                if b >= 1:
                    dve.wait_ge(S["lo_ready"], 2 * b)
                for x in range(2):
                    dve.wait_ge(S["hi_ready"], 2 * b + x + 1)
                    dve.tensor_tensor(s["rest"][:, x, :], s["qk32"][:, x, :], s["parts"][:, b % 2, x, 0, :],
                                      ALU.subtract).then_inc(S["rest_ready"], 1)
                dve.wait_ge(S["v_psum"], b + 1)
                for t in range(NT):
                    ins = dve.tensor_tensor(across["v"][:, b, t, :, 0:DH],
                                            tiles(ps[(3 * b + 2) % 4])[:, t, :].rearrange("p (h x) -> p h x", h=HEADS),
                                            across["rows"][:, R_BV].rearrange("p (h x) -> p h x", h=HEADS), ALU.add)
                ins.then_inc(S["v_ready"], 1)
                for x in range(2):
                    dve.wait_ge(S["mid_ready"], 2 * b + x + 1)
                    dve.tensor_tensor(s["parts"][:, b % 2, x, 2, :], s["rest"][:, x, :], s["parts"][:, b % 2, x, 1, :],
                                      ALU.subtract).then_inc(S["lo_ready"], 1)

        @block.tensor
        def _(pe):
            slots = Slots(pe)
            pe.wait_ge(S["weights_in"], 48)
            for b in range(B):
                pe.wait_ge(patches_in[b % 2], 16 * (b // 2) + 16)
                slots.take(b, S["h0_ready"], b + 1)
                for t in range(2):
                    for c in range(PCH):
                        ins = pe.matmul(tiles(ps[b])[:, t, :], s["patches"][:, b % 2, c, t * P:(t + 1) * P],
                                        s["w_tok"][:, c, :], start=c == 0, stop=c == PCH - 1)
                ins.then_inc(S["tokens_psum"], 1)
            pe.wait_ge(S["ident_in"], 64)
            for b in range(B):
                pe.wait_ge(S["normed"], b + 1)
                slots.take(b, S["xT_ready"], b + 1)
                turn(pe, ps[b], n1[:, b], keep["ident"][:]).then_inc(S["turned"], 1)
            for b in range(B):
                pe.wait_ge(S["xT_ready"], b + 1)
                x = s["xT"][:, b, :]
                slots.take(3 * b % 4, S["q32_ready"], b + 1)
                over_tokens(pe, ps[3 * b % 4], s["w_qkv"][:, 0:HID], x).then_inc(S["q_psum"], 1)
                slots.take((3 * b + 1) % 4, S["k32_ready"], b + 1)
                over_tokens(pe, ps[(3 * b + 1) % 4], s["w_qkv"][:, HID:2 * HID], x).then_inc(S["k_psum"], 1)
                slots.take((3 * b + 2) % 4, S["v_ready"], b + 1)
                for t in range(NT):
                    ins = pe.matmul(tiles(ps[(3 * b + 2) % 4])[:, t, :], x[:, t * P:(t + 1) * P],
                                    s["w_qkv"][:, 2 * HID:3 * HID], start=True, stop=True)
                ins.then_inc(S["v_psum"], 1)


def attention_phase(nc, d, keep, across, ps, parts_out, stacked):
    with ExitStack() as ctx:
        s = allocate(nc, ctx, {
            "probs": ([P, 2, GH, T], F32), "vg": ([P, GROUPS, NT, GH, 32], F32),
            "half_top": ([P, 2, GH * NT], F32), "top": ([P, GH * NT], F32),
            "top_hi": ([GH * NT, P], BF16), "top_lo": ([GH * NT, P], BF16),
            "spare": ([P, 2], F32),
        }, "a_")
        S = semaphores(nc, ctx, """
            band_part band_rest tails_cleared values_in0 values_in1 s_psum maxed top_ready top_turned top_hi_ready top_lo_ready top_rows_in
            logits_psum exp_done av_done oT_ready sum_psum den_ready inv_ready att_ready
        """, "a_")
        band_f = band_floats(across)
        s["oT"], s["den"] = keep["n2T"][:, 0:2, :], keep["n2T"][:, 2:4, :]
        s["waste"] = keep["rt_place"][:, 0, :]
        values_in = (S["values_in0"], S["values_in1"])
        N_IN = len(PAIRS) + 1
        NG = GH * NT
        SCORE_HALVES = ((0, 0, (T + 1) // 2), (HALF, (T + 1) // 2, T))
        LAST_G = B * GROUPS - 1
        FIRST_SCORES = 6
        block = ctx.enter_context(nc.Block())

        @block.sync
        def _(sp):
            def load(b, g):
                load_stacks(sp, d, across, stacked, b, g)
                load_values(b, g)

            def load_values(b, g):
                sp.dma_start(s["vg"][:, g, :, :, :].rearrange("p t h x -> p t (h x)"),
                             across["v"][:, bass.ds(b, 1), :, g * GH:(g + 1) * GH, :].rearrange(
                                 "p o t h x -> p (o t) (h x)")).then_inc(values_in[g], 16)

            def top_rows(G, g):
                sp.wait_ge(S["top_lo_ready"], G + 1)
                for r, src in enumerate((s["top_hi"], s["top_lo"])):
                    dst = across["q_st"][QR + r:QR + r + 1, g, :, :].rearrange("o h (t c) -> o (h t) c", c=P)
                    sp.dma_start(dst, src[:, :]).then_inc(S["top_rows_in"], 16)

            for g in range(GROUPS):
                load_values(0, g)
            top_rows(0, 0)
            for b in range(1, B):
                sp.wait_ge(parts_out[b], PARTS_OUT)
            with sp.Fori(0, B - 1) as i:
                top_rows(2 * i + 1, 1)
                for g in range(GROUPS):
                    if g == 1:
                        top_rows(2 * i + 2, 0)
                    sp.wait_ge(S["av_done"], NT * (2 * i + g + 1))
                    load(i + 1, g)
            top_rows(LAST_G, 1)

        @block.scalar
        def _(act):
            def copy_sums(G, g):
                act.wait_ge(S["sum_psum"], G + 1)
                act.activation(s["den"][:, g, :], ps[3][:, 0:T], ACT.Copy).then_inc(S["den_ready"], 1)

            def group(G, g, first=False, last=False):
                for n in range(NG):
                    kt, j = divmod(n, GH)
                    act.wait_ge(S["logits_psum"], NG * G + n + 1)
                    if kt >= 2:
                        act.wait_ge(S["av_done"], NT * G + kt - 1)
                    m = rows_of(kt)
                    act.activation(s["probs"][0:m, kt % 2, j, :], ps[n % 2][0:m, 0:T], ACT.Exp).then_inc(S["exp_done"], 1)
                    if n == GH - 1 and not first:
                        copy_sums(G - 1, 1 - g)
                act.wait_ge(S["av_done"], NT * G + NT)
                if last:
                    act.wait_ge(S["att_ready"], LAST_G - 1)
                act.activation(s["oT"][:, g, :], ps[3][:, 0:T], ACT.Copy).then_inc(S["oT_ready"], 1)

            for part in range(3):
                if part:
                    act.wait_ge(S["band_rest"], part)
                act.activation(across["bias_kq"][:, part, :, :], band_f, ACT.Copy).then_inc(S["band_part"], 1)
            for b in range(B):
                act.wait_ge(parts_out[b], PARTS_OUT)
            group(0, 0, first=True)
            with act.Fori(0, B - 1) as i:
                group(2 * i + 1, 1)
                group(2 * i + 2, 0)
            group(LAST_G, 1, last=True)
            copy_sums(LAST_G, 1)

        @block.vector
        def _(dve):
            def maxima(G, g):
                for n in range(NG):
                    t, j = divmod(n, GH)
                    off = (NT - 1 - t) * P
                    for half, (bank, x, y) in enumerate(SCORE_HALVES):
                        dve.wait_ge(S["s_psum"], 2 * NG * G + 2 * n + half + 1)
                        apart(dve, s["spare"][:, half:half + 1])
                        dve.tensor_tensor_reduce(
                            s["waste"][:, x:y], ps[2][:, bank:bank + y - x],
                            across["bias_qk"][:, g * GH + j, off + x:off + y], 1.0, LOWEST, ALU.add, ALU.max,
                            s["half_top"][:, half, j * NT + t:j * NT + t + 1]).then_inc(S["maxed"], 1)

            def top_rows(G, first=False):
                dve.wait_ge(S["maxed"], 2 * NG * G + 2 * NG)
                dve.tensor_tensor(s["top"][:], s["half_top"][:, 0, :], s["half_top"][:, 1, :], ALU.max).then_inc(S["top_ready"], 1)
                dve.wait_ge(S["top_turned"], G + 1)
                if not first:
                    dve.wait_ge(S["top_rows_in"], 32 * G)
                src = ps[2][0:NG, 0:P]
                dve.tensor_scalar(s["top_hi"][:], src, -1.0, None, ALU.mult).then_inc(S["top_hi_ready"], 1)
                dve.wait_ge(S["top_hi_ready"], G + 1)
                dve.scalar_tensor_tensor(s["top_lo"][:], src, -1.0, s["top_hi"][:], ALU.mult,
                                         ALU.subtract).then_inc(S["top_lo_ready"], 1)

            def normalise(G, g, b):
                den = s["den"][:, g, :]
                dve.wait_ge(S["den_ready"], G + 1)
                dve.reciprocal(den, den).then_inc(S["inv_ready"], 1)
                dve.wait_ge(S["inv_ready"], G + 1)
                dve.tensor_tensor(across["att"][:, bass.ds(b, 1), g, 0:T], s["oT"][:, g, :].unsqueeze(1),
                                  den.unsqueeze(1), ALU.mult).then_inc(S["att_ready"], 1)

            maxima(0, 0)
            dve.wait_ge(S["tails_cleared"], 1)
            top_rows(0, first=True)
            maxima(1, 1)
            top_rows(1)
            with dve.Fori(0, B - 1) as i:
                maxima(2 * i + 2, 0)
                top_rows(2 * i + 2)
                normalise(2 * i, 0, i)
                maxima(2 * i + 3, 1)
                top_rows(2 * i + 3)
                normalise(2 * i + 1, 1, i)
            normalise(LAST_G - 1, 0, B - 1)
            normalise(LAST_G, 1, B - 1)

        @block.gpsimd
        def _(pool):
            for part in range(2):
                pool.wait_ge(S["band_part"], part + 1)
                pool.tensor_tensor(band_f, band_f, across["bias_kq"][:, part, :, :], ALU.subtract).then_inc(S["band_rest"], 1)
            pool.wait_ge(S["band_part"], 3)
            pool.memset(across["att"][:, :, :, T:TPAD], 0.0).then_inc(S["tails_cleared"], 1)

        @block.tensor
        def _(pe):
            def scores(G, g, n):
                t, j = divmod(n // 2, GH)
                bank, x, y = SCORE_HALVES[n % 2]
                if n >= 2:
                    pe.wait_ge(S["maxed"], 2 * NG * G + n - 1)
                pe.matmul(ps[2][:, bank:bank + y - x], across["q_st"][0:QR, g, j, t * P:(t + 1) * P],
                          across["k_st"][0:QR, g, j, x:y], start=True, stop=True).then_inc(S["s_psum"], 1)

            def turn_top(G):
                pe.wait_ge(S["top_ready"], G + 1)
                pe.transpose(ps[2][0:NG, 0:P], s["top"][:], keep["ident"][:]).then_inc(S["top_turned"], 1)

            def logits(G, g, n, between):
                kt, j = divmod(n, GH)
                h, m, k0 = g * GH + j, rows_of(kt), kt * P
                if n >= 2:
                    pe.wait_ge(S["exp_done"], NG * G + n - 1)
                out = ps[n % 2][0:m, :]
                lo, hi = max(0, k0 - P), min(T, k0 + 2 * P)
                for x, y in HALVES:
                    ins = pe.matmul(out[:, x:y], across["k_st"][0:KR, g, j, k0:k0 + m], across["q_st"][0:KR, g, j, x:y],
                                    start=True, stop=True)
                between()
                for x, y in HALVES:
                    x, y = max(x, lo), min(y, hi)
                    if x < y:
                        for part in range(3):
                            ins = pe.matmul(out[:, x:y], across["ident_b"][:, 0:m],
                                            across["bias_kq"][:, part, h, x - k0 + P:y - k0 + P],
                                            start=False, stop=True, skip_group_check=True)
                ins.then_inc(S["logits_psum"], 1)

            def values(G, g, kt):
                m = rows_of(kt)
                pe.wait_ge(S["exp_done"], NG * G + GH * (kt + 1))
                for x, y in HALVES:
                    for j in range(GH):
                        ins = pe.matmul(ps[3][32 * j:32 * j + 32, x:y], s["vg"][0:m, g, kt, j, :],
                                        s["probs"][0:m, kt % 2, j, x:y], start=kt == 0, stop=kt == NT - 1,
                                        tile_position=(0, 32 * j))
                ins.then_inc(S["av_done"], 1)

            def sums(G, g):
                pe.wait_ge(S["oT_ready"], G + 1)
                over_tokens(pe, ps[3], across["head_sum"][:], s["oT"][:, g, :]).then_inc(S["sum_psum"], 1)

            def start_scores(G, g, b, first=False):
                pe.wait_ge(stacked[g], 16 * N_IN * (b + 1))
                if not first:
                    pe.wait_ge(S["top_lo_ready"], G)

            def group(G, g, b, next_b=None, first=False):
                pe.wait_ge(S["top_rows_in"], 32 * G + 32)
                pe.wait_ge(values_in[g], 16 * b + 16)
                todo = iter(range(2 * NG) if next_b is not None else ())
                for n in range(NG):
                    def between(count=1, n=n):
                        if n >= FIRST_SCORES:
                            for _, half in zip(range(count), todo):
                                scores(G + 1, 1 - g, half)

                    if n == FIRST_SCORES and next_b is not None:
                        start_scores(G + 1, 1 - g, next_b)
                    logits(G, g, n, between)
                    between()
                    if n == 1 and not first:
                        sums(G - 1, 1 - g)
                    if n >= GH and n % GH == 3:
                        if n == GH + 3 and not first:
                            pe.wait_ge(S["den_ready"], G)
                        values(G, g, n // GH - 1)
                    between()
                    if n == NG - 2 and next_b is not None:
                        for half in todo:
                            scores(G + 1, 1 - g, half)
                        turn_top(G + 1)
                values(G, g, NT - 1)

            start_scores(0, 0, 0, first=True)
            for half in range(2 * NG):
                scores(0, 0, half)
            turn_top(0)
            pe.wait_ge(S["band_part"], 3)
            group(0, 0, 0, next_b=0, first=True)
            with pe.Fori(0, B - 1) as i:
                group(2 * i + 1, 1, i, next_b=i + 1)
                group(2 * i + 2, 0, i + 1, next_b=i + 1)
            group(LAST_G, 1, B - 1)
            sums(LAST_G, 1)


def closing_phase(nc, d, keep, across, ps, weights_in):
    with ExitStack() as ctx:
        s = allocate(nc, ctx, {
            "w_mlp1": ([P, INNER], F32), "w_mlp2": ([P, NCH, HID], F32),
            "router_w": ([P, E], F32),
            "x1bT": ([P, B, TPAD], F32), "shift": ([P, 1], F32),
            "iota_e": ([P, E], F32),
            "lg": ([P, B, NT, E], F32), "v8": ([P, B, NT, 8], F32), "i8": ([P, B, NT, 8], U32),
            "if8": ([P, B, NT, 8], F32), "gap": ([P, B, NT], F32), "egap": ([P, B, NT], F32),
            "den": ([P, B, NT], F32), "w2": ([P, B, NT, 2], F32), "wk": ([P, B, NT, 16], F32),
            "wr": ([P, B, NT, 16], F32), "rt": ([P, B, NT, 64], BF16), **NORM_TILES,
        }, "c_")
        S = semaphores(nc, ctx, NORM_SEMS + """
            weights_in eps_ready iota_ready lg_cleared o_psum r_ready turned xT_ready m1_psum gel_ready m2_psum
            shifted shift_ready y_ready h1_ready n2_ready x1b_ready n2_turned n2T_ready route_psum lg_ready tops_ready places_ready route_step gap_ready egap_ready route_ready
            rt_turned rt_ready
        """, "c_")
        h0 = keep["h1"][:, :, :].rearrange("p b (t c) -> p b t c", t=NT)
        n1b = across["n1b"]
        gel = across["bias_qk"][:].rearrange("p h n -> p (h n)")[:, 0:2 * NCH * TPAD].rearrange(
            "p (u c n) -> p u c n", u=2, c=NCH)
        q_mem, k_mem = (across[name][:].rearrange("p g h n -> p (g h n)").bitcast(F32) for name in ("q_st", "k_st"))
        s["r"] = q_mem.rearrange("p (b t c) -> p b t c", b=B, t=NT)
        s["x1T"] = k_mem.rearrange("p (b n) -> p b n", b=B)
        WORK = [("o", b) for b in range(B)] + [("x", 0), ("x", 1), ("m2", 0), ("x", 2), ("m2", 1), ("x", 3), ("m2", 2),
                                               ("m2", 3), ("n2", 0), ("n2", 1), ("n2", 2), ("n2", 3)]
        RT_SLOT = (3, 0, 1, 2)
        NORMS = [(1, b) for b in range(B)]
        for b in range(B):
            NORMS += [(2, b), (3, b)]

        def slot(what, b):
            return ps[WORK.index((what, b)) % 2]

        def nth(norm, b):
            return NORMS.index((norm, b))

        def applied(norm, b):
            return [n for n in NORMS if n[0] < 3].index((norm, b)) + 1

        block = ctx.enter_context(nc.Block())

        @block.sync
        def _(sp):
            for dst, src in ((s["w_mlp1"][:], d["w_mlp1"]),
                             (s["w_mlp2"][:], d["w_mlp2"].rearrange("(c p) n -> p c n", p=P)), (s["router_w"][:], d["router_w"])):
                sp.dma_start(dst, src).then_inc(S["weights_in"], 16)
            places = weight_places(keep)
            for e in range(2):
                load_expert(sp, d, places, weights_in, e, e)

        @block.scalar
        def _(act):
            def copy_n2(b):
                act.wait_ge(S["n2_turned"], b + 1)
                act.activation(keep["n2T"][:, b, :], slot("n2", b)[:, 0:T], ACT.Copy).then_inc(S["n2T_ready"], 1)

            for b in range(B):
                act.wait_ge(S["turned"], b + 1)
                act.activation(s["x1T"][:, b, :], slot("x", b)[:, 0:TPAD], ACT.Identity,
                               bias=across["cols"][:, C_LN1B:C_LN1B + 1],
                               scale=across["cols"][:, C_LN1G:C_LN1G + 1]).then_inc(S["x1b_ready"], 1)
                act.wait_ge(S["shift_ready"], 1)
                act.activation(s["x1bT"][:, b, :], slot("x", b)[:, 0:TPAD], ACT.Identity, bias=s["shift"][:],
                               scale=across["cols"][:, C_LN1G:C_LN1G + 1]).then_inc(S["xT_ready"], 1)
                if b >= 2:
                    act.wait_ge(S["m2_psum"], b - 1)
                for c in range(NCH):
                    act.wait_ge(S["m1_psum"], NCH * b + c + 1)
                    act.activation(gel[:, b % 2, c, :], ps[2 + c % 2][:, 0:TPAD], ACT.Gelu,
                                   bias=across["cols"][:, C_BMLP1 + c:C_BMLP1 + c + 1]).then_inc(S["gel_ready"], 1)
            for b in range(B):
                copy_n2(b)
            act.wait_ge(S["gap_ready"], 1)
            act.activation(s["egap"][:], s["gap"][:], ACT.Exp).then_inc(S["egap_ready"], 1)
            for b in (0, 2):
                act.wait_ge(S["rt_turned"], b + 1)
                act.activation(keep["rt"][:, b, :], ps[RT_SLOT[b]][0:64, 0:T], ACT.Copy).then_inc(S["rt_ready"], 1)

        @block.gpsimd
        def _(pool):
            pool.memset(s["minus_half"][:], -0.5)
            pool.memset(s["eps"][:], EPS).then_inc(S["eps_ready"], 1)
            pool.iota(s["iota_e"][:], pattern=[[1, E]], base=0, channel_multiplier=0,
                      allow_small_or_imprecise_dtypes=True).then_inc(S["iota_ready"], 1)
            pool.memset(s["lg"][:], 0.0).then_inc(S["lg_cleared"], 1)
            pool.tensor_tensor(s["shift"][:], across["cols"][:, C_LN1B:C_LN1B + 1], across["cols"][:, C_BMLP2:C_BMLP2 + 1],
                               ALU.add).then_inc(S["shift_ready"], 1)
            pool.wait_ge(S["eps_ready"], 1)
            for b in range(B):
                pool.tensor_tensor(h0[:, b], h0[:, b], over_tiles(across["rows"][:, R_LN2B]), ALU.add
                                   ).then_inc(S["shifted"], 1)
                norm_rstd(pool, s, S, b, nth(1, b))
            for b in range(B):
                norm_rstd(pool, s, S, b, nth(2, b))
                norm_rstd(pool, s, S, b, nth(3, b))

        @block.vector
        def _(dve):
            def route(b):
                dve.wait_ge(S["route_psum"], b + 1)
                logits = ps[2 + b % 2][:, 0:NT * E].rearrange("p (t e) -> p t e", t=NT)
                bias = across["rows"][:, R_RB]
                dve.tensor_tensor(s["lg"][:, b, 0:NT - 1, :], logits[:, 0:NT - 1, :],
                                  bias.unsqueeze(1).broadcast_to([P, NT - 1, E]), ALU.add)
                dve.tensor_tensor(s["lg"][0:LAST, b, NT - 1, :], logits[0:LAST, NT - 1, :], bias[0:LAST], ALU.add
                                  ).then_inc(S["lg_ready"], 1)
                dve.wait_ge(S["lg_ready"], b + 1)
                for t in range(NT):
                    ins = dve.max(s["v8"][:, b, t, :], s["lg"][:, b, t, :])
                ins.then_inc(S["tops_ready"], 1)
                dve.wait_ge(S["tops_ready"], b + 1)
                for t in range(NT):
                    ins = dve.max_index(s["i8"][:, b, t, :], s["v8"][:, b, t, :], s["lg"][:, b, t, :])
                ins.then_inc(S["places_ready"], 1)

            for b in range(B):
                dve.wait_ge(S["o_psum"], b + 1)
                dve.tensor_tensor(s["r"][:, b], tiles(slot("o", b)), n1b[:, b], ALU.add).then_inc(S["r_ready"], 1)
                dve.wait_ge(S["r_ready"], b + 1)
                norm_stats(dve, s, S, b, s["r"][:, b])
                norm_moments(dve, s, S, b, nth(1, b))
                if b >= 1:
                    norm_apply(dve, s, S, b - 1, nth(1, b - 1), s["r"][:, b - 1], n1b[:, b - 1])
            norm_apply(dve, s, S, B - 1, nth(1, B - 1), s["r"][:, B - 1], n1b[:, B - 1])
            for b in range(B):
                dve.wait_ge(S["m2_psum"], b + 1)
                norm_stats(dve, s, S, b, tiles(slot("m2", b)))
                norm_moments(dve, s, S, b, nth(2, b))
                if b == B - 1:
                    route(0)
                norm_apply(dve, s, S, b, nth(2, b), tiles(slot("m2", b)), n1b[:, b])
                dve.wait_ge(S["normed"], applied(2, b))
                dve.tensor_tensor(n1b[:, b], n1b[:, b], over_tiles(across["rows"][:, R_LN2G]), ALU.mult
                                  ).then_inc(S["y_ready"], 1)
                dve.wait_ge(S["y_ready"], b + 1)
                dve.wait_ge(S["shifted"], b + 1)
                dve.tensor_tensor(h0[:, b], h0[:, b], n1b[:, b], ALU.add).then_inc(S["h1_ready"], 1)
                dve.wait_ge(S["h1_ready"], b + 1)
                norm_stats(dve, s, S, b, h0[:, b])
                norm_moments(dve, s, S, b, nth(3, b))
                if b == B - 1:
                    route(1)
                norm_apply(dve, s, S, b, nth(3, b), h0[:, b], s["r"][:, b], done=S["n2_ready"])
            route(2)
            route(3)

            def step(ins, n):
                ins.then_inc(S["route_step"], 1)
                dve.wait_ge(S["route_step"], n)

            dve.tensor_tensor(s["gap"][:], s["v8"][:, :, :, 1], s["v8"][:, :, :, 0], ALU.subtract).then_inc(S["gap_ready"], 1)
            dve.wait_ge(S["places_ready"], B)
            step(dve.tensor_copy(s["if8"][:], s["i8"][:]), 1)
            dve.wait_ge(S["iota_ready"], 1)
            by_e = [P, B, NT, E]
            for k in range(2):
                dve.tensor_tensor(s["rt"][:, :, :, E * k:E * k + E], s["iota_e"][:].unsqueeze(1).unsqueeze(1).broadcast_to(by_e),
                                  s["if8"][:, :, :, k:k + 1].broadcast_to(by_e), ALU.is_equal)
            dve.wait_ge(S["egap_ready"], 1)
            step(dve.tensor_scalar(s["den"][:], s["egap"][:], 1.0, None, ALU.add), 2)
            step(dve.reciprocal(s["w2"][:, :, :, 0], s["den"][:]), 3)
            step(dve.tensor_tensor(s["w2"][:, :, :, 1], s["egap"][:], s["w2"][:, :, :, 0], ALU.mult), 4)
            for k in range(2):
                ins = dve.tensor_tensor(s["wk"][:, :, :, E * k:E * k + E], s["rt"][:, :, :, E * k:E * k + E],
                                        s["w2"][:, :, :, k:k + 1].broadcast_to(by_e), ALU.mult)
            step(ins, 5)
            step(dve.tensor_copy(s["rt"][:, :, :, 16:32], s["wk"][:]), 6)
            step(dve.tensor_tensor(s["wr"][:], s["wk"][:], s["rt"][:, :, :, 16:32], ALU.subtract), 7)
            step(dve.tensor_copy(s["rt"][:, :, :, 32:48], s["wr"][:]), 8)
            dve.tensor_tensor(s["rt"][:, :, :, 48:64], s["wr"][:], s["rt"][:, :, :, 32:48], ALU.subtract
                              ).then_inc(S["route_ready"], 1)
            for b in (1, 3):
                dve.wait_ge(S["rt_turned"], b + 1)
                dve.tensor_copy(keep["rt"][:, b, :], ps[RT_SLOT[b]][0:64, 0:T]).then_inc(S["rt_ready"], 1)

        @block.tensor
        def _(pe):
            slots = Slots(pe)

            def project(b):
                slots.take(b % 2, S["r_ready"], b + 1)
                for t in range(NT):
                    for g in range(GROUPS):
                        ins = pe.matmul(tiles(slot("o", b))[:, t, :], across["att"][:, b, g, t * P:(t + 1) * P],
                                        across["w_out"][:, g, :], start=g == 0, stop=g == GROUPS - 1)
                ins.then_inc(S["o_psum"], 1)

            def take(what, b, sem, value):
                slots.take(WORK.index((what, b)) % 2, sem, value)

            def inner(b):
                pe.wait_ge(S["normed"], applied(1, b))
                take("x", b, S["xT_ready"], b + 1)
                turn(pe, slot("x", b), n1b[:, b], keep["ident"][:]).then_inc(S["turned"], 1)
                pe.wait_ge(S["x1b_ready"], b + 1)
                for c in range(NCH):
                    slots.take(2 + c % 2, S["gel_ready"], NCH * b + c + 1)
                    for x, y in ((0, HALF), (HALF, TPAD)):
                        ins = pe.matmul(ps[2 + c % 2][:, x:y], s["w_mlp1"][:, c * P:(c + 1) * P], s["x1T"][:, b, x:y],
                                        start=True, stop=True)
                    ins.then_inc(S["m1_psum"], 1)

            def outer(b):
                pe.wait_ge(S["gel_ready"], NCH * b + NCH)
                pe.wait_ge(S["xT_ready"], b + 1)
                take("m2", b, S["normed"], applied(2, b))
                out = tiles(slot("m2", b))
                for t in range(NT):
                    for c in range(NCH):
                        pe.matmul(out[:, t, :], gel[:, b % 2, c, t * P:(t + 1) * P], s["w_mlp2"][:, c, :],
                                  start=c == 0, stop=False)
                    ins = pe.matmul(out[:, t, :], s["x1bT"][:, b, t * P:(t + 1) * P], keep["ident"][:], start=False, stop=True)
                ins.then_inc(S["m2_psum"], 1)

            def turn_n2(b):
                pe.wait_ge(S["n2_ready"], b + 1)
                take("n2", b, S["n2T_ready"], b + 1)
                turn(pe, slot("n2", b), s["r"][:, b], keep["ident"][:]).then_inc(S["n2_turned"], 1)

            def route(b):
                pe.wait_ge(S["n2T_ready"], b + 1)
                slots.take(2 + b % 2, S["lg_ready"], b + 1)
                for t in range(NT):
                    m = rows_of(t)
                    ins = pe.matmul(ps[2 + b % 2][0:m, t * E:t * E + E], keep["n2T"][:, b, t * P:t * P + m],
                                    s["router_w"][:], start=True, stop=True)
                ins.then_inc(S["route_psum"], 1)

            for b in range(B):
                project(b)
            pe.wait_ge(S["weights_in"], 48)
            inner(0)
            for b in range(1, B):
                inner(b)
                outer(b - 1)
            outer(B - 1)
            for b in range(B):
                turn_n2(b)
                route(b)
            pe.wait_ge(S["route_ready"], 1)
            for b in range(B):
                slots.take(RT_SLOT[b], S["rt_ready"], B)
                for t in range(NT):
                    ins = pe.matmul(ps[RT_SLOT[b]][0:64, t * P:(t + 1) * P], s["rt"][:, b, t, :], across["ident_b"][:],
                                    start=True, stop=True)
                ins.then_inc(S["rt_turned"], 1)


class Place:
    UNITS = ("u5", "u1", "u2", "u3", "u4", "u0")
    AUX = {
        "u5": {2: ("y2",), 3: ("w3",)}, "u1": {1: ("y3",), 2: ("x20",), 3: ("x21",)},
        "u2": {1: ("w0", "w10"), 2: ("y0",)}, "u3": {1: ("w11",)},
        "u4": {0: ("y1", "x10"), 1: ("x11",), 2: ("w20",), 3: ("merge",)}, "u0": {1: ("w21",), 2: ("s0", "s1")},
    }
    NEXT = ("x10", "x11", "s0", "s1")
    SPLITS = {"s0": -2, "s1": -1, "h10": 0, "h11": 1, "m": 2}

    def __init__(self, i, c, kind=""):
        self.i, self.c, self.kind, self.par = i, c, kind, c % 2
        order = [name for u in self.UNITS for g in range(4) for name in self.AUX[u].get(g, ())]
        if kind == "prologue":
            self.order = list(self.NEXT)
            self.aux_start = 0
        else:
            self.order = [n for n in order if not (kind == "last" and n in self.NEXT)]
            self.aux_start = len(self.NEXT) - 3 + len(order) * c - (len(self.NEXT) if kind == "tail" else 0)
        self.aux_per = len(order)

    def linear(self, per, n):
        return 2 * per * self.i + n

    def unit(self, u):
        n = {"prologue": 0, "tail": 6 * self.c - 1}.get(self.kind, 6 * self.c + self.UNITS.index(u))
        return self.linear(6, n)

    def unit_parity(self, u):
        return {"prologue": 0, "tail": 1}.get(self.kind, self.UNITS.index(u) % 2)

    def _gate(self, u, m):
        n = {"prologue": 0, "tail": 23 * self.c - 4}.get(self.kind, 23 * self.c - 1 + 4 * self.UNITS.index(u))
        return n + m

    def gate(self, u, m):
        return self.linear(23, self._gate(u, m))

    def gate_slot(self, u, m):
        return self._gate(u, m) % 2

    def aux(self, name):
        return self.linear(self.aux_per, self.aux_start + self.order.index(name))

    def aux_slot(self, name):
        return 2 + (self.aux_start + self.order.index(name)) % 2

    def cell(self, u):
        return self.linear(5, 5 * self.c - 1 + self.UNITS.index(u))

    def split(self, name, expert_after=False):
        return self.linear(5, 5 * self.c + 2 + self.SPLITS[name] + (5 if expert_after else 0))

    def expert(self, after=0):
        return self.linear(1, self.c + after)

    def hs(self, n):
        return self.linear(2, 2 * self.c + n)


N_LOADS = 5


def weight_places(keep):
    places, start = {}, 0
    for name, shape in (("wi", (4 * HID,)), ("wh", (4 * HID,)), ("wo", (HID,)), ("b", (4,)), ("pick_f", (PICKS, P))):
        size = 2 * int(np.prod(shape))
        place = keep["shared"][0:64 if name == "pick_f" else P, start:start + size]
        places[name] = (place.rearrange("p (u a n) -> p u a n", u=2, a=shape[0]) if len(shape) == 2 else
                        place.rearrange("p (u n) -> p u n", u=2))
        start += size
    places["bo_f"] = keep["shared"][0:64, start:start + HID]
    places["bo_p"] = keep["shared"][0:64, start + HID:start + HID + 3 * HID // 2].bitcast(BF16).rearrange(
        "p (m n) -> p m n", m=3)
    return places


def load_expert(sp, d, s, weights_in, u, e):
    for dst, src in ((s["wi"][:, u, :], d["Wi"][bass.ds(e, 1)].rearrange("o p n -> (o p) n")),
                     (s["wh"][:, u, :], d["Wh"][bass.ds(e, 1)].rearrange("o p n -> (o p) n")),
                     (s["wo"][:, u, :], d["Wo"][bass.ds(e, 1)].rearrange("o p n -> (o p) n")),
                     (s["b"][:, u, :], d["b"][bass.ds(e, 1)].rearrange("o p g -> (o p) g")),
                     (s["pick_f"][:, u, :, :], d["c_pick"][bass.ds(e, 1)].rearrange("o p a n -> (o p) a n"))):
        sp.dma_start(dst, src).then_inc(weights_in[u], 16)


def expert_phase(nc, d, keep, ps, weights_in):
    with ExitStack() as ctx:
        s = allocate(nc, ctx, {
            "w": ([P, 2, 2, 2, 4 * HID], F32R),
            "pick": ([64, 2, PICKS, P], BF16),
            "z": ([P, 2, 8], F32),
            "n2": ([P, 2, B, TE], F32R),
            "x": ([P, 2, 4, TE], F32R),
            "gate": ([P, 2, 4, T], F32),
            "h_first": ([P, T], F32), "c_first": ([P, T], F32), "h_seed": ([P, 2, T], F32),
            "h": ([P, 2, T], F32), "c": ([P, 2, 2, T], F32),
            "seed": ([P, 2, 2, TE], F32R), "chain": ([P, 2, 2, TE], F32R), "merged": ([P, 2, TE], F32R),
            "tc": ([P, T], F32), "ig": ([P, T], F32), "fc": ([P, T], F32),
            "part": ([P, 2, T], F32), "hs": ([P, 2, T], F32),
            "spare": ([P, 1], F32),
        }, "e_")
        S = semaphores(nc, ctx, """
            pick_ready w_hi_ready w_lo_ready n2_hi_ready n2_lo_ready
            pads_ready bo_zeroed bo_in bo_step bo_ready y_zeroed
            z_gates z_c z_tc z_h gate_psum gate_read aux_psum aux_read ig_ready fc_ready c_first_ready c_ready
            tc_ready h_ready merged_ready hs_ready hi_ready lo_ready biased yb_ready turned_y out_ready stored
        """, "e_")
        s |= weight_places(keep)
        IG, FG, GG, OG = range(4)
        ZI, ZG, ZO, ZC, ZT, ZH = range(6)
        UNITS = {"u0": (0, None), "u1": (1, 0), "u2": (1, 1), "u3": (2, 0), "u4": (2, 1), "u5": (3, None)}
        FREE = 2
        PROLOGUE, FIRST, LAST_P, TAIL = (Place(0, 0, "prologue"), Place(0, 0, "first"), Place(0, E - 1, "last"),
                                         Place(0, E, "tail"))
        s["yT"] = keep["n2T"]
        flat = s["gate"][:].rearrange("p a g n -> p (a g n)")
        yb = flat[:, 0:2 * TPAD].rearrange("p (a n) -> p a n", a=2)
        out = flat[:, 2 * TPAD:(2 + B) * TPAD].rearrange("p (b n) -> p b n", b=B)

        def order(u):
            return (IG, GG, OG) if u == "u0" else (IG, GG, FG, OG)

        def parity(at, u):
            return {"u0": at.par if at.kind == "prologue" else 1 - at.par, "u5": 1 - at.par}.get(u, at.par)

        block = ctx.enter_context(nc.Block())

        @block.sync
        def _(sp):
            sp.wait_ge(S["bo_zeroed"], 1)
            for part in range(3):
                for k in range(2):
                    row = 16 + 16 * part + E * k
                    sp.dma_start(s["bo_f"][row:row + E, :], d["bo"]).then_inc(S["bo_in"], 16)
            with sp.Fori(0, E // 2 - 1) as i:
                for c in (1, 2):
                    at = Place(i, c)
                    sp.wait_ge(S["aux_read"], FREE + at.aux("y3") + 1)
                    load_expert(sp, d, s, weights_in, 1 - at.par, 2 * i + c + 1)
            for b in range(B):
                sp.wait_ge(S["out_ready"], b + 1)
                sp.dma_start(d["out"][b, 0:(NT - 1) * P, :].rearrange("(t p) c -> p t c", p=P),
                             out[:, b, 0:(NT - 1) * P].rearrange("p (t c) -> p t c", c=HID)).then_inc(S["stored"], 16)
                sp.dma_start(d["out"][b, (NT - 1) * P:T, :], out[0:LAST, b, (NT - 1) * P:TPAD]).then_inc(S["stored"], 16)
            sp.wait_ge(S["stored"], 32 * B)

        @block.gpsimd
        def _(pool):
            def halve_weights(e, u):
                for w, src in ((0, s["wi"]), (1, s["wh"])):
                    pool.wait_ge(S["w_hi_ready"], 2 * e + w + 1)
                    pool.tensor_tensor(s["w"][:, u, w, 1, :], src[:, u, :], s["w"][:, u, w, 0, :].bitcast(F32),
                                       ALU.subtract).then_inc(S["w_lo_ready"], 1)

            def input_gate(at, u):
                gate = s["gate"][:, at.unit_parity(u)]
                pool.wait_ge(S["gate_read"], FREE + at.gate(u, 2))
                if u == "u0":
                    pool.tensor_tensor(s["c_first"][:], gate[:, IG, :], gate[:, GG, :], ALU.mult
                                       ).then_inc(S["c_first_ready"], 1)
                else:
                    if not (at.kind == "first" and u == "u1"):
                        pool.wait_ge(S["c_ready"], at.cell(u))
                    pool.tensor_tensor(s["ig"][:], gate[:, IG, :], gate[:, GG, :], ALU.mult).then_inc(S["ig_ready"], 1)

            def sum_choices(at, st, after):
                pool.wait_ge(S["aux_read"], FREE + at.aux(after) + 1)
                pool.tensor_tensor(s["hs"][:, st % 2, :], s["part"][:, 0, :], s["part"][:, 1, :], ALU.add
                                   ).then_inc(S["hs_ready"], 1)

            def period(at):
                if at.kind != "first":
                    input_gate(at, "u5")
                if at.kind == "tail":
                    return
                input_gate(at, "u1")
                input_gate(at, "u2")
                if at.kind != "last":
                    halve_weights(at.expert(1), 1 - at.par)
                input_gate(at, "u3")
                sum_choices(at, 1, "w11")
                input_gate(at, "u4")
                if at.kind != "last":
                    input_gate(at, "u0")
                sum_choices(at, 2, "w21")

            pool.sem_inc(S["h_ready"], FREE)
            pool.sem_inc(S["gate_read"], FREE)
            pool.sem_inc(S["aux_read"], FREE)
            for halves in (s["n2"], s["x"], s["seed"], s["chain"]):
                pool.memset(halves[:, :, :, T:TE].bitcast(F32), 0.0)
            pool.memset(s["merged"][:, :, T:TE].bitcast(F32), 0.0).then_inc(S["pads_ready"], 1)
            halve_weights(0, 0)
            pool.memset(s["bo_f"], 0.0).then_inc(S["bo_zeroed"], 1)
            input_gate(PROLOGUE, "u0")
            pool.wait_ge(S["n2_lo_ready"], B)
            pool.memset(s["yT"][:], 0.0).then_inc(S["y_zeroed"], 1)
            period(FIRST)
            with pool.Fori(0, E // 2 - 1) as i:
                period(Place(i, 1))
                period(Place(i, 2))
            period(LAST_P)
            period(TAIL)

        @block.vector
        def _(dve):
            def aux(at, name):
                dve.wait_ge(S["aux_psum"], at.aux(name) + 1)
                return ps[at.aux_slot(name)][:, 0:T]

            def masked(at, name, st, k):
                m = aux(at, name)
                dve.tensor_tensor(s["x"][:, 0, 2 * (st - 1) + k, 0:T], s["n2"][:, 0, st, 0:T].bitcast(F32), m, ALU.mult)
                dve.tensor_tensor(s["x"][:, 1, 2 * (st - 1) + k, 0:T], s["n2"][:, 1, st, 0:T].bitcast(F32), m,
                                  ALU.mult).then_inc(S["aux_read"], 1)

            def scale(at, name, src, dst):
                dve.tensor_tensor(dst, src, aux(at, name), ALU.mult).then_inc(S["aux_read"], 1)

            def output(at, name):
                y = s["yT"][:, int(name[1]), :]
                dve.tensor_tensor(y, y, aux(at, name), ALU.add).then_inc(S["aux_read"], 1)

            def cell(at, u):
                st, k = UNITS[u]
                par = parity(at, u)
                z, c, gate = s["z"][:, par, :], s["c"][:, par, k or 0, :], s["gate"][:, at.unit_parity(u)]
                dve.wait_ge(S["gate_read"], FREE + at.gate(u, 3))
                if st == 1:
                    dve.scalar_tensor_tensor(s["fc"][:], c, z[:, ZC:ZC + 1], gate[:, FG, :], ALU.add, ALU.mult
                                             ).then_inc(S["fc_ready"], 1)
                else:
                    dve.tensor_tensor(s["fc"][:], c, gate[:, FG, :], ALU.mult).then_inc(S["fc_ready"], 1)
                dve.wait_ge(S["fc_ready"], at.cell(u) + 1)
                dve.wait_ge(S["ig_ready"], at.cell(u) + 1)
                dve.tensor_tensor(c, s["fc"][:], s["ig"][:], ALU.add).then_inc(S["c_ready"], 1)

            def state(at, u):
                k = UNITS[u][1]
                dst = s["h_first"][:] if u == "u0" else s["h"][:, k or 0, :]
                dve.wait_ge(S["tc_ready"], at.unit(u) + 1)
                dve.tensor_tensor(dst, s["gate"][:, at.unit_parity(u), OG, :], s["tc"][:], ALU.mult).then_inc(S["h_ready"], 1)
                return FREE + at.unit(u) + 1

            def lower(n, src, halves):
                dve.wait_ge(S["hi_ready"], n + 1)
                dve.tensor_tensor(halves[:, 1, 0:T], src, halves[:, 0, 0:T].bitcast(F32), ALU.subtract
                                  ).then_inc(S["lo_ready"], 1)

            def empty_c(e, u):
                z = s["z"][:, u, :]
                dve.wait_ge(S["z_gates"], e + 1)
                dve.tensor_tensor(z[:, ZC:ZC + 1], z[:, ZI:ZI + 1], z[:, ZG:ZG + 1], ALU.mult).then_inc(S["z_c"], 1)

            def empty_h(e, u):
                z = s["z"][:, u, :]
                dve.wait_ge(S["z_tc"], e + 1)
                dve.tensor_tensor(z[:, ZH:ZH + 1], z[:, ZO:ZO + 1], z[:, ZT:ZT + 1], ALU.mult).then_inc(S["z_h"], 1)

            def first_step(at, e, u, after):
                z = s["z"][:, u, :]
                dve.wait_ge(S["h_ready"], state(at, "u0"))
                for k, name in enumerate(("s0", "s1")):
                    m = aux(at, name)
                    dve.scalar_tensor_tensor(s["h_seed"][:, k, :], s["h_first"][:], z[:, ZH:ZH + 1], m,
                                             ALU.subtract, ALU.mult)
                    dve.scalar_tensor_tensor(s["c"][:, u, k, :], s["c_first"][:], z[:, ZC:ZC + 1], m,
                                             ALU.subtract, ALU.mult).then_inc(S["aux_read"], 1)
                for k, name in enumerate(("s0", "s1")):
                    dve.wait_ge(S["hi_ready"], at.split(name, expert_after=after) + 1)
                    dve.scalar_tensor_tensor(s["seed"][:, k, 1, 0:T], s["h_seed"][:, k, :], z[:, ZH:ZH + 1],
                                             s["seed"][:, k, 0, 0:T].bitcast(F32), ALU.add, ALU.subtract
                                             ).then_inc(S["lo_ready"], 1)

            def last_step(at):
                cell(at, "u5")
                output(at, "y2")
                dve.wait_ge(S["h_ready"], state(at, "u5"))
                scale(at, "w3", s["h"][:, 0, :], s["hs"][:, 1, :])

            def period(at):
                par = at.par
                if at.kind != "first":
                    last_step(at)
                    output(at, "y3")
                masked(at, "x20", 2, 0)
                cell(at, "u1")
                masked(at, "x21", 2, 1)
                done = state(at, "u1")
                scale(at, "w0", s["h_first"][:], s["hs"][:, 0, :])
                dve.wait_ge(S["h_ready"], done)
                scale(at, "w10", s["h"][:, 0, :], s["part"][:, 0, :])
                lower(at.split("h10"), s["h"][:, 0, :], s["chain"][:, 0])
                cell(at, "u2")
                output(at, "y0")
                dve.wait_ge(S["h_ready"], state(at, "u2"))
                scale(at, "w11", s["h"][:, 1, :], s["part"][:, 1, :])
                lower(at.split("h11"), s["h"][:, 1, :], s["chain"][:, 1])
                if at.kind != "last":
                    empty_c(at.expert(1), 1 - par)
                cell(at, "u3")
                done = state(at, "u3")
                output(at, "y1")
                if at.kind != "last":
                    empty_h(at.expert(1), 1 - par)
                    masked(at, "x10", 1, 0)
                    masked(at, "x11", 1, 1)
                dve.wait_ge(S["h_ready"], done)
                scale(at, "w20", s["h"][:, 0, :], s["part"][:, 0, :])
                cell(at, "u4")
                dve.wait_ge(S["h_ready"], state(at, "u4"))
                m = aux(at, "merge").bitcast(I32)
                apart(dve, s["spare"])
                dve.copy_predicated(s["h"][:, 0, :], m, s["h"][:, 1, :]).then_inc(S["merged_ready"], 1)
                dve.copy_predicated(s["c"][:, par, 0, :], m, s["c"][:, par, 1, :]).then_inc(S["aux_read"], 1)
                scale(at, "w21", s["h"][:, 1, :], s["part"][:, 1, :])
                lower(at.split("m"), s["h"][:, 0, :], s["merged"])
                if at.kind != "last":
                    first_step(at, at.expert(1), 1 - par, True)

            def inputs_lower(st):
                dve.wait_ge(S["n2_hi_ready"], st + 1)
                dve.tensor_tensor(s["n2"][:, 1, st, 0:T], keep["n2T"][:, st, :], s["n2"][:, 0, st, 0:T].bitcast(F32), ALU.subtract
                                  ).then_inc(S["n2_lo_ready"], 1)

            inputs_lower(0)
            inputs_lower(1)
            dve.wait_ge(S["n2_lo_ready"], 2)
            masked(PROLOGUE, "x10", 1, 0)
            masked(PROLOGUE, "x11", 1, 1)
            empty_c(0, 0)
            empty_h(0, 0)
            first_step(PROLOGUE, 0, 0, False)
            inputs_lower(2)
            inputs_lower(3)
            dve.wait_ge(S["bo_in"], 16 * 6)
            for part in range(3):
                dve.tensor_copy(s["bo_p"][:, part, :], s["bo_f"]).then_inc(S["bo_step"] if part < 2 else S["bo_ready"], 1)
                if part < 2:
                    dve.wait_ge(S["bo_step"], 2 * part + 1)
                    dve.tensor_tensor(s["bo_f"], s["bo_f"], s["bo_p"][:, part, :], ALU.subtract).then_inc(S["bo_step"], 1)
                    dve.wait_ge(S["bo_step"], 2 * part + 2)
            dve.wait_ge(S["y_zeroed"], 1)
            dve.wait_ge(S["n2_lo_ready"], B)
            period(FIRST)
            with dve.Fori(0, E // 2 - 1) as i:
                period(Place(i, 1))
                period(Place(i, 2))
            period(LAST_P)
            last_step(TAIL)
            dve.memset(yb[:, :, T:TPAD], 0.0)

            def add_bias(b):
                dve.wait_ge(S["biased"], b + 1)
                if b >= 2:
                    dve.wait_ge(S["turned_y"], b - 1)
                dve.tensor_tensor(yb[:, b % 2, 0:T], ps[b % 2][:, 0:T], s["yT"][:, b, :], ALU.add).then_inc(S["yb_ready"], 1)

            def add_h1(b):
                dve.wait_ge(S["turned_y"], b + 1)
                dve.tensor_tensor(out[:, b], ps[2 + b % 2][:, 0:TPAD], keep["h1"][:, b, :], ALU.add
                                  ).then_inc(S["out_ready"], 1)

            add_bias(0)
            add_bias(1)
            output(TAIL, "y3")
            add_h1(0)
            add_bias(2)
            add_h1(1)
            dve.wait_ge(S["aux_read"], FREE + TAIL.aux("y3") + 1)
            add_bias(3)
            add_h1(2)
            add_h1(3)

        @block.scalar
        def _(act):
            def prepare(u):
                z, b = s["z"][:, u, :], s["b"][:, u, :]
                act.activation(s["w"][:, u, 0, 0, :], s["wi"][:, u, :], ACT.Copy).then_inc(S["w_hi_ready"], 1)
                act.activation(s["pick"][:, u, :, :], s["pick_f"][:, u, :, :], ACT.Copy).then_inc(S["pick_ready"], 1)
                act.activation(s["w"][:, u, 1, 0, :], s["wh"][:, u, :], ACT.Copy).then_inc(S["w_hi_ready"], 1)
                act.activation(z[:, ZI:ZI + 1], b[:, IG:IG + 1], ACT.Sigmoid)
                act.activation(z[:, ZG:ZG + 1], b[:, GG:GG + 1], ACT.Tanh)
                act.activation(z[:, ZO:ZO + 1], b[:, OG:OG + 1], ACT.Sigmoid).then_inc(S["z_gates"], 1)

            def empty_tanh(e, u):
                act.wait_ge(S["z_c"], e + 1)
                act.activation(s["z"][:, u, ZT:ZT + 1], s["z"][:, u, ZC:ZC + 1], ACT.Tanh).then_inc(S["z_tc"], 1)

            def gate(at, u, m):
                g, st, par = order(u)[m], UNITS[u][0], parity(at, u)
                if m == 0:
                    act.wait_ge(S["h_ready"], at.unit(u) + 1)
                act.wait_ge(S["gate_psum"], at.gate(u, m) + 1)
                act.activation(s["gate"][:, at.unit_parity(u), g, :], ps[at.gate_slot(u, m)][:, 0:T],
                               ACT.Tanh if g == GG else ACT.Sigmoid,
                               bias=s["b"][:, par, g:g + 1]).then_inc(S["gate_read"], 1)

            def tanh_c(at, u, e=None):
                src = s["c_first"][:] if u == "u0" else s["c"][:, parity(at, u), UNITS[u][1] or 0, :]
                if u == "u0":
                    act.wait_ge(S["c_first_ready"], e + 1)
                else:
                    act.wait_ge(S["c_ready"], at.cell(u) + 1)
                act.wait_ge(S["h_ready"], at.unit(u) + FREE)
                act.activation(s["tc"][:], src, ACT.Tanh).then_inc(S["tc_ready"], 1)

            def upper(sem, value, src, halves):
                act.wait_ge(sem, value)
                act.activation(halves[:, 0, 0:T], src, ACT.Copy).then_inc(S["hi_ready"], 1)

            def upper_seeds(par, seeds_at):
                for k, name in enumerate(("s0", "s1")):
                    act.wait_ge(S["aux_read"], FREE + seeds_at.aux(name) + 1)
                    act.activation(s["seed"][:, k, 0, 0:T], s["h_seed"][:, k, :], ACT.Identity,
                                   bias=s["z"][:, par, ZH:ZH + 1], scale=1.0).then_inc(S["hi_ready"], 1)

            def last_step(at, before=None):
                gate(at, "u5", 0)
                gate(at, "u5", 1)
                if before is not None:
                    upper_seeds(at.par, before)
                gate(at, "u5", 2)
                gate(at, "u5", 3)
                tanh_c(at, "u5")

            def loads(at):
                return N_LOADS * 16 * at.i + N_LOADS * 16 * (1 if at.c == 0 else 2)

            def period(at, before=None):
                if at.kind != "first":
                    last_step(at, before)
                for m in range(4):
                    gate(at, "u1", m)
                tanh_c(at, "u1")
                gate(at, "u2", 0)
                upper(S["h_ready"], FREE + at.unit("u1") + 1, s["h"][:, 0, :], s["chain"][:, 0])
                for m in (1, 2, 3):
                    gate(at, "u2", m)
                tanh_c(at, "u2")
                if at.kind != "last":
                    act.wait_ge(weights_in[1 - at.par], loads(at))
                    prepare(1 - at.par)
                gate(at, "u3", 0)
                upper(S["h_ready"], FREE + at.unit("u2") + 1, s["h"][:, 1, :], s["chain"][:, 1])
                gate(at, "u3", 1)
                if at.kind != "last":
                    empty_tanh(at.expert(1), 1 - at.par)
                gate(at, "u3", 2)
                gate(at, "u3", 3)
                tanh_c(at, "u3")
                gate(at, "u4", 0)
                gate(at, "u4", 1)
                gate(at, "u4", 2)
                gate(at, "u4", 3)
                tanh_c(at, "u4")
                if at.kind != "last":
                    for m in range(3):
                        gate(at, "u0", m)
                upper(S["merged_ready"], at.expert(1), s["h"][:, 0, :], s["merged"])
                if at.kind != "last":
                    tanh_c(at, "u0", at.expert(1))

            act.activation(s["n2"][:, 0, 0, 0:T], keep["n2T"][:, 0, :], ACT.Copy).then_inc(S["n2_hi_ready"], 1)
            act.wait_ge(weights_in[0], 16 * N_LOADS)
            prepare(0)
            act.activation(s["n2"][:, 0, 1, 0:T], keep["n2T"][:, 1, :], ACT.Copy).then_inc(S["n2_hi_ready"], 1)
            empty_tanh(0, 0)
            for st in (2, 3):
                act.activation(s["n2"][:, 0, st, 0:T], keep["n2T"][:, st, :], ACT.Copy).then_inc(S["n2_hi_ready"], 1)
            for m in range(3):
                gate(PROLOGUE, "u0", m)
            tanh_c(PROLOGUE, "u0", 0)
            upper_seeds(0, PROLOGUE)
            period(FIRST)
            with act.Fori(0, E // 2 - 1) as i:
                period(Place(i, 1), before=Place(i, 0))
                period(Place(i, 2), before=Place(i, 1))
            period(LAST_P, before=Place(0, E - 2))
            last_step(TAIL)

        @block.tensor
        def _(pe):
            def halves_product(slot, w, x, start, stop):
                terms = ((0, 0), (0, 1), (1, 0))
                for a, b in ((0, HALF), (HALF, TE)):
                    for n, (p, q) in enumerate(terms):
                        ins = pe.matmul(ps[slot][:, a:b], w[:, p], x[:, q, a:b], start=start and n == 0,
                                        stop=stop and n == len(terms) - 1)
                return ins

            def aux(at, name, par):
                pe.wait_ge(S["aux_read"], at.aux(name) + 1)
                slot = at.aux_slot(name)
                if name[0] == "y":
                    st = int(name[1])
                    if st in (0, 3):
                        pe.wait_ge(S["aux_read"], FREE + at.aux("w0" if st == 0 else "w3") + 1)
                    else:
                        pe.wait_ge(S["hs_ready"], at.hs(1) if st == 1 else at.hs(0))
                    ins = over_tokens(pe, ps[slot], s["wo"][:, par, :], s["hs"][:, st % 2, :])
                else:
                    row, st = {"x10": (M0, 1), "x11": (M1, 1), "x20": (M0, 2), "x21": (M1, 2), "s0": (M0, 0),
                               "s1": (M1, 0), "w0": (W01, 0), "w10": (W0, 1), "w11": (W1, 1), "w20": (W0, 2),
                               "w21": (W1, 2), "w3": (W01, 3), "merge": (M1, 3)}[name]
                    ins = over_tokens(pe, ps[slot], s["pick"][:, par, row, :], keep["rt"][:, st, :])
                ins.then_inc(S["aux_psum"], 1)

            def unit(at, u, before=None):
                st, k = UNITS[u]
                par = parity(at, u)
                w = s["w"][:, par]
                x = s["n2"][:, :, st, :] if k is None else s["x"][:, :, 2 * (st - 1) + k, :]
                h = {1: s["seed"][:, k or 0], 2: s["chain"][:, k or 0], 3: s["merged"][:]}.get(st)
                if k is not None:
                    if st == 2:
                        pe.wait_ge(S["aux_read"], FREE + at.aux(f"x2{k}") + 1)
                    elif at.kind == "first":
                        pe.wait_ge(S["aux_read"], FREE + PROLOGUE.aux(f"x1{k}") + 1)
                    else:
                        pe.wait_ge(S["lo_ready"], at.split("s0") + 1)

                def own(m):
                    cols = slice(order(u)[m] * HID, (order(u)[m] + 1) * HID)
                    pe.wait_ge(S["gate_read"], at.gate(u, m) + 1)
                    ins = halves_product(at.gate_slot(u, m), w[:, 0, :, cols], x, True, st == 0)
                    if st == 0:
                        ins.then_inc(S["gate_psum"], 1)

                def from_state(m):
                    cols = slice(order(u)[m] * HID, (order(u)[m] + 1) * HID)
                    halves_product(at.gate_slot(u, m), w[:, 1, :, cols], h, False, True).then_inc(S["gate_psum"], 1)

                def after(m):
                    for name in Place.AUX[u].get(m, ()):
                        if name in ("s0", "s1") and at.kind != "prologue":
                            continue
                        if name in at.order and not (name == "y3" and at.kind == "first"):
                            aux(at, name, PROLOGUE.par if at.kind == "prologue" else
                                (1 - at.par if name in Place.NEXT + ("y2", "w3", "y3") else at.par))

                if st == 0:
                    for m in range(3):
                        own(m)
                        after(m)
                    return
                own(0)
                own(1)
                if before is not None:
                    aux(before, "s0", at.par)
                    aux(before, "s1", at.par)
                pe.wait_ge(S["lo_ready"], at.split({1: "s", 2: "h1", 3: "m"}[st] + ("" if k is None else str(k)))
                           + (1 if st < 3 else -4))
                from_state(0)
                after(0)
                from_state(1)
                after(1)
                for m in (2, 3):
                    own(m)
                    from_state(m)
                    after(m)

            def weights_ready(n):
                pe.wait_ge(S["w_lo_ready"], 2 * n)

            pe.wait_ge(S["pick_ready"], 1)
            aux(PROLOGUE, "x10", 0)
            aux(PROLOGUE, "x11", 0)
            pe.wait_ge(S["w_lo_ready"], 1)
            pe.wait_ge(S["n2_lo_ready"], 1)
            pe.wait_ge(S["pads_ready"], 1)
            unit(PROLOGUE, "u0")

            def period(at, before=None):
                if at.kind != "first":
                    unit(at, "u5", before)
                for u in ("u1", "u2", "u3"):
                    unit(at, u)
                if at.kind != "last":
                    weights_ready(at.expert(2))
                unit(at, "u4")
                if at.kind != "last":
                    unit(at, "u0")
                else:
                    aux(at, "w21", at.par)

            weights_ready(1)
            period(FIRST)
            with pe.Fori(0, E // 2 - 1) as i:
                period(Place(i, 1), before=Place(i, 0))
                period(Place(i, 2), before=Place(i, 1))
            period(LAST_P, before=Place(0, E - 2))
            unit(TAIL, "u5")

            def bias(b):
                if b >= 2:
                    pe.wait_ge(S["yb_ready"], b - 1)
                for x, y in HALVES:
                    for part in range(3):
                        ins = pe.matmul(ps[b % 2][:, x:y], s["bo_p"][:, part, :], keep["rt"][:, b, x:y],
                                        start=part == 0, stop=part == 2)
                ins.then_inc(S["biased"], 1)

            def turn_back(b):
                pe.wait_ge(S["yb_ready"], b + 1)
                if b >= 2:
                    pe.wait_ge(S["out_ready"], b - 1)
                for t in range(NT):
                    ins = pe.transpose(ps[2 + b % 2][:, t * P:(t + 1) * P], yb[:, b % 2, t * P:(t + 1) * P],
                                       keep["ident"][:])
                ins.then_inc(S["turned_y"], 1)

            pe.wait_ge(S["bo_ready"], 1)
            pe.wait_ge(S["gate_read"], FREE + TAIL.gate("u5", 3) + 1)
            bias(0)
            bias(1)
            aux(TAIL, "y3", 1 - TAIL.par)
            pe.wait_ge(S["aux_read"], FREE + TAIL.aux("y3") + 1)
            turn_back(0)
            bias(2)
            turn_back(1)
            bias(3)
            turn_back(2)
            turn_back(3)


def build(nc, d):
    with ExitStack() as ctx:
        keep = allocate(nc, ctx, {
            "ident": ([P, P], F32),
            "h1": ([P, B, TPAD], F32),
            "n2T": ([P, B, T], F32),
            "rt_place": ([P, B, T], BF16),
            "shared": ([P, 3 * HEADS * BAND // 2], F32),
        }, "k_")
        keep["rt"] = keep["rt_place"][0:64]
        weights_in = [ctx.enter_context(nc.semaphore(f"weights_in{u}")) for u in range(2)]
        ps = [ctx.enter_context(nc.psum_tensor(f"ps{n}", [P, 2 * HALF], F32)) for n in range(4)]
        with ExitStack() as block_ctx:
            across = allocate(nc, block_ctx, {
                "q_st": ([P, GROUPS, GH, TPAD], BF16), "k_st": ([P, GROUPS, GH, TPAD], BF16),
                "v": ([P, B, NT, HEADS, 32], F32),
                "n1b": ([P, B, NT, HID], F32), "att": ([P, B, GROUPS, TPAD], F32),
                "bias_qk": ([P, HEADS, GW], F32), "w_out": ([P, GROUPS, HID], F32),
                "cols": ([P, COLS_N], F32), "rows": ([P, ROWS_N], F32), "head_sum": ([P, P], F32),
                "ident_b": ([P, P], BF16),
            }, "x_")
            across["bias_kq"] = keep["shared"][:].bitcast(BF16).rearrange("p (m h n) -> p m h n", m=3, h=HEADS)
            parts_out = [block_ctx.enter_context(nc.semaphore(f"parts_out{b}")) for b in range(B)]
            stacked = [block_ctx.enter_context(nc.semaphore(f"stacked{g}")) for g in range(GROUPS)]
            embedding_phase(nc, d, keep, across, ps, parts_out, stacked)
            attention_phase(nc, d, keep, across, ps, parts_out, stacked)
            closing_phase(nc, d, keep, across, ps, weights_in)
        expert_phase(nc, d, keep, ps, weights_in)


def arranged(x, txt, **p):
    import numpy as np

    f = lambda a: np.ascontiguousarray(np.asarray(a))
    x = f(x).reshape(B, 3, NP_SIDE, NP_SIDE, NP_SIDE, NP_SIDE)
    patches = np.zeros((B, PATCH_DIM, 2 * P), np.float32)
    patches[:, :, 1:1 + N_PATCH] = x.transpose(0, 1, 3, 5, 2, 4).reshape(B, PATCH_DIM, N_PATCH)
    table = f(p["L0_attn_rel_table"]).T
    side = TPAD - MAXD
    ext = np.pad(table, ((0, 0), (side, side - 1)), mode="edge")
    const_rows = np.zeros((NT, HEADS, T), np.float32)
    for kt in range(NT):
        left, right = max(0, kt * P - P), min(T, kt * P + 2 * P)
        const_rows[kt, :, 0:left], const_rows[kt, :, right:T] = table[:, 0:1], table[:, -1:]
    row, col, band = np.arange(P)[:, None], np.arange(GW)[None, :], np.arange(BAND)[None, :]
    head_sum = np.zeros((P, P), np.float32)
    for j in range(GH):
        head_sum[32 * j + DH, 32 * j:32 * j + 32] = 1.0
    key_rows = np.zeros((XR, TPAD), np.float32)
    key_rows[0:2] = 1.0
    for r in range(3 * NT):
        key_rows[2 + r, (r % NT) * P:(r % NT + 1) * P] = 1.0
    tok_b, pos = f(p["L0_tok_b"]), np.zeros((2 * P, HID), np.float32)
    pos[0:1 + N_PATCH] = f(p["L0_tok_pos"])
    tok_add = np.zeros((2 * P, HID), np.float32)
    tok_add[0:1], tok_add[1:1 + N_PATCH] = f(p["L0_tok_token"]), tok_b
    by_tile = lambda a: f(a.reshape(2, P, HID).transpose(1, 0, 2))
    w_out = np.zeros((GROUPS, GH, 32, HID), np.float32)
    w_out[:, :, 0:DH] = f(p["L0_attn_w_out"]).reshape(GROUPS, GH, DH, HID)
    b_qkv = f(p["L0_attn_b_qkv"])
    cols = np.concatenate([np.stack([b_qkv[0:HID], b_qkv[HID:2 * HID], f(p["L0_attn_ln1_g"]), f(p["L0_attn_ln1_b"]),
                                     f(p["L0_attn_b_mlp2"])]),
                           f(p["L0_attn_b_mlp1"]).reshape(NCH, P)]).T
    rows = np.concatenate([b_qkv[2 * HID:], f(p["L0_attn_b_out"]), f(p["L0_attn_ln2_g"]),
                           f(p["L0_attn_ln2_b"]), f(p["L0_ffn_router_b"])])
    pick = np.zeros((E, 64, PICKS, P), np.float32)
    for e in range(E):
        pick[e, e, M0] = pick[e, E + e, M1] = 1.0
        for part in range(3):
            r = 16 + 16 * part + e
            pick[e, r, W0] = pick[e, r, W01] = pick[e, r + E, W1] = pick[e, r + E, W01] = 1.0
    return {
        "patches": patches, "txt": f(txt), "tok_W": f(f(p["L0_tok_W"]).T), "tok_add": by_tile(tok_add),
        "pos": by_tile(pos), "cols": f(cols), "rows": rows,
        "w_qkv": f(p["L0_attn_w_qkv"]), "w_out": f(w_out.reshape(GROUPS, P, HID).transpose(1, 0, 2)),
        "w_mlp1": f(p["L0_attn_w_mlp1"]), "w_mlp2": f(p["L0_attn_w_mlp2"]), "router_w": f(p["L0_ffn_router_w"]),
        "const_rows": const_rows.reshape(NT * HEADS, T), "rel_strip": f(ext[:, TPAD + row - col + (NT - 1) * P]),
        "rel_band": f(ext[:, TPAD - P + band - row]),
        "Wi": f(p["L0_ffn_Wi"]), "Wh": f(p["L0_ffn_Wh"]), "b": f(f(p["L0_ffn_b"]).reshape(E, 4, HID).transpose(0, 2, 1)), "Wo": f(p["L0_ffn_Wo"]),
        "bo": f(p["L0_ffn_bo"]),
        "c_ident": np.eye(P, dtype=np.float32), "c_head_sum": head_sum, "c_key_rows": key_rows, "c_pick": pick,
    }


def kernel(**inputs):
    import concourse.bacc as bacc
    from concourse.bass_utils import run_bass_kernel_spmd

    nc = bacc.Bacc("TRN2", target_bir_lowering=False, num_devices=1)
    arrays = {f"in_{name}": a for name, a in arranged(**inputs).items()}
    d = {
        name[3:]: nc.dram_tensor(name, a.shape, mybir.dt.from_np(a.dtype), kind="ExternalInput").ap()
        for name, a in arrays.items()}
    d["out"] = nc.dram_tensor("out_0", (B, T, HID), F32, kind="ExternalOutput").ap()
    d["q_parts"] = nc.dram_tensor("q_parts", (B, QR, HEADS, T), BF16, kind="Internal").ap()
    d["k_parts"] = nc.dram_tensor("k_parts", (B, 3 * DH, HEADS, T), BF16, kind="Internal").ap()
    d["const_d"] = nc.dram_tensor("const_scratch", (3, NT, HEADS, T), BF16, kind="Internal").ap()
    build(nc, d)
    return run_bass_kernel_spmd(nc, [arrays], core_ids=[0]).results[0]["out_0"]
```
